# Optimizing a Trainium2 kernel written in Bass

```python
import numpy as np
import jax
import jax.numpy as jnp

def _softmax(x, axis=-1):
    return jax.nn.softmax(x, axis=axis)

def _gelu(x):
    return jax.nn.gelu(x, approximate=True)

def _silu(x):
    return jax.nn.silu(x)

def _sigmoid(x):
    return jax.nn.sigmoid(x)

def _layernorm(x, axis=-1, eps=1e-05):
    m = jnp.mean(x, axis=axis, keepdims=True)
    v = jnp.var(x, axis=axis, keepdims=True)
    return (x - m) / jnp.sqrt(v + eps)

def _scatter_add(tgt, idx, src, axis=0):
    return tgt.at[idx].add(src)

def _segment_sum(src, seg, n):
    return jax.ops.segment_sum(src, seg, n)
kernel_name = 'mk_decoder_preln_d1_seqx_r8_c6dde1'

def setup_inputs(seed: int=0):
    np.random.seed(seed)
    _w = jnp.asarray

    def _rec_inputs():
        import jax
        import jax.numpy as jnp
        _rk = jax.random.key(seed)
        x = 7.22e-05 + 1 * jax.random.normal(jax.random.fold_in(_rk, 1), (32, 64, 256), jnp.float32)
        _lenS = 64 - jax.random.randint(jax.random.fold_in(_rk, 7), (32,), 0, max(1, 64 // 4) + 1, jnp.int32)
        _lenS2 = 64 - jax.random.randint(jax.random.fold_in(_rk, 8), (32,), 0, max(1, 64 // 4) + 1, jnp.int32)
        _ctx_1024P = jax.random.normal(jax.random.fold_in(_rk, 11), (32, 16, 128), jnp.float32)
        _ctx_1024c = jax.random.dirichlet(jax.random.fold_in(_rk, 511), 0.3 * jnp.ones((16,), jnp.float32), (32, 64))
        _ctx_1024t = jnp.einsum('bsk,bkd->bsd', _ctx_1024c, _ctx_1024P)
        _ctx_1024t = _ctx_1024t * jax.lax.rsqrt(jnp.mean(jnp.square(_ctx_1024t)) + 1e-12) * 0.953939
        ctx_1024 = -1.39393e-06 + 0.999914 * (_ctx_1024t + 0.3 * jax.random.normal(jax.random.fold_in(_rk, 611), (32, 64, 128), jnp.float32))
        fside_BxSx2_0 = jax.random.uniform(jax.random.fold_in(_rk, 12), (32, 64, 2), jnp.float32, 0.0, 0.999707)
        return (x, ctx_1024, fside_BxSx2_0)
    x, ctx_1024, fside_BxSx2_0 = _rec_inputs()

    def _L0_attn_setup():
        import jax, jax.numpy as jnp
        import numpy as np
        B, S, DIN = (2, 256, 256)
        HQ, HKV, DH = (16, 1, 128)
        key = jax.random.key(seed)
        ks = jax.random.split(key, 9)
        sc_in = 1.0 / np.sqrt(DIN)
        sc_o = 1.0 / np.sqrt(HQ * DH)
        return {'q': jax.random.normal(ks[0], (B, S, DIN), dtype=jnp.float32), 'Wq': jax.random.normal(ks[1], (DIN, HQ * DH), dtype=jnp.float32) * sc_in, 'bq': jnp.zeros((HQ * DH,), dtype=jnp.float32), 'Wk': jax.random.normal(ks[2], (DIN, HKV * DH), dtype=jnp.float32) * sc_in, 'bk': jnp.zeros((HKV * DH,), dtype=jnp.float32), 'Wv': jax.random.normal(ks[3], (DIN, HKV * DH), dtype=jnp.float32) * sc_in, 'bv': jnp.zeros((HKV * DH,), dtype=jnp.float32), 'Wo': jax.random.normal(ks[4], (HQ * DH, DIN), dtype=jnp.float32) * sc_o, 'bo': jnp.zeros((DIN,), dtype=jnp.float32)}
    _L0_attn_all = _L0_attn_setup()
    _L0_attn_in = {k: v for k, v in _L0_attn_all.items() if k in ('Wq', 'bq', 'Wk', 'bk', 'Wv', 'bv', 'Wo', 'bo')}
    del _L0_attn_all

    def _L0_xattn_setup():
        import jax, jax.numpy as jnp
        import numpy as np
        DIM = 256
        CTX_DIM = 128
        N_HEADS = 32
        HEAD_DIM = DIM // N_HEADS
        POS_DIM = 2
        B, N, CTXN = (2, 256, 256)
        ROPE_BASE = 10000.0

        def apply_axial_rope(x, pos):
            b, n, h, d = x.shape
            p = pos.shape[-1]
            dpa = d // p
            half = dpa // 2
            freqs = ROPE_BASE ** (-jnp.arange(half, dtype=x.dtype) / half)
            ang = pos[..., :, None] * freqs
            cos = jnp.cos(ang)[:, :, None, :, :]
            sin = jnp.sin(ang)[:, :, None, :, :]
            xr = x.reshape(b, n, h, p, half, 2)
            x1, x2 = (xr[..., 0], xr[..., 1])
            out = jnp.stack([x1 * cos - x2 * sin, x1 * sin + x2 * cos], axis=-1)
            return out.reshape(b, n, h, d)
        key = jax.random.key(seed)
        ks = jax.random.split(key, 8)
        x = jax.random.normal(ks[0], (B, N, DIM), jnp.float32)
        ctx = jax.random.normal(ks[1], (B, CTXN, CTX_DIM), jnp.float32)
        pos_map = jax.random.uniform(ks[2], (B, N, POS_DIM), jnp.float32)
        ctx_pos_map = jax.random.uniform(ks[3], (B, CTXN, POS_DIM), jnp.float32)
        Wq = jax.random.normal(ks[4], (DIM, DIM), jnp.float32) / np.sqrt(DIM)
        Wkv = jax.random.normal(ks[5], (CTX_DIM, 2 * DIM), jnp.float32) / np.sqrt(CTX_DIM)
        Wout = jax.random.normal(ks[6], (DIM, DIM), jnp.float32) / np.sqrt(DIM)
        bout = jnp.zeros((DIM,), jnp.float32)
        return {'x': x, 'ctx': ctx, 'pos_map': pos_map, 'ctx_pos_map': ctx_pos_map, 'Wq': Wq, 'Wkv': Wkv, 'Wout': Wout, 'bout': bout}
    _L0_xattn_all = _L0_xattn_setup()
    _L0_xattn_in = {k: v for k, v in _L0_xattn_all.items() if k in ('Wq', 'Wkv', 'Wout', 'bout')}
    del _L0_xattn_all

    def _L0_ffn_setup():
        import jax, jax.numpy as jnp
        import numpy as np
        H = 256
        I = 176
        E = 16
        G = 4
        TOPK_GROUP = 2
        K = 4
        SI = 2 * I
        SCALE = 1.0
        NORM = True
        B, S = (4, 64)

        def _swiglu(h):
            g, u = jnp.split(h, 2, axis=-1)
            return jax.nn.silu(g) * u

        def _combine_weights(xt, gate_w):
            T = xt.shape[0]
            scores = jax.nn.softmax(xt @ gate_w.T, axis=-1)
            group_scores = scores.reshape(T, G, E // G).max(axis=-1)
            _, gidx = jax.lax.top_k(group_scores, TOPK_GROUP)
            gmask = jnp.zeros((T, G), bool).at[jnp.arange(T)[:, None], gidx].set(True)
            emask = jnp.repeat(gmask, E // G, axis=1)
            masked = jnp.where(emask, scores, 0.0)
            w, eidx = jax.lax.top_k(masked, K)
            if NORM:
                w = w / (w.sum(-1, keepdims=True) + 1e-20)
            w = w * SCALE
            return jnp.zeros((T, E), xt.dtype).at[jnp.arange(T)[:, None], eidx].add(w)
        key = jax.random.key(seed)
        ks = jax.random.split(key, 6)
        sc = lambda fan_in: 1.0 / np.sqrt(fan_in)
        return {'x': jax.random.normal(ks[0], (B, S, H), jnp.float32), 'gate_w': jax.random.normal(ks[1], (E, H), jnp.float32) * sc(H), 'expert_up_w': jax.random.normal(ks[2], (E, 2 * I, H), jnp.float32) * sc(H), 'expert_down_w': jax.random.normal(ks[3], (E, H, I), jnp.float32) * sc(I), 'shared_up_w': jax.random.normal(ks[4], (2 * SI, H), jnp.float32) * sc(H), 'shared_down_w': jax.random.normal(ks[5], (H, SI), jnp.float32) * sc(SI)}
    _L0_ffn_all = _L0_ffn_setup()
    _L0_ffn_in = {k: v for k, v in _L0_ffn_all.items() if k in ('gate_w', 'expert_up_w', 'expert_down_w', 'shared_up_w', 'shared_down_w')}
    del _L0_ffn_all
    return {'x': x, 'ctx_1024': ctx_1024, 'fside_BxSx2_0': fside_BxSx2_0, 'L0_attn_Wq': _L0_attn_in['Wq'], 'L0_attn_bq': _L0_attn_in['bq'], 'L0_attn_Wk': _L0_attn_in['Wk'], 'L0_attn_bk': _L0_attn_in['bk'], 'L0_attn_Wv': _L0_attn_in['Wv'], 'L0_attn_bv': _L0_attn_in['bv'], 'L0_attn_Wo': _L0_attn_in['Wo'], 'L0_attn_bo': _L0_attn_in['bo'], 'L0_xattn_Wq': _L0_xattn_in['Wq'], 'L0_xattn_Wkv': _L0_xattn_in['Wkv'], 'L0_xattn_Wout': _L0_xattn_in['Wout'], 'L0_xattn_bout': _L0_xattn_in['bout'], 'L0_ffn_gate_w': _L0_ffn_in['gate_w'], 'L0_ffn_expert_up_w': _L0_ffn_in['expert_up_w'], 'L0_ffn_expert_down_w': _L0_ffn_in['expert_down_w'], 'L0_ffn_shared_up_w': _L0_ffn_in['shared_up_w'], 'L0_ffn_shared_down_w': _L0_ffn_in['shared_down_w']}

def reference(x, ctx_1024, fside_BxSx2_0, L0_attn_Wq, L0_attn_bq, L0_attn_Wk, L0_attn_bk, L0_attn_Wv, L0_attn_bv, L0_attn_Wo, L0_attn_bo, L0_xattn_Wq, L0_xattn_Wkv, L0_xattn_Wout, L0_xattn_bout, L0_ffn_gate_w, L0_ffn_expert_up_w, L0_ffn_expert_down_w, L0_ffn_shared_up_w, L0_ffn_shared_down_w):
    import jax
    import jax.numpy as jnp

    def _L0_attn_ref(q, Wq, bq, Wk, bk, Wv, bv, Wo, bo):
        import jax, jax.numpy as jnp
        import numpy as np
        B, S, DIN = (2, 256, 256)
        HQ, HKV, DH = (16, 1, 128)
        r = HQ // HKV
        lead = q.shape[:-1]
        k_lin = (q @ Wk + bk).reshape(*lead, HKV, DH)
        v_lin = (q @ Wv + bv).reshape(*lead, HKV, DH)
        qx = jnp.swapaxes(v_lin, -3, -2)
        kx = jnp.repeat(jnp.swapaxes(k_lin, -3, -2), r, axis=-3)
        vx = jnp.repeat(qx, r, axis=-3)
        scores = jnp.einsum('...jd,...id->...ji', qx, kx) / DH
        attn = jax.nn.softmax(scores, axis=-1)
        out = jnp.einsum('...jk,...kd->...jd', attn, vx)
        out = jnp.swapaxes(out, -3, -2).reshape(*lead, HQ * DH)
        return out @ Wo + bo

    def _L0_xattn_ref(x, ctx, pos_map, ctx_pos_map, Wq, Wkv, Wout, bout):
        import jax, jax.numpy as jnp
        import numpy as np
        DIM = 256
        CTX_DIM = 128
        N_HEADS = 32
        HEAD_DIM = DIM // N_HEADS
        POS_DIM = 2
        B, N, CTXN = (2, 256, 256)
        ROPE_BASE = 10000.0

        def apply_axial_rope(x, pos):
            b, n, h, d = x.shape
            p = pos.shape[-1]
            dpa = d // p
            half = dpa // 2
            freqs = ROPE_BASE ** (-jnp.arange(half, dtype=x.dtype) / half)
            ang = pos[..., :, None] * freqs
            cos = jnp.cos(ang)[:, :, None, :, :]
            sin = jnp.sin(ang)[:, :, None, :, :]
            xr = x.reshape(b, n, h, p, half, 2)
            x1, x2 = (xr[..., 0], xr[..., 1])
            out = jnp.stack([x1 * cos - x2 * sin, x1 * sin + x2 * cos], axis=-1)
            return out.reshape(b, n, h, d)
        b, n, _ = x.shape
        ctx_n = ctx.shape[1]
        q = (x @ Wq).reshape(b, n, N_HEADS, HEAD_DIM)
        k, v = jnp.split(ctx @ Wkv, 2, axis=-1)
        k = k.reshape(b, ctx_n, N_HEADS, HEAD_DIM)
        v = v.reshape(b, ctx_n, N_HEADS, HEAD_DIM)
        q = apply_axial_rope(q, pos_map)
        k = apply_axial_rope(k, ctx_pos_map)
        scale = 1.0 / np.sqrt(HEAD_DIM).astype(np.float32)
        logits = jnp.einsum('bqhd,bkhd->bhqk', q, k) * scale
        w = jax.nn.softmax(logits, axis=-1)
        attn = jnp.einsum('bhqk,bkhd->bqhd', w, v)
        attn = attn.reshape(b, n, N_HEADS * HEAD_DIM)
        return attn @ Wout + bout

    def _L0_ffn_ref(x, gate_w, expert_up_w, expert_down_w, shared_up_w, shared_down_w):
        import jax, jax.numpy as jnp
        import numpy as np
        H = 256
        I = 176
        E = 16
        G = 4
        TOPK_GROUP = 2
        K = 4
        SI = 2 * I
        SCALE = 1.0
        NORM = True
        B, S = (4, 64)

        def _swiglu(h):
            g, u = jnp.split(h, 2, axis=-1)
            return jax.nn.silu(g) * u

        def _combine_weights(xt, gate_w):
            T = xt.shape[0]
            scores = jax.nn.softmax(xt @ gate_w.T, axis=-1)
            group_scores = scores.reshape(T, G, E // G).max(axis=-1)
            _, gidx = jax.lax.top_k(group_scores, TOPK_GROUP)
            gmask = jnp.zeros((T, G), bool).at[jnp.arange(T)[:, None], gidx].set(True)
            emask = jnp.repeat(gmask, E // G, axis=1)
            masked = jnp.where(emask, scores, 0.0)
            w, eidx = jax.lax.top_k(masked, K)
            if NORM:
                w = w / (w.sum(-1, keepdims=True) + 1e-20)
            w = w * SCALE
            return jnp.zeros((T, E), xt.dtype).at[jnp.arange(T)[:, None], eidx].add(w)
        Bq, Sq, _ = x.shape
        xt = x.reshape(-1, H)
        cw = _combine_weights(xt, gate_w)
        out = jnp.zeros_like(xt)
        for e in range(E):
            a = _swiglu(xt @ expert_up_w[e].T)
            out = out + cw[:, e:e + 1] * (a @ expert_down_w[e].T)
        out = out + _swiglu(xt @ shared_up_w.T) @ shared_down_w.T
        return out.reshape(Bq, Sq, H)
    x = x + _L0_attn_ref(_layernorm(x, axis=-1), L0_attn_Wq, L0_attn_bq, L0_attn_Wk, L0_attn_bk, L0_attn_Wv, L0_attn_bv, L0_attn_Wo, L0_attn_bo)
    x = x + _L0_xattn_ref(_layernorm(x, axis=-1), ctx_1024, fside_BxSx2_0, fside_BxSx2_0, L0_xattn_Wq, L0_xattn_Wkv, L0_xattn_Wout, L0_xattn_bout)
    x = x + _L0_ffn_ref(_layernorm(x, axis=-1), L0_ffn_gate_w, L0_ffn_expert_up_w, L0_ffn_expert_down_w, L0_ffn_shared_up_w, L0_ffn_shared_down_w)
    return x

_drawn_inputs = setup_inputs


def setup_inputs(seed=0):
    import zlib

    import numpy as np

    out = dict(_drawn_inputs(seed))
    spreads = {'L0_attn_bq': (0.0, 0.1),
     'L0_attn_bk': (0.0, 0.1),
     'L0_attn_bv': (0.0, 0.1),
     'L0_attn_bo': (0.0, 0.1),
     'L0_xattn_bout': (0.0, 0.1)}
    factors = {}
    for name, (base, spread) in spreads.items():
        noise = np.random.default_rng([zlib.crc32(name.encode()), seed]).standard_normal(out[name].shape)
        drawn = base * np.exp(spread * noise) if base else spread * noise
        out[name] = jnp.asarray(drawn.astype(out[name].dtype))
    for name, factor in factors.items():
        out[name] = (out[name] * factor).astype(out[name].dtype)
    return out
```

```python
from contextlib import ExitStack

import concourse.bass as bass
from concourse import mybir

ALU = mybir.AluOpType
ACT = mybir.ActivationFunctionType
AX = mybir.AxisListType
F32 = mybir.dt.float32
BF16 = mybir.dt.bfloat16
I32 = mybir.dt.int32
U32 = mybir.dt.uint32

P = 128
D = 256
C2 = D // P
SEQ = 64
TOK = 2048
T = TOK // P
HEADS, HD = 32, 8
CTX = 128
E, TOPK, GROUPS, TOPG = 16, 4, 4, 2
INTER = 176
HALF_I = INTER // 2
SI = 352
SC = (SI + P - 1) // P
SIP = SC * P
REGION = TOK + P
ROW = D + 1 + E
PAD_TILE = E * REGION
RING = 8
RT = -(-((TOK * TOPK + E * (P - 1)) // P) // RING) * RING
ACC = TOK + P
EPS = 1e-5
XSCALE = float(HD) ** -0.5
ASCALE = 1.0 / 128.0
TWO_PI_HI = 6.28125
TWO_PI_LO = 6.283185307179586 - 6.28125
ROUND = 1.5 * 2.0 ** 23
PI_IN = 3.1415925
AHEAD = 3


def decoder_kernel(nc, x, ctxT, pos, wk, wv, bk, bv, wo, bo, xwq, xwk, xwv, xwout, xbout, gate, upw, downw,
                   supw, sdownw, identity, identity_b, head_mask, inject_rows, before, rope_freq, region_base, iota_e,
                   token_ids, pad_rows, tile_ids, ones_f, ones_b, out):
    with ExitStack() as ctx:
        def sb(name, shape, dt=F32):
            return ctx.enter_context(nc.sbuf_tensor(name, shape, dt))

        def sem(name):
            return ctx.enter_context(nc.semaphore(name))

        routed = nc.dram_tensor("routed", [PAD_TILE + P, ROW], F32).ap()
        acc = [nc.dram_tensor(f"acc{k}", [ACC, D], F32).ap() for k in range(2)]

        scores = ctx.enter_context(nc.psum_tensor("scores", [P, 2048], F32))
        B4, B5, B6, B7 = (ctx.enter_context(nc.psum_tensor(f"bank{k}", [P, 512], F32)) for k in range(4, 8))
        SB = [scores[:, 512 * k:512 * k + 512] for k in range(4)]

        ident = sb("ident", [P, P])
        hmask = sb("hmask", [P, 4])
        inj = sb("inj", [P, 512], BF16)
        tri = sb("tri", [P, P], BF16)
        ones = sb("ones", [P, P], BF16)
        identb = sb("identb", [P, P], BF16)
        onesf = sb("onesf", [P, P])
        freq = sb("freq", [P, 2])
        base_e = sb("base_e", [P, E])
        iota = sb("iota", [P, E])
        tokid = sb("tokid", [P, T], I32)
        tileid = sb("tileid", [P, 1])
        pad = sb("pad", [P, ROW])
        zeros = sb("zeros", [P, D])
        wk_s = sb("wk_s", [P, C2, P])
        wv_s = sb("wv_s", [P, C2, P])
        bk_s = sb("bk_s", [P, 1])
        bv_s = sb("bv_s", [P, 1])
        wosum = sb("wosum", [P, D])
        bo_s = sb("bo_s", [P, D])
        xwq_s = sb("xwq_s", [P, C2, 2, D])
        xwk_s = sb("xwk_s", [P, 2, D])
        xwv_s = sb("xwv_s", [P, D])
        xwout_s = sb("xwout_s", [P, C2, D])
        xbout_s = sb("xbout_s", [P, D])
        gate_s = sb("gate_s", [P, C2, E])
        up_s = sb("up_s", [P, E, C2, 2 * INTER])
        down_s = sb("down_s", [HALF_I, E, 2, D])
        sup_s = sb("sup_s", [P, C2, 2, SIP])
        sdown_s = sb("sdown_s", [P, SC, D])
        xres = sb("xres", [P, T, D])
        xn3T_all = sb("xn3T_all", [P, T, D])
        cosT = sb("cosT", [P, TOK])
        sinT = sb("sinT", [P, TOK])
        prob = sb("prob", [P, 2048])
        probT = sb("probT", [P, 16, P])
        ctxK = sb("ctxK", [P, P])
        ctxV = sb("ctxV", [P, 2, 2, SEQ])
        st = sb("st", [P, 6])
        ln = [(sb(f"mv{k}", [P, 2]), sb(f"lnv{k}", [P, 1]), sb(f"rs{k}", [P, 1]), sb(f"nt{k}", [P, 2]),
               sb(f"rstd{k}", [P, 1])) for k in range(3)]
        xn1 = sb("xn1", [P, D])
        xn1T = sb("xn1T", [P, D])
        xbo = sb("xbo", [P, D])
        kT1 = sb("kT1", [P, P])
        vT1 = sb("vT1", [P, P])
        v1 = sb("v1", [P, P])
        mx1 = sb("mx1", [P, 1])
        nmx1 = sb("nmx1", [P, 1])
        p1 = sb("p1", [P, P])
        p1n = sb("p1n", [P, P])
        sum1 = sb("sum1", [P, 1])
        rsum1 = sb("rsum1", [P, 1])
        p1T = sb("p1T", [P, P])
        oT1 = sb("oT1", [P, P])
        xn2 = sb("xn2", [P, D])
        xn2T = sb("xn2T", [P, D])
        xbout1 = sb("xbout1", [P, D])
        qr = sb("qr", [P, 2, P])
        qs = sb("qs", [P, 2, P])
        qT = sb("qT", [P, 2, P])
        kr = sb("kr", [P, 2, P])
        ks = sb("ks", [P, 2, P])
        kT = sb("kT", [P, 2, P])
        kblk = sb("kblk", [P, 2, 2, 4, SEQ])
        vblk = sb("vblk", [P, 2, 16, 2, 9])
        mS = sb("mS", [P, 4, 8])
        mstack = sb("mstack", [P, 4, 32], BF16)
        mT = sb("mT", [P, P], BF16)
        rden = sb("rden", [P, HEADS])
        o2 = sb("o2", [P, D])
        o2T = sb("o2T", [P, D])
        xrow = sb("xrow", [P, ROW])
        xn3T = sb("xn3T", [P, D])
        lmx = sb("lmx", [P, 1])
        lsh = sb("lsh", [P, E])
        lex = sb("lex", [P, E])
        lsum = sb("lsum", [P, 1])
        lrs = sb("lrs", [P, 1])
        prb = sb("prb", [P, E])
        gmax = sb("gmax", [P, 8])
        gtop = sb("gtop", [P, 8])
        gidx = sb("gidx", [P, 8], U32)
        gidf = sb("gidf", [P, TOPG])
        ghot = sb("ghot", [P, TOPG, GROUPS])
        gm = sb("gm", [P, GROUPS])
        msc = sb("msc", [P, E])
        etop = sb("etop", [P, 8])
        eidx = sb("eidx", [P, 8], U32)
        eidf = sb("eidf", [P, TOPK])
        ehot = sb("ehot", [P, TOPK, E])
        self32 = sb("self32", [P, E])
        sel = sb("sel", [P, E], BF16)
        msel = sb("msel", [P, E])
        wsum = sb("wsum", [P, 1])
        wsum1 = sb("wsum1", [P, 1])
        wrec = sb("wrec", [P, 1])
        macc = sb("macc", [P, E], BF16)
        slotE = sb("slotE", [P, E])
        slot4 = sb("slot4", [P, TOPK, E])
        slotf = sb("slotf", [P, TOPK])
        sloti = sb("sloti", [P, TOPK], I32)
        cnt = sb("cnt", [P, E])
        tail_f = sb("tail_f", [1, E])
        tail_i = sb("tail_i", [1, E], I32)
        cpad = sb("cpad", [P, E])
        cint = sb("cint", [P, E], I32)
        cfl = sb("cfl", [P, E])
        cgt = sb("cgt", [P, E])
        nt = sb("nt", [P, E])
        tend = sb("tend", [P, E])
        past = sb("past", [P, E])
        rowt = sb("rowt", [P, E])
        tcols = sb("tcols", [P, 4])
        tabT = sb("tabT", [1, 2, P], I32)
        sg = prob[:, 0:SIP]
        saT = prob[:, SIP:2 * SIP]
        y = [cosT[:, D * k:D * k + D] for k in range(RING)]
        xg = [(sinT[:], probT[:].rearrange("p c q -> p (c q)"))[k % 2][:, ROW * (k // 2):ROW * (k // 2) + ROW] for k in range(RING)]
        xgT = sb("xgT", [P, D])
        sil = sb("sil", [P, INTER])
        act_ = sb("act_", [P, INTER])
        aT = sb("aT", [HALF_I, 2, P])

        spare = {(eng.engine, k): eng.alloc_register(f"spare{k}") for eng in (nc.vector, nc.gpsimd) for k in range(2)}

        block = ctx.enter_context(nc.Block())

        S = {name: sem(name) for name in (
            "aT_ev aTp_done a_done abs_done acc_zeroed agg0 agg1 agg2 angle angle_step av_done "
            "bn0 bn1 bn2 c1_in cnt_done cos_done ctxK_in ctxV_in cw_done dn_done eidf_done eidx_done lmx_done wrec_done fin_add fin_in0 fin_in1 "
            "fin_step gate_done ident_in inj_done kT1_ev kT_done kblk_done kp_done kr_done ks_done lex_done "
            "lnv0 lnv1 lnv2 lsh_done mT_ev mTp_done macc_done max_done mhi_done mlo_done mx1_done nmx1_done "
            "nt0 nt1 nt2 o2T_ev o2Tp_done o2_done oT1_done oT1_ev out_done p1T_ev p1Tp_done p1a p1b p1n_done "
            "pad_out pads_done pos_in pr1_done pre_done prob_done qT_done q_done qkv1_done qr_done qs_done "
            "r_step rden_done rs00 rs01 rs02 rstd0 rstd1 rstd2 rsum1_done rw_in s1_done s_done saT_done "
            "scattered sdn_done sel_done selx_done sg_done sil_done sin_done slot4_done slotE_done "
            "slotf_done slots_done supg_done supu_done sw_in t_step tabTp_done tab_done tcols_done tok_done "
            "tpA_ev tpD_ev tp_done up_done v1_ev vT1_ev v_done vblk_ev vblk_set w1_in wo_in wosum_done "
            "wosum_step wout_done ws_step x0_in x1_done x2_done xTp_done x_in xbo_done xbout_done xgT_ev "
            "xn1T_ev xn1Tp_done xn1_done xn2T_ev xn2Tp_done xn2_done xn3T_ev xn3T_kept xn3Tp_done xn3_done "
            "xs_done xw_in y_done zero_set ").split()}
        S.update({f"xg_in{k}": sem(f"xg_in{k}") for k in range(RING)})
        S.update({f"added{k}": sem(f"added{k}") for k in range(2)})

        def tile_of(buf, t):
            return buf[:, bass.ds(t, 1), :].rearrange("p a d -> p (a d)")

        def hold(eng, count, k=0):
            if isinstance(count, int):
                return count
            eng.reg_add(spare[eng.engine, k], count, 0)
            return spare[eng.engine, k]

        def past_wait(eng):
            eng.wait_ge(S["zero_set"], 5)

        def fin_part(h, q):
            return ((cosT[:], sinT[:]), (prob[:], probT[:].rearrange("p c q -> p (c q)")))[h][q] \
                .rearrange("p (t d) -> p t d", d=D)

        def first(t):
            return isinstance(t, int) and t == 0

        def more(n):
            return not isinstance(n, int) or n + 1 < T

        def loop1(eng, body):
            for n in range(AHEAD):
                body(n, lambda k, n=n: k <= n)
            with eng.Fori(AHEAD, T - 1) as n:
                body(n, lambda k: True)
            for n in range(T - 1, T + AHEAD):
                body(n, lambda k, n=n: n - k < T)

        posb = xn3T_all[:, 0:8, :].rearrange("p t d -> p (t d)")
        angle = xn3T_all[:, 8:16, :].rearrange("p t d -> p (t d)")
        LN = [{what: f"{what}{k}" for what in ("bn", "agg", "lnv", "rs0", "nt", "rstd")} for k in range(3)]

        @block.sync
        def _(sp):
            sp.dma_start(ident[:], identity).then_inc(S["ident_in"], 16)
            sp.dma_start(tile_of(xres, 0), x[0:P, :]).then_inc(S["x0_in"], 16)
            sp.dma_start(wk_s[:], wk.rearrange("(c p) n -> p c n", p=P)).then_inc(S["w1_in"], 16)
            sp.dma_start(wv_s[:], wv.rearrange("(c p) n -> p c n", p=P)).then_inc(S["w1_in"], 16)
            sp.dma_start(bk_s[:], bk.rearrange("(p a) -> p a", a=1)).then_inc(S["w1_in"], 16)
            sp.dma_start(bv_s[:], bv.rearrange("(p a) -> p a", a=1)).then_inc(S["w1_in"], 16)
            sp.dma_start(bo_s[:], bo.partition_broadcast(P)).then_inc(S["w1_in"], 16)
            sp.dma_start(xres[:, 1:T, :], x[P:TOK, :].rearrange("(t p) d -> p t d", p=P)).then_inc(S["x_in"], 16)
            for dst, src in ((hmask, head_mask), (inj, inject_rows), (tri, before), (ones, ones_b), (identb, identity_b), (onesf, ones_f),
                             (base_e, region_base), (iota, iota_e), (tokid, token_ids), (tileid, tile_ids), (pad, pad_rows)):
                sp.dma_start(dst[:], src).then_inc(S["c1_in"], 16)
            sp.dma_start(xwq_s[:], xwq).then_inc(S["xw_in"], 16)
            sp.dma_start(xwout_s[:], xwout.rearrange("(c p) n -> p c n", p=P)).then_inc(S["xw_in"], 16)
            sp.dma_start(gate_s[:], gate.rearrange("(c p) n -> p c n", p=P)).then_inc(S["xw_in"], 16)

            def step(n, live):
                if live(0):
                    if not first(n):
                        sp.wait_ge(S["kp_done"], n)
                    sp.dma_start(ctxK[:], ctxT[:, bass.ds(n * P, P)]).then_inc(S["ctxK_in"], 16)
                if live(1):
                    if not first(n - 1):
                        sp.wait_ge(S["v_done"], n - 1)
                    for hp in range(2):
                        sp.dma_start(ctxV[:, :, hp, :], ctxT[:, bass.ds((n - 1) * P, P)].rearrange("c (s k) -> c s k", s=2)) \
                            .then_inc(S["ctxV_in"], 16)

            loop1(sp, step)

            sp.wait_ge(S["tab_done"], 2)
            sp.wait_ge(S["scattered"], 16 * TOPK * T)
            for e in range(E):
                end = sp.value_load(tail_i[0:1, e:e + 1], min_val=e * REGION, max_val=e * REGION + TOK)
                sp.dma_start(routed[bass.ds(end, P), :], pad[:]).then_inc(S["pads_done"], 16)
            sp.wait_ge(S["pads_done"], 16 * E)
            sp.wait_ge(S["pad_out"], 16)

            for k in range(RING):
                row = sp.value_load(tabT[0:1, 0, k:k + 1], min_val=0, max_val=PAD_TILE)
                sp.dma_start(xg[k], routed[bass.ds(row, P), :]).then_inc(S[f"xg_in{k}"], 16)
            with sp.Fori(1, RT // RING) as g:
                for k in range(RING):
                    sp.wait_ge(S[f"added{k % 2}"], g * 16 * (RING // 2) - 16 * (RING // 2 - 1 - k // 2))
                    row = sp.value_load(tabT[0:1, 0, bass.ds(g * RING + k, 1)], min_val=0, max_val=PAD_TILE)
                    sp.dma_start(xg[k], routed[bass.ds(row, P), :]).then_inc(S[f"xg_in{k}"], 16)

            sp.wait_ge(S["added0"], 16 * (RT // 2))
            sp.wait_ge(S["added1"], 16 * (RT // 2))
            for h in range(2):
                for q in range(2):
                    sp.dma_start(fin_part(h, q), acc[q][1024 * h:1024 * h + 1024, :].rearrange("(t p) d -> p t d", p=P)) \
                        .then_inc(S[f"fin_in{h}"], 16)
            for h in range(2):
                sp.wait_ge(S["fin_add"], h + 1)
                sp.dma_start(out[1024 * h:1024 * h + 1024, :].rearrange("(t p) d -> p t d", p=P),
                             xres[:, 8 * h:8 * h + 8, :]).then_inc(S["out_done"], 16)
            sp.wait_ge(S["out_done"], 32)

        @block.gpsimd
        def _(pool):
            pool.memset(zeros[:], 0.0).then_inc(S["zero_set"], 1)
            pool.memset(p1[:], 0.0).then_inc(S["zero_set"], 1)
            pool.memset(mstack[:], 0.0).then_inc(S["zero_set"], 1)
            pool.memset(macc[:], 0.0).then_inc(S["zero_set"], 1)
            pool.memset(gmax[:], -1.0).then_inc(S["zero_set"], 1)
            pool.memset(vblk[:], 0.0).then_inc(S["vblk_set"], 1)
            pool.wait_ge(S["vblk_set"], 1)
            for hp in range(2):
                pool.memset(vblk[64 * hp:64 * hp + 64, :, :, hp, 8:9], 1.0).then_inc(S["vblk_set"], 1)
            pool.wait_ge(S["vblk_set"], 3)
            pool.wait_ge(S["wo_in"], 32)
            wob = prob[:]
            wob2 = probT[:].rearrange("p c q -> p (c q)")
            pool.tensor_tensor(wob, wob, wob2, op=ALU.add).then_inc(S["wosum_step"], 1)
            for k, w in enumerate((1024, 512)):
                pool.wait_ge(S["wosum_step"], k + 1)
                pool.tensor_tensor(wob[:, 0:w], wob[:, 0:w], wob[:, w:2 * w], op=ALU.add).then_inc(S["wosum_step"], 1)
            pool.wait_ge(S["wosum_step"], 3)
            pool.tensor_tensor(wosum[:], wob[:, 0:D], wob[:, D:2 * D], op=ALU.add).then_inc(S["wosum_done"], 1)
            pool.wait_ge(S["w1_in"], 80)
            pool.wait_ge(S["x0_in"], 16)
            pool.wait_ge(S["x_in"], 16)
            pool.wait_ge(S["xw_in"], 16 * 6)

            def step(n, live):
                if live(0):
                    if not first(n):
                        pool.wait_ge(S["x1_done"], n)
                    pool.tensor_tensor(xbo[:], tile_of(xres, n), bo_s[:], op=ALU.add).then_inc(S["xbo_done"], 1)
                if live(2):
                    c = n - 2
                    pool.wait_ge(S["x1_done"], c + 1)
                    if not first(c):
                        pool.wait_ge(S["x2_done"], c)
                    pool.tensor_tensor(xbout1[:], tile_of(xres, c), xbout_s[:], op=ALU.add).then_inc(S["xbout_done"], 1)
                if live(3):
                    d = n - 3
                    pool.wait_ge(S["xn3T_ev"], d + 1)
                    pool.tensor_copy(tile_of(xn3T_all, d), xn3T[:]).then_inc(S["xn3T_kept"], 1)
                    pool.wait_ge(S["xn3_done"], d + 1)
                    pool.tensor_copy(xrow[:, D:D + 1].bitcast(I32), tokid[:, bass.ds(d, 1)]).then_inc(S["tok_done"], 1)
                    held = hold(pool, d + 1)
                    past_wait(pool)
                    pool.wait_ge(S["tok_done"], held)
                    pool.wait_ge(S["cw_done"], held)
                    pool.wait_ge(S["slots_done"], held)
                    for k in range(TOPK):
                        pool.indirect_dma_start(routed, bass.IndirectOffsetOnAxis(ap=sloti[:, k:k + 1], axis=0),
                                                xrow[:], None).then_inc(S["scattered"], 16)
                if live(0):
                    pool.wait_ge(S["ks_done"], n + 1)
                    pool.tensor_tensor(kT[:], kr[:], ks[:], op=ALU.add).then_inc(S["kT_done"], 1)
                    pool.wait_ge(S["kT_done"], n + 1)
                    if not first(n):
                        pool.wait_ge(S["s_done"], 2 * n)
                    pool.tensor_tensor(kblk[:].rearrange("p f b h k -> p (f b) h k"),
                                       kT[:].rearrange("p f (b k) -> p (f b) k", k=SEQ)[:, :, None, :].to_broadcast([P, 4, 4, SEQ]),
                                       hmask[:, None, :, None].to_broadcast([P, 4, 4, SEQ]), op=ALU.mult).then_inc(S["kblk_done"], 1)

            loop1(pool, step)

            pool.wait_ge(S["acc_zeroed"], 32)
            def add(t, k, seen):
                made = hold(pool, t + 1)
                before_it = None if seen is None else hold(pool, seen, 1)
                past_wait(pool)
                pool.wait_ge(S["y_done"], made)
                if before_it is not None:
                    pool.wait_ge(S[f"added{k % 2}"], before_it)
                pool.indirect_dma_start(acc[k % 2], bass.IndirectOffsetOnAxis(ap=xg[k][:, D:D + 1].bitcast(I32), axis=0),
                                        y[k], None, compute_op=ALU.add).then_inc(S[f"added{k % 2}"], 16)

            for k in range(RING):
                add(k, k, None if k < 2 else 16 * (k // 2))
            with pool.Fori(1, RT // RING) as g:
                for k in range(RING):
                    add(g * RING + k, k, g * 16 * (RING // 2) + 16 * (k // 2))

        @block.scalar
        def _(act):
            act.dma_start(freq[:], rope_freq).then_inc(S["pos_in"], 16)
            act.dma_start(posb, pos).then_inc(S["pos_in"], 16)
            act.dma_start(prob[:].rearrange("p (h n) -> p h n", n=D),
                          wo.rearrange("(h d) n -> d h n", d=P)[:, 0:8, :]).then_inc(S["wo_in"], 16)
            act.dma_start(probT[:].rearrange("p c q -> p (c q)").rearrange("p (h n) -> p h n", n=D),
                          wo.rearrange("(h d) n -> d h n", d=P)[:, 8:16, :]).then_inc(S["wo_in"], 16)
            act.dma_start(xwk_s[:], xwk.rearrange("v p n -> p v n")).then_inc(S["xw_in"], 16)
            act.dma_start(xwv_s[:], xwv).then_inc(S["xw_in"], 16)
            act.dma_start(xbout_s[:], xbout.partition_broadcast(P)).then_inc(S["xw_in"], 16)
            act.wait_ge(S["zero_set"], 5)
            for a in acc:
                act.dma_start(a.rearrange("(t p) d -> p t d", p=P),
                              zeros[:, None, :].to_broadcast([P, ACC // P, D])).then_inc(S["acc_zeroed"], 16)
            act.wait_ge(S["c1_in"], 16 * 11)
            act.dma_start(routed[PAD_TILE:PAD_TILE + P, :], pad[:]).then_inc(S["pad_out"], 16)
            act.dma_start(sup_s[:], supw).then_inc(S["sw_in"], 16)
            act.dma_start(sdown_s[:], sdownw.rearrange("(c p) n -> p c n", p=P)).then_inc(S["sw_in"], 16)
            act.dma_start(up_s[:], upw).then_inc(S["rw_in"], 16)
            act.dma_start(down_s[:], downw).then_inc(S["rw_in"], 16)
            act.wait_ge(S["angle"], 1)
            act.activation(sinT[:], angle, ACT.Sin, scale=freq[:, 1:2]).then_inc(S["sin_done"], 1)
            act.activation(posb, angle, ACT.Abs).then_inc(S["abs_done"], 1)
            act.wait_ge(S["abs_done"], 1)
            act.activation(cosT[:], posb, ACT.Sin, scale=-1.0, bias=1.5707963267948966).then_inc(S["cos_done"], 1)
            act.preload_act_table_set("natural_log_exp_and_others")

            def rsqrt(k, t):
                mv, lnv, rs, _, _ = ln[k]
                act.wait_ge(S[LN[k]["agg"]], t + 1)
                act.activation(lnv[:], mv[:, 1:2], ACT.Ln, bias=EPS).then_inc(S[LN[k]["lnv"]], 1)
                act.wait_ge(S[LN[k]["lnv"]], t + 1)
                act.activation(rs[:], lnv[:], ACT.Exp, scale=-0.5).then_inc(S[LN[k]["rs0"]], 1)

            def next_xn1T(t):
                act.wait_ge(S["xn1Tp_done"], t + 1)
                act.activation(xn1T[:], B4[:, 0:D], ACT.Copy).then_inc(S["xn1T_ev"], 1)

            rsqrt(0, 0)
            next_xn1T(0)

            def step(n, live):
                a, b, c, d = n, n - 1, n - 2, n - 3
                if live(0):
                    act.wait_ge(S["qkv1_done"], a + 1)
                    act.activation(kT1[:], B6[:, 0:P], ACT.Identity, bias=bk_s[:]).then_inc(S["kT1_ev"], 1)
                    act.activation(vT1[:], B6[:, P:2 * P], ACT.Identity, bias=bv_s[:]).then_inc(S["vT1_ev"], 1)
                    act.activation(v1[:], B6[:, 2 * P:3 * P], ACT.Copy).then_inc(S["v1_ev"], 1)
                if live(3):
                    act.wait_ge(S["xn3Tp_done"], d + 1)
                    if not first(d):
                        act.wait_ge(S["xn3T_kept"], d)
                    act.activation(xn3T[:], B5[:, 0:D], ACT.Copy).then_inc(S["xn3T_ev"], 1)
                if live(2):
                    act.wait_ge(S["tp_done"], 4 * c + 1)
                    act.activation(probT[:, 0:4, :].rearrange("p c q -> p (c q)"), B4[:], ACT.Copy).then_inc(S["tpA_ev"], 1)
                if live(3):
                    act.wait_ge(S["lsh_done"], d + 1)
                    act.activation(lex[:], lsh[:], ACT.Exp, accum_out=lsum[:]).then_inc(S["lex_done"], 1)
                if live(2):
                    act.wait_ge(S["tp_done"], 4 * c + 3)
                    act.activation(probT[:, 8:12, :].rearrange("p c q -> p (c q)"), B4[:], ACT.Copy).then_inc(S["tpA_ev"], 1)
                if live(0):
                    for h, name in ((0, "p1a"), (1, "p1b")):
                        r = slice(SEQ * h, SEQ * h + SEQ)
                        if h == 0:
                            act.wait_ge(S["nmx1_done"], a + 1)
                            if not first(a):
                                act.wait_ge(S["p1n_done"], a)
                        act.activation(p1[r, r], B5[r, r], ACT.Exp, bias=nmx1[r, :], scale=ASCALE,
                                       accum_out=sum1[r, :]).then_inc(S[name], 1)
                if live(1):
                    act.wait_ge(S["xn2Tp_done"], b + 1)
                    act.activation(xn2T[:], B6[:, 0:D], ACT.Copy).then_inc(S["xn2T_ev"], 1)
                if live(0):
                    act.wait_ge(S["p1Tp_done"], a + 1)
                    act.activation(p1T[:], B5[:, 0:P], ACT.Copy).then_inc(S["p1T_ev"], 1)
                if more(n):
                    rsqrt(0, n + 1)
                if live(0):
                    act.wait_ge(S["oT1_done"], a + 1)
                    act.activation(oT1[:], B5[:, 0:P], ACT.Identity, bias=bv_s[:]).then_inc(S["oT1_ev"], 1)
                if live(1):
                    act.wait_ge(S["v_done"], b + 1)
                    if first(b):
                        act.wait_ge(S["vblk_set"], 3)
                    if live(2):
                        act.wait_ge(S["av_done"], c + 1)
                    for hp in range(2):
                        r = slice(64 * hp, 64 * hp + 64)
                        act.activation(vblk[r, :, :, hp, 0:8],
                                       B7[r, :].rearrange("p (b c h d) -> p b c h d", b=2, h=2, d=HD)[:, :, :, hp, :],
                                       ACT.Copy).then_inc(S["vblk_ev"], 1)
                if live(2):
                    act.wait_ge(S["o2Tp_done"], c + 1)
                    act.activation(o2T[:], B5[:, 0:D], ACT.Copy).then_inc(S["o2T_ev"], 1)
                if live(0):
                    rsqrt(1, a)
                if more(n):
                    next_xn1T(n + 1)
                if live(1):
                    act.wait_ge(S["mTp_done"], b + 1)
                    act.activation(mT[:], B6[:, 0:64].bitcast(BF16), ACT.Copy).then_inc(S["mT_ev"], 1)
                if live(2):
                    rsqrt(2, c)
                if live(1):
                    for h in range(2):
                        act.wait_ge(S["inj_done"], 2 * b + 1 + h)
                        if h == 0 and not first(b):
                            act.wait_ge(S["tp_done"], 4 * b)
                        act.activation(prob[:, 1024 * h:1024 * h + 1024], scores[:, 1024 * h:1024 * h + 1024],
                                       ACT.Exp, scale=XSCALE).then_inc(S["prob_done"], 1)

            loop1(act, step)

            act.preload_act_table_set("silu_and_others")

            def shared(t):
                act.wait_ge(S["supg_done"], t + 1)
                if not first(t):
                    act.wait_ge(S["saT_done"], t)
                act.activation(sg, SB[0][:, 0:SIP], ACT.Silu).then_inc(S["sg_done"], 1)

            shared(0)
            with act.Fori(1, T) as t:
                shared(t)

            def transposed(k, n):
                act.wait_ge(S["xTp_done"], n)
                act.activation(xgT[:], B4[:, 0:D], ACT.Copy).then_inc(S["xgT_ev"], 1)

            def routed_tile(t, k, more):
                act.wait_ge(S["up_done"], t + 1)
                act.activation(sil[:], SB[0][:, 0:INTER], ACT.Silu).then_inc(S["sil_done"], 1)
                if more:
                    transposed(k, t + 2)
                act.wait_ge(S["aTp_done"], t + 1)
                act.activation(aT[:].rearrange("p c q -> p (c q)"), SB[2][0:HALF_I, 0:2 * P], ACT.Copy).then_inc(S["aT_ev"], 1)

            transposed(0, 1)
            for k in range(RING):
                routed_tile(k, k, True)
            with act.Fori(1, RT // RING - 1) as g:
                for k in range(RING):
                    routed_tile(g * RING + k, k, True)
            for k in range(RING):
                routed_tile(RT - RING + k, k, k < RING - 1)

        @block.vector
        def _(dve):
            dve.wait_ge(S["pos_in"], 32)
            st_n = [0]

            def turn(ins):
                ins.then_inc(S["angle_step"], 1)
                st_n[0] += 1
                dve.wait_ge(S["angle_step"], st_n[0])

            turn(dve.tensor_scalar(angle, posb, freq[:, 0:1], None, ALU.mult))
            turn(dve.tensor_scalar(cosT[:], angle, 1.0 / 6.283185307179586, ROUND, ALU.mult, ALU.add))
            turn(dve.tensor_scalar(cosT[:], cosT[:], ROUND, None, ALU.subtract))
            turn(dve.scalar_tensor_tensor(sinT[:], cosT[:], -TWO_PI_HI, angle, ALU.mult, ALU.add))
            turn(dve.scalar_tensor_tensor(angle, cosT[:], -TWO_PI_LO, sinT[:], ALU.mult, ALU.add))
            dve.tensor_scalar(angle, angle, PI_IN, -PI_IN, ALU.min, ALU.max).then_inc(S["angle"], 1)

            def ln_stats(k, t):
                mv = ln[k][0]
                dve.bn_stats(st[:], tile_of(xres, t)).then_inc(S[LN[k]["bn"]], 1)
                held = hold(dve, t + 1)
                past_wait(dve)
                dve.wait_ge(S[LN[k]["bn"]], held)
                dve.bn_aggr(mv[:], st[:]).then_inc(S[LN[k]["agg"]], 1)

            def ln_finish(k, t, dst):
                mv, _, rs, ntm, rstd = ln[k]
                dve.wait_ge(S[LN[k]["rs0"]], t + 1)
                dve.tensor_scalar(ntm[:, 0:1], mv[:, 1:2], EPS, rs[:], ALU.add, ALU.mult).then_inc(S[LN[k]["nt"]], 1)
                dve.wait_ge(S[LN[k]["nt"]], 2 * t + 1)
                dve.tensor_scalar(ntm[:, 1:2], ntm[:, 0:1], rs[:], -0.5, ALU.mult, ALU.mult).then_inc(S[LN[k]["nt"]], 1)
                dve.wait_ge(S[LN[k]["nt"]], 2 * t + 2)
                dve.tensor_scalar(rstd[:], ntm[:, 1:2], 1.5, rs[:], ALU.add, ALU.mult).then_inc(S[LN[k]["rstd"]], 1)
                dve.wait_ge(S[LN[k]["rstd"]], t + 1)
                return dve.tensor_scalar(dst, tile_of(xres, t), mv[:, 0:1], rstd[:], ALU.subtract, ALU.mult)

            dve.wait_ge(S["x0_in"], 16)
            ln_stats(0, 0)
            dve.wait_ge(S["x_in"], 16)
            ln_finish(0, 0, xn1[:]).then_inc(S["xn1_done"], 1)
            dve.wait_ge(S["c1_in"], 176)
            dve.wait_ge(S["zero_set"], 5)
            dve.wait_ge(S["cos_done"], 1)
            dve.wait_ge(S["sin_done"], 1)

            def logits(d):
                dve.wait_ge(S["gate_done"], d + 1)
                dve.reduce_max(lmx[:], B6[:, 0:E], AX.X).then_inc(S["lmx_done"], 1)
                dve.wait_ge(S["lmx_done"], d + 1)
                dve.tensor_scalar(lsh[:], B6[:, 0:E], lmx[:], None, ALU.subtract).then_inc(S["lsh_done"], 1)

            def route(d):
                R = 14
                k = [0]

                def then(ins, next_is_max=False):
                    ins.then_inc(S["r_step"], 1)
                    k[0] += 1
                    if next_is_max:
                        held = hold(dve, d * R + k[0])
                        past_wait(dve)
                        dve.wait_ge(S["r_step"], held)
                    else:
                        dve.wait_ge(S["r_step"], d * R + k[0])

                dve.wait_ge(S["lex_done"], d + 1)
                then(dve.reciprocal(lrs[:], lsum[:]))
                then(dve.tensor_scalar(prb[:], lex[:], lrs[:], None, ALU.mult))
                then(dve.reduce_max(gmax[:, 0:GROUPS], prb[:].rearrange("p (g e) -> p g e", g=GROUPS), AX.X), True)
                then(dve.max(gtop[:], gmax[:]), True)
                then(dve.max_index(gidx[:], gtop[:], gmax[:]))
                then(dve.tensor_copy(gidf[:], gidx[:, 0:TOPG]))
                then(dve.tensor_tensor(ghot[:], gidf[:, :, None].to_broadcast([P, TOPG, GROUPS]),
                                       iota[:, None, 0:GROUPS].to_broadcast([P, TOPG, GROUPS]), op=ALU.is_equal))
                then(dve.tensor_tensor(gm[:], ghot[:, 0, :], ghot[:, 1, :], op=ALU.add))
                then(dve.tensor_tensor(msc[:].rearrange("p (g e) -> p g e", g=GROUPS), prb[:].rearrange("p (g e) -> p g e", g=GROUPS),
                                       gm[:, :, None].to_broadcast([P, GROUPS, E // GROUPS]), op=ALU.mult), True)
                then(dve.max(etop[:], msc[:]), True)
                dve.max_index(eidx[:], etop[:], msc[:]).then_inc(S["eidx_done"], 1)
                dve.reduce_sum(wsum[:], etop[:, 0:TOPK], AX.X).then_inc(S["ws_step"], 1)
                dve.wait_ge(S["eidx_done"], d + 1)
                dve.tensor_copy(eidf[:], eidx[:, 0:TOPK]).then_inc(S["eidf_done"], 1)
                dve.wait_ge(S["ws_step"], d + 1)
                then(dve.tensor_scalar(wsum1[:], wsum[:], 1e-20, None, ALU.add))
                dve.reciprocal(wrec[:], wsum1[:]).then_inc(S["wrec_done"], 1)
                dve.wait_ge(S["eidf_done"], d + 1)
                then(dve.tensor_tensor(ehot[:], eidf[:, :, None].to_broadcast([P, TOPK, E]),
                                       iota[:, None, :].to_broadcast([P, TOPK, E]), op=ALU.is_equal))
                then(dve.tensor_reduce(self32[:], ehot[:].rearrange("p k e -> p e k"), AX.X, ALU.add))
                dve.tensor_copy(sel[:], self32[:]).then_inc(S["sel_done"], 1)
                dve.wait_ge(S["wrec_done"], d + 1)
                then(dve.tensor_tensor(msel[:], msc[:], self32[:], op=ALU.mult))
                assert k[0] == R, k
                if not first(d):
                    dve.wait_ge(S["scattered"], d * 16 * TOPK)
                dve.tensor_scalar(xrow[:, D + 1:ROW], msel[:], wrec[:], None, ALU.mult).then_inc(S["cw_done"], 1)

            def step(n, live):
                a, b, c, d = n, n - 1, n - 2, n - 3
                if live(2):
                    dve.wait_ge(S["tp_done"], 4 * c + 2)
                    dve.tensor_copy(probT[:, 4:8, :].rearrange("p c q -> p (c q)"), B7[:]).then_inc(S["tpD_ev"], 1)
                if live(3):
                    logits(d)
                if live(0):
                    dve.wait_ge(S["s1_done"], a + 1)
                    for h in range(2):
                        r = slice(SEQ * h, SEQ * h + SEQ)
                        dve.reduce_max(mx1[r, :], B5[r, r], AX.X).then_inc(S["mx1_done"], 1)
                    dve.wait_ge(S["mx1_done"], 2 * a + 2)
                    dve.tensor_scalar(nmx1[:], mx1[:], -ASCALE, None, ALU.mult).then_inc(S["nmx1_done"], 1)
                if live(2):
                    dve.wait_ge(S["tp_done"], 4 * c + 4)
                    dve.tensor_copy(probT[:, 12:16, :].rearrange("p c q -> p (c q)"), B7[:]).then_inc(S["tpD_ev"], 1)
                if live(0):
                    dve.wait_ge(S["p1a"], a + 1)
                    dve.wait_ge(S["p1b"], a + 1)
                    dve.reciprocal(rsum1[:], sum1[:]).then_inc(S["rsum1_done"], 1)
                    dve.wait_ge(S["rsum1_done"], a + 1)
                    dve.tensor_scalar(p1n[:], p1[:], rsum1[:], None, ALU.mult).then_inc(S["p1n_done"], 1)
                if live(3):
                    route(d)
                if live(1):
                    dve.wait_ge(S["q_done"], b + 1)
                    rope(B6, qr, qs, b, "qr_done", "qs_done")
                    dve.wait_ge(S["qs_done"], b + 1)
                    dve.tensor_tensor(qT[:], qr[:], qs[:], op=ALU.add).then_inc(S["qT_done"], 1)
                if more(n):
                    ln_stats(0, n + 1)
                if live(2):
                    dve.wait_ge(S["av_done"], c + 1)
                    av = B4[:, 0:HEADS * 9].rearrange("p (h d) -> p h d", d=9)
                    dve.reciprocal(rden[:, :, None], av[:, :, 8:9]).then_inc(S["rden_done"], 1)
                    dve.wait_ge(S["rden_done"], c + 1)
                    dve.tensor_tensor(o2[:].rearrange("p (h d) -> p h d", d=HD), av[:, :, 0:HD],
                                      rden[:, :, None].to_broadcast([P, HEADS, HD]), op=ALU.mult).then_inc(S["o2_done"], 1)
                if more(n):
                    ln_finish(0, n + 1, xn1[:]).then_inc(S["xn1_done"], 1)
                if live(3):
                    dve.wait_ge(S["pre_done"], d + 1)
                    dve.tensor_tensor(slotE[:], B6[:, 0:E], base_e[:], op=ALU.add).then_inc(S["slotE_done"], 1)
                    dve.tensor_tensor(macc[:], macc[:], sel[:], op=ALU.add).then_inc(S["macc_done"], 1)
                    dve.wait_ge(S["slotE_done"], d + 1)
                    dve.tensor_tensor(slot4[:], ehot[:], slotE[:, None, :].to_broadcast([P, TOPK, E]), op=ALU.mult) \
                        .then_inc(S["slot4_done"], 1)
                    dve.wait_ge(S["slot4_done"], d + 1)
                    dve.reduce_sum(slotf[:], slot4[:], AX.X).then_inc(S["slotf_done"], 1)
                    dve.wait_ge(S["slotf_done"], d + 1)
                    dve.tensor_copy(sloti[:], slotf[:]).then_inc(S["slots_done"], 1)
                if live(0):
                    dve.wait_ge(S["pr1_done"], a + 1)
                    dve.wait_ge(S["xbo_done"], a + 1)
                    dve.tensor_tensor(tile_of(xres, a), B4[:, 0:D], xbo[:], op=ALU.add).then_inc(S["x1_done"], 1)
                    held = hold(dve, a + 1)
                    past_wait(dve)
                    dve.wait_ge(S["x1_done"], held)
                    ln_stats(1, a)
                if live(1):
                    maxima(b, 0)
                if live(0):
                    ln_finish(1, a, xn2[:]).then_inc(S["xn2_done"], 1)
                if live(1):
                    maxima(b, 1)
                    dve.wait_ge(S["max_done"], 2 * b + 2)
                    dve.tensor_scalar(mstack[:, :, 0:8], mS[:], -1.0, None, ALU.mult).then_inc(S["mhi_done"], 1)
                    dve.wait_ge(S["mhi_done"], b + 1)
                    dve.scalar_tensor_tensor(mstack[:, :, 8:16], mS[:], -1.0, mstack[:, :, 0:8], ALU.mult, ALU.subtract) \
                        .then_inc(S["mlo_done"], 1)
                if live(2):
                    dve.wait_ge(S["wout_done"], c + 1)
                    dve.wait_ge(S["xbout_done"], c + 1)
                    dve.tensor_tensor(tile_of(xres, c), B5[:, 0:D], xbout1[:], op=ALU.add).then_inc(S["x2_done"], 1)
                    held = hold(dve, c + 1)
                    past_wait(dve)
                    dve.wait_ge(S["x2_done"], held)
                    ln_stats(2, c)
                if live(0):
                    dve.wait_ge(S["kp_done"], a + 1)
                    if not first(a):
                        dve.wait_ge(S["kT_done"], a)
                    rope(B7, kr, ks, a, "kr_done", "ks_done")
                if live(2):
                    if not first(c):
                        dve.wait_ge(S["scattered"], c * 16 * TOPK)
                    ln_finish(2, c, xrow[:, 0:D]).then_inc(S["xn3_done"], 1)

            def maxima(t, h):
                dve.wait_ge(S["s_done"], 2 * t + 1 + h)
                dve.reduce_max(mS[:, 2 * h:2 * h + 2, :], scores[:, 1024 * h:1024 * h + 1024]
                               .rearrange("p (r h k) -> p r h k", r=2, k=SEQ), AX.X).then_inc(S["max_done"], 1)

            def rope(bank, r, s_, t, r_name, s_name):
                both = bank[:].rearrange("p (f v q) -> p f v q", f=2, v=2)
                tab = lambda x: x[:, None, bass.ds(t * P, P)].to_broadcast([P, 2, P])
                dve.tensor_tensor(r[:], both[:, :, 0, :], tab(cosT), op=ALU.mult).then_inc(S[r_name], 1)
                dve.tensor_tensor(s_[:], both[:, :, 1, :], tab(sinT), op=ALU.mult).then_inc(S[s_name], 1)

            loop1(dve, step)

            dve.wait_ge(S["cnt_done"], 1)
            tn = [0]

            def then(ins):
                ins.then_inc(S["t_step"], 1)
                tn[0] += 1
                dve.wait_ge(S["t_step"], tn[0])

            then(dve.tensor_copy(cnt[:], B5[:, 0:E]))
            then(dve.tensor_tensor(tail_f[:], cnt[0:1, :], base_e[0:1, :], op=ALU.add))
            dve.tensor_copy(tail_i[:], tail_f[:]).then_inc(S["tab_done"], 1)
            then(dve.tensor_scalar(cpad[:], cnt[:], 1.0 / P, (P - 1.0) / (2 * P), ALU.mult, ALU.add))
            then(dve.tensor_scalar(cfl[:], cpad[:], ROUND, None, ALU.add))
            then(dve.tensor_scalar(nt[:], cfl[:], ROUND, None, ALU.subtract))
            then(dve.tensor_tensor_scan(tend[:], onesf[:, 0:E], nt[:], 0.0, ALU.mult, ALU.add))
            then(dve.tensor_scalar(past[:], tend[:], tileid[:], None, ALU.is_le))
            then(dve.reduce_sum(tcols[:, 2:3], past[:], AX.X))
            then(dve.tensor_tensor(rowt[:], past[:], nt[:], op=ALU.mult))
            then(dve.reduce_sum(tcols[:, 3:4], rowt[:], AX.X))
            then(dve.tensor_scalar(tcols[:, 1:2], tcols[:, 2:3], E - 1.0, None, ALU.min))
            then(dve.tensor_scalar(cgt[:, 0:1], tcols[:, 2:3], float(E), float(P), ALU.is_lt, ALU.mult))
            then(dve.tensor_tensor(cgt[:, 1:2], tileid[:], tcols[:, 3:4], op=ALU.subtract))
            then(dve.tensor_tensor(cgt[:, 2:3], cgt[:, 0:1], cgt[:, 1:2], op=ALU.mult))
            dve.scalar_tensor_tensor(tcols[:, 0:1], tcols[:, 2:3], float(REGION), cgt[:, 2:3], ALU.mult, ALU.add) \
                .then_inc(S["tcols_done"], 1)
            dve.wait_ge(S["tabTp_done"], 1)
            dve.tensor_copy(tabT[:].rearrange("a b t -> a (b t)"), B5[0:1, 0:2 * P]).then_inc(S["tab_done"], 1)

            def shared_act(t):
                dve.wait_ge(S["sg_done"], t + 1)
                dve.wait_ge(S["supu_done"], t + 1)
                if not first(t):
                    dve.wait_ge(S["sdn_done"], t)
                dve.tensor_tensor(saT, sg, SB[1][:, 0:SIP], op=ALU.mult).then_inc(S["saT_done"], 1)

            def shared_sum(t):
                dve.wait_ge(S["sdn_done"], t + 1)
                dve.tensor_tensor(tile_of(xres, t), SB[2][:, 0:D], tile_of(xres, t), op=ALU.add).then_inc(S["xs_done"], 1)

            shared_act(0)
            with dve.Fori(1, T) as t:
                shared_act(t)
                shared_sum(t - 1)
            shared_sum(T - 1)

            dve.wait_ge(S["tab_done"], 2)

            def gated(t):
                dve.wait_ge(S["sil_done"], t + 1)
                dve.tensor_tensor(act_[:], sil[:], SB[0][:, INTER:2 * INTER], op=ALU.mult).then_inc(S["a_done"], 1)

            def weighted(t, k):
                dve.wait_ge(S["dn_done"], t + 1)
                e = dve.value_load(tabT[0:1, 1, bass.ds(t, 1)], min_val=0, max_val=E - 1)
                dve.tensor_scalar(y[k], SB[1][:, 0:D], xg[k][:, bass.ds(e + (D + 1), 1)], None, ALU.mult).then_inc(S["y_done"], 1)

            for k in range(RING):
                gated(k)
                if k:
                    weighted(k - 1, k - 1)
            with dve.Fori(1, RT // RING) as g:
                for k in range(RING):
                    gated(g * RING + k)
                    weighted(g * RING + k - 1, (k - 1) % RING)
            weighted(RT - 1, RING - 1)

            for h in range(2):
                dve.wait_ge(S[f"fin_in{h}"], 32)
                part = xres[:, 8 * h:8 * h + 8, :]
                dve.tensor_tensor(part, part, fin_part(h, 0), op=ALU.add).then_inc(S["fin_step"], 1)
                dve.wait_ge(S["fin_step"], h + 1)
                dve.tensor_tensor(part, part, fin_part(h, 1), op=ALU.add).then_inc(S["fin_add"], 1)

        @block.tensor
        def _(pe):
            pe.wait_ge(S["ident_in"], 16)
            pe.wait_ge(S["w1_in"], 80)
            pe.wait_ge(S["wosum_done"], 1)
            pe.wait_ge(S["xw_in"], 96)
            pe.wait_ge(S["c1_in"], 176)

            def transpose2(bank, src):
                for h in range(2):
                    last = pe.transpose(bank[:, h * P:h * P + P], src[:, h * P:h * P + P], ident[:])
                return last

            def quarter(bank, q):
                for j in range(4):
                    cc = 4 * q + j
                    last = pe.transpose(bank[:, j * P:j * P + P], prob[:, cc * P:cc * P + P], ident[:])
                return last

            def av_half(h):
                for cc in range(8 * h, 8 * h + 8):
                    for s_ in range(2):
                        r = slice(SEQ * s_, SEQ * s_ + SEQ)
                        last = pe.matmul(B4[r, 18 * cc:18 * cc + 18], probT[:, cc, r],
                                         vblk[:, s_, cc, :, :].rearrange("p h d -> p (h d)"), start=True, stop=True)
                return last

            def next_xn1T(t):
                pe.wait_ge(S["xn1_done"], t + 1)
                if not first(t):
                    pe.wait_ge(S["x1_done"], t)
                transpose2(B4, xn1).then_inc(S["xn1Tp_done"], 1)

            def step(n, live):
                a, b, c, d = n, n - 1, n - 2, n - 3
                if live(0):
                    pe.wait_ge(S["xn1T_ev"], a + 1)
                    if live(2):
                        pe.wait_ge(S["mT_ev"], b)
                    elif not first(a):
                        pe.wait_ge(S["v1_ev"], a)
                    for i, w in enumerate((wk_s, wv_s)):
                        for h in range(C2):
                            pe.matmul(B6[:, i * P:i * P + P], w[:, h, :], xn1T[:, h * P:h * P + P], start=h == 0, stop=h == 1)
                    for h in range(C2):
                        last = pe.matmul(B6[:, 2 * P:3 * P], xn1T[:, h * P:h * P + P], wv_s[:, h, :], start=h == 0, stop=h == 1)
                    last.then_inc(S["qkv1_done"], 1)
                if live(3):
                    pe.wait_ge(S["xn3_done"], d + 1)
                    transpose2(B5, xrow).then_inc(S["xn3Tp_done"], 1)
                if live(2):
                    pe.wait_ge(S["prob_done"], 2 * c + 1)
                    if live(0):
                        pe.wait_ge(S["xn1T_ev"], a + 1)
                        pe.wait_ge(S["ks_done"], a)
                    else:
                        pe.wait_ge(S["x1_done"], T)
                        pe.wait_ge(S["o2_done"], c)
                        pe.wait_ge(S["ks_done"], T)
                        pe.wait_ge(S["vblk_ev"], 2 * c + 2)
                    quarter(B4, 0).then_inc(S["tp_done"], 1)
                    quarter(B7, 1).then_inc(S["tp_done"], 1)
                if live(3):
                    pe.wait_ge(S["xn3T_ev"], d + 1)
                    if live(0):
                        pe.wait_ge(S["v1_ev"], a + 1)
                    elif live(2):
                        pe.wait_ge(S["mT_ev"], c + 1)
                    else:
                        pe.wait_ge(S["slotE_done"], d)
                    for h in range(C2):
                        last = pe.matmul(B6[:, 0:E], xn3T[:, h * P:h * P + P], gate_s[:, h, :], start=h == 0, stop=h == 1)
                    last.then_inc(S["gate_done"], 1)
                if live(0):
                    pe.wait_ge(S["kT1_ev"], a + 1)
                    pe.wait_ge(S["vT1_ev"], a + 1)
                    if not live(3) and not first(a):
                        pe.wait_ge(S["oT1_ev"], a)
                    pe.matmul(B5[:, 0:P], vT1[:], kT1[:], start=True, stop=True).then_inc(S["s1_done"], 1)
                if live(2):
                    pe.wait_ge(S["prob_done"], 2 * c + 2)
                    pe.wait_ge(S["tpA_ev"], 2 * c + 1)
                    quarter(B4, 2).then_inc(S["tp_done"], 1)
                    pe.wait_ge(S["tpD_ev"], 2 * c + 1)
                    quarter(B7, 3).then_inc(S["tp_done"], 1)
                if live(1):
                    pe.wait_ge(S["xn2_done"], b + 1)
                    if live(3):
                        pe.wait_ge(S["lsh_done"], d + 1)
                    else:
                        pe.wait_ge(S["v1_ev"], a + 1)
                    transpose2(B6, xn2).then_inc(S["xn2Tp_done"], 1)
                if live(2):
                    pe.wait_ge(S["tpA_ev"], 2 * c + 2)
                    pe.wait_ge(S["tpD_ev"], 2 * c + 1)
                    pe.wait_ge(S["vblk_ev"], 2 * c + 2)
                    av_half(0)
                if live(1):
                    pe.wait_ge(S["xn2T_ev"], b + 1)
                    for f in range(2):
                        for v in range(2):
                            o = (2 * f + v) * P
                            for h in range(C2):
                                last = pe.matmul(B6[:, o:o + P], xwq_s[:, h, v, f * P:f * P + P], xn2T[:, h * P:h * P + P],
                                                 start=h == 0, stop=h == 1)
                    last.then_inc(S["q_done"], 1)
                if live(0):
                    pe.wait_ge(S["p1n_done"], a + 1)
                    pe.transpose(B5[:, 0:P], p1n[:], ident[:]).then_inc(S["p1Tp_done"], 1)
                if live(2):
                    pe.wait_ge(S["tpD_ev"], 2 * c + 2)
                    av_half(1).then_inc(S["av_done"], 1)
                if live(0):
                    pe.wait_ge(S["p1T_ev"], a + 1)
                    pe.matmul(B5[:, 0:P], v1[:], p1T[:], start=True, stop=True).then_inc(S["oT1_done"], 1)
                if live(1):
                    pe.wait_ge(S["ctxV_in"], 32 * (b + 1))
                    if not live(2):
                        pe.wait_ge(S["ks_done"], a)
                    for s_ in range(2):
                        last = pe.matmul(B7[:, D * s_:D * s_ + D], ctxV[:, s_, :, :].rearrange("c h k -> c (h k)"),
                                         xwv_s[:], start=True, stop=True)
                    last.then_inc(S["v_done"], 1)
                if live(2):
                    pe.wait_ge(S["o2_done"], c + 1)
                    if live(0):
                        pe.wait_ge(S["oT1_ev"], a + 1)
                    else:
                        pe.wait_ge(S["xn3T_ev"], d + 1)
                    transpose2(B5, o2).then_inc(S["o2Tp_done"], 1)
                if live(3):
                    pe.wait_ge(S["sel_done"], d + 1)
                    if live(1):
                        pe.wait_ge(S["qs_done"], b + 1)
                    if not first(d):
                        pe.wait_ge(S["macc_done"], d)
                    pe.matmul(B6[:, 0:E], tri[:], sel[:], start=True, stop=False)
                    pe.matmul(B6[:, 0:E], ones[:], macc[:], start=False, stop=True).then_inc(S["pre_done"], 1)
                if live(0):
                    pe.wait_ge(S["oT1_ev"], a + 1)
                    pe.matmul(B4[:, 0:D], oT1[:], wosum[:], start=True, stop=True).then_inc(S["pr1_done"], 1)
                if live(1):
                    pe.wait_ge(S["qT_done"], b + 1)
                    pe.wait_ge(S["kblk_done"], b + 1)
                    if not first(b):
                        pe.wait_ge(S["prob_done"], 2 * b)
                    for pair in range(2):
                        for f in range(2):
                            for r_ in (2 * pair, 2 * pair + 1):
                                g = slice(32 * r_, 32 * r_ + 32)
                                for s_ in range(2):
                                    q = slice(SEQ * s_, SEQ * s_ + SEQ)
                                    last = pe.matmul(SB[r_][q, D * f:D * f + D], qT[g, f, q],
                                                     kblk[g, f, s_, :, :].rearrange("p h k -> p (h k)"),
                                                     start=f == 0, stop=False, skip_group_check=True)
                        last.then_inc(S["s_done"], 1)
                if live(2):
                    pe.wait_ge(S["o2T_ev"], c + 1)
                    for h in range(C2):
                        last = pe.matmul(B5[:, 0:D], o2T[:, h * P:h * P + P], xwout_s[:, h, :], start=h == 0, stop=h == 1)
                    last.then_inc(S["wout_done"], 1)
                if more(n):
                    next_xn1T(a + 1)
                if live(1):
                    pe.wait_ge(S["mlo_done"], b + 1)
                    if live(3):
                        pe.wait_ge(S["slotE_done"], d + 1)
                    pe.transpose(B6[:, 0:64].bitcast(BF16), mstack[:].rearrange("p r m -> p (r m)"), identb[:]) \
                        .then_inc(S["mTp_done"], 1)
                if live(0):
                    pe.wait_ge(S["ctxK_in"], 16 * (a + 1))
                    if live(1):
                        pe.wait_ge(S["vblk_ev"], 2 * b + 2)
                    for f in range(2):
                        for v in range(2):
                            o = (2 * f + v) * P
                            last = pe.matmul(B7[:, o:o + P], xwk_s[:, v, f * P:f * P + P], ctxK[:], start=True, stop=True)
                    last.then_inc(S["kp_done"], 1)
                if live(1):
                    pe.wait_ge(S["mT_ev"], b + 1)
                    for r_ in range(4):
                        g = slice(32 * r_, 32 * r_ + 32)
                        last = pe.matmul(SB[r_], mT[g, :], inj[g, :], start=False, stop=True, skip_group_check=True)
                        if r_ % 2:
                            last.then_inc(S["inj_done"], 1)

            next_xn1T(0)
            loop1(pe, step)

            pe.wait_ge(S["macc_done"], T)
            pe.wait_ge(S["x2_done"], T)
            pe.matmul(B5[:, 0:E], ones[:], macc[:], start=True, stop=True).then_inc(S["cnt_done"], 1)

            pe.wait_ge(S["sw_in"], 32)
            pe.wait_ge(S["xn3T_kept"], T)

            def shared_up(t):
                for v, name in ((0, "supg_done"), (1, "supu_done")):
                    if not first(t):
                        pe.wait_ge(S[("sg_done", "saT_done")[v]], t)
                    for j in range(SC):
                        for h in range(C2):
                            last = pe.matmul(SB[v][:, j * P:j * P + P], sup_s[:, h, v, j * P:j * P + P],
                                             xn3T_all[:, bass.ds(t, 1), h * P:h * P + P].rearrange("p a q -> p (a q)"),
                                             start=h == 0, stop=h == 1)
                    last.then_inc(S[name], 1)

            def shared_down(t):
                pe.wait_ge(S["saT_done"], t + 1)
                if not first(t):
                    pe.wait_ge(S["xs_done"], t)
                for j in range(SC):
                    last = pe.matmul(SB[2][:, 0:D], saT[:, j * P:j * P + P], sdown_s[:, j, :], start=j == 0, stop=j == SC - 1)
                last.then_inc(S["sdn_done"], 1)

            shared_up(0)
            pe.wait_ge(S["tcols_done"], 1)
            pe.matmul(B5[0:1, 0:P], tcols[:, 0:1], ident[:], start=True, stop=True)
            pe.matmul(B5[0:1, P:2 * P], tcols[:, 1:2], ident[:], start=True, stop=True).then_inc(S["tabTp_done"], 1)
            with pe.Fori(1, T) as t:
                shared_up(t)
                shared_down(t - 1)
            shared_down(T - 1)

            pe.wait_ge(S["rw_in"], 32)
            pe.wait_ge(S["tab_done"], 2)
            pe.wait_ge(S["xs_done"], T)

            def expert(t):
                return pe.value_load(tabT[0:1, 1, bass.ds(t, 1)], min_val=0, max_val=E - 1)

            def rows_in(t, k, g):
                pe.wait_ge(S[f"xg_in{k}"], (g + 1) * 16)
                transpose2(B4, xg[k]).then_inc(S["xTp_done"], 1)

            def up(t, e):
                pe.wait_ge(S["xgT_ev"], t + 1)
                for h in range(C2):
                    last = pe.matmul(SB[0][:, 0:2 * INTER], xgT[:, h * P:h * P + P],
                                     up_s[:, bass.ds(e, 1), h, :].rearrange("p a n -> p (a n)"), start=h == 0, stop=h == 1)
                last.then_inc(S["up_done"], 1)

            def down(t, e):
                pe.wait_ge(S["aT_ev"], t + 1)
                if not first(t):
                    pe.wait_ge(S["y_done"], t)
                for h in range(2):
                    last = pe.matmul(SB[1][:, 0:D], aT[:, h, :], down_s[:, bass.ds(e, 1), h, :].rearrange("p a n -> p (a n)"),
                                     start=h == 0, stop=h == 1)
                last.then_inc(S["dn_done"], 1)

            def gated_T(t):
                pe.wait_ge(S["a_done"], t + 1)
                for h in range(2):
                    last = pe.transpose(SB[2][0:HALF_I, h * P:h * P + P], act_[:, h * HALF_I:h * HALF_I + HALF_I], ident[:])
                last.then_inc(S["aTp_done"], 1)

            def four(g, is_first, is_last):
                t0 = g * RING
                e_before = None if is_first else expert(t0 - 1)
                for k in range(RING):
                    t = t0 + k
                    e = expert(t)
                    up(t, e)
                    if not (is_last and k == RING - 1):
                        rows_in(t + 1, (k + 1) % RING, g + (1 if k == RING - 1 else 0))
                    if e_before is not None:
                        down(t - 1, e_before)
                    gated_T(t)
                    e_before = e
                if is_last:
                    down(t0 + RING - 1, e_before)

            rows_in(0, 0, 0)
            four(0, True, False)
            with pe.Fori(1, RT // RING - 1) as g:
                four(g, False, False)
            four(RT // RING - 1, False, True)


def kernel(**inputs):
    import numpy as np
    import ml_dtypes
    import concourse.bacc as bacc
    from concourse import mybir as mb
    from concourse.bass_utils import run_bass_kernel_spmd

    f = np.float32
    a = {k: np.asarray(v) for k, v in inputs.items()}

    def swapped(w):
        return np.stack([w, w.reshape(w.shape[0], -1, 2)[:, :, ::-1].reshape(w.shape)])

    wkv = a["L0_xattn_Wkv"]
    wv_x = wkv[:, D:].reshape(CTX, 2, 4, 2, 2, HD).transpose(0, 2, 1, 3, 4, 5).reshape(CTX, D)
    wout_x = a["L0_xattn_Wout"].reshape(2, 4, 2, 2, HD, D).transpose(1, 0, 2, 3, 4, 5).reshape(D, D)
    sup = np.zeros((D, 2, SIP), f)
    sup[:, :, :SI] = a["L0_ffn_shared_up_w"].T.reshape(D, 2, SI)
    sdown = np.zeros((SIP, D), f)
    sdown[:SI] = a["L0_ffn_shared_down_w"].T
    part = np.arange(P)
    inject = np.zeros((P, 512), f)
    for r in range(P):
        if r % 32 < 16:
            inject[r] = np.arange(512) // SEQ == r % 8
    arrays = {
        "x": a["x"].reshape(TOK, D),
        "ctxT": a["ctx_1024"].reshape(TOK, CTX).T,
        "pos": a["fside_BxSx2_0"].reshape(TOK, 2).T[(part % HD) // 4],
        "wk": a["L0_attn_Wk"], "wv": a["L0_attn_Wv"], "bk": a["L0_attn_bk"], "bv": a["L0_attn_bv"],
        "wo": a["L0_attn_Wo"], "bo": a["L0_attn_bo"],
        "xwq": swapped(a["L0_xattn_Wq"]).reshape(2, C2, P, D).transpose(2, 1, 0, 3), "xwk": swapped(wkv[:, :D]), "xwv": wv_x, "xwout": wout_x,
        "xbout": a["L0_xattn_bout"], "gate": a["L0_ffn_gate_w"].T,
        "upw": a["L0_ffn_expert_up_w"].reshape(E, 2 * INTER, C2, P).transpose(3, 0, 2, 1),
        "downw": a["L0_ffn_expert_down_w"].reshape(E, D, 2, HALF_I).transpose(3, 0, 2, 1),
        "supw": sup.reshape(C2, P, 2, SIP).transpose(1, 0, 2, 3),
        "sdownw": sdown,
        "identity": np.eye(P, dtype=f),
        "identity_b": np.eye(P, dtype=ml_dtypes.bfloat16),
        "head_mask": ((part // HD % 4)[:, None] == np.arange(4)[None]).astype(f),
        "inject_rows": inject.astype(ml_dtypes.bfloat16),
        "before": (part[:, None] < part[None]).astype(ml_dtypes.bfloat16),
        "rope_freq": np.stack([np.where(part % 4 // 2 == 0, 1.0, 0.01), np.where(part % 2 == 0, -1.0, 1.0)], 1).astype(f),
        "region_base": np.broadcast_to(np.arange(E) * REGION, (P, E)).astype(f),
        "iota_e": np.broadcast_to(np.arange(E), (P, E)).astype(f),
        "token_ids": (part[:, None] + P * np.arange(T)[None]).astype(np.int32),
        "pad_rows": np.zeros((P, ROW), f),
        "tile_ids": part[:, None].astype(f),
        "ones_f": np.ones((P, P), f),
        "ones_b": np.ones((P, P), ml_dtypes.bfloat16),
    }
    arrays["pad_rows"].view(np.int32)[:, D] = TOK + part
    nc = bacc.Bacc("TRN2", target_bir_lowering=False, num_devices=1)
    sent, args = {}, {}
    for name, value in arrays.items():
        value = np.ascontiguousarray(value)
        sent[f"in_{name}"] = value
        args[name] = nc.dram_tensor(f"in_{name}", value.shape, mb.dt.from_np(value.dtype), kind="ExternalInput").ap()
    args["out"] = nc.dram_tensor("out_0", (TOK, D), mb.dt.float32, kind="ExternalOutput").ap()
    decoder_kernel(nc, **args)
    got = run_bass_kernel_spmd(nc, [sent], core_ids=[0])
    return got.results[0]["out_0"].reshape(inputs["x"].shape)
```

```python
from contextlib import ExitStack

import concourse.bass as bass
from concourse import mybir

ALU = mybir.AluOpType
ACT = mybir.ActivationFunctionType
AX = mybir.AxisListType
F32 = mybir.dt.float32
BF16 = mybir.dt.bfloat16
I32 = mybir.dt.int32
U32 = mybir.dt.uint32

P = 128
D = 256
C2 = D // P
SEQ = 64
TOK = 2048
T = TOK // P
HEADS, HD = 32, 8
CTX = 128
E, TOPK, GROUPS, TOPG = 16, 4, 4, 2
INTER = 176
HALF_I = INTER // 2
SI = 352
SC = (SI + P - 1) // P
SIP = SC * P
REGION = TOK + P
ROW = D + 1 + E
PAD_TILE = E * REGION
RING = 8
RT = -(-((TOK * TOPK + E * (P - 1)) // P) // RING) * RING
ACC = TOK + P
EPS = 1e-5
XSCALE = float(HD) ** -0.5
ASCALE = 1.0 / 128.0
TWO_PI_HI = 6.28125
TWO_PI_LO = 6.283185307179586 - 6.28125
ROUND = 1.5 * 2.0 ** 23
PI_IN = 3.1415925
AHEAD = 3


def decoder_kernel(nc, x, ctxT, pos, wk, wv, bk, bv, wo, bo, xwq, xwk, xwv, xwout, xbout, gate, upw, downw,
                   supw, sdownw, identity, identity_b, head_mask, inject_rows, before, rope_freq, region_base, iota_e,
                   token_ids, pad_rows, tile_ids, ones_f, ones_b, out):
    with ExitStack() as ctx:
        def sb(name, shape, dt=F32):
            return ctx.enter_context(nc.sbuf_tensor(name, shape, dt))

        def sem(name):
            return ctx.enter_context(nc.semaphore(name))

        routed = nc.dram_tensor("routed", [PAD_TILE + P, ROW], F32).ap()
        acc = [nc.dram_tensor(f"acc{k}", [ACC, D], F32).ap() for k in range(2)]

        scores = ctx.enter_context(nc.psum_tensor("scores", [P, 2048], F32))
        B4, B5, B6, B7 = (ctx.enter_context(nc.psum_tensor(f"bank{k}", [P, 512], F32)) for k in range(4, 8))
        SB = [scores[:, 512 * k:512 * k + 512] for k in range(4)]

        ident = sb("ident", [P, P])
        hmask = sb("hmask", [P, 8])
        inj = sb("inj", [P, 512], BF16)
        tri = sb("tri", [P, P], BF16)
        ones = sb("ones", [P, P], BF16)
        identb = sb("identb", [P, P], BF16)
        onesf = sb("onesf", [P, P])
        freq = sb("freq", [P, 2])
        base_e = sb("base_e", [P, E])
        iota = sb("iota", [P, E])
        tokid = sb("tokid", [P, T], I32)
        tileid = sb("tileid", [P, 1])
        pad = sb("pad", [P, ROW])
        zeros = sb("zeros", [P, D])
        wk_s = sb("wk_s", [P, C2, P])
        wv_s = sb("wv_s", [P, C2, P])
        bk_s = sb("bk_s", [P, 1])
        bv_s = sb("bv_s", [P, 1])
        wosum = sb("wosum", [P, D])
        bo_s = sb("bo_s", [P, D])
        xwq_s = sb("xwq_s", [P, C2, 2, D])
        xwk_s = sb("xwk_s", [P, 2, D])
        xwv_s = sb("xwv_s", [P, D])
        xwout_s = sb("xwout_s", [P, C2, D])
        xbout_s = sb("xbout_s", [P, D])
        gate_s = sb("gate_s", [P, C2, E])
        up_s = sb("up_s", [P, E, C2, 2 * INTER])
        down_s = sb("down_s", [HALF_I, E, 2, D])
        sup_s = sb("sup_s", [P, C2, 2, SIP])
        sdown_s = sb("sdown_s", [P, SC, D])
        xres = sb("xres", [P, T, D])
        xn3T_all = sb("xn3T_all", [P, T, D])
        cosT = sb("cosT", [P, TOK])
        sinT = sb("sinT", [P, TOK])
        prob = sb("prob", [P, 2048])
        probT = sb("probT", [P, 16, P])
        ctxK = sb("ctxK", [P, P])
        ctxV = sb("ctxV", [P, 2, 2, SEQ])
        st = sb("st", [P, 6])
        ln = [(sb(f"mv{k}", [P, 2]), sb(f"lnv{k}", [P, 1]), sb(f"rs{k}", [P, 1]), sb(f"nt{k}", [P, 2]),
               sb(f"rstd{k}", [P, 1])) for k in range(3)]
        xn1 = sb("xn1", [P, D])
        xn1T = sb("xn1T", [P, D])
        xbo = sb("xbo", [P, D])
        kT1 = sb("kT1", [P, P])
        vT1 = sb("vT1", [P, P])
        v1 = sb("v1", [P, P])
        mx1 = sb("mx1", [P, 1])
        nmx1 = sb("nmx1", [P, 1])
        p1 = sb("p1", [P, P])
        p1n = sb("p1n", [P, P])
        sum1 = sb("sum1", [P, 1])
        rsum1 = sb("rsum1", [P, 1])
        p1T = sb("p1T", [P, P])
        oT1 = sb("oT1", [P, P])
        xn2 = sb("xn2", [P, D])
        xn2T = sb("xn2T", [P, D])
        xbout1 = sb("xbout1", [P, D])
        qr = sb("qr", [P, 2, P])
        qs = sb("qs", [P, 2, P])
        qT = sb("qT", [P, 2, P])
        kr = sb("kr", [P, 2, P])
        ks = sb("ks", [P, 2, P])
        kT = sb("kT", [P, 2, P])
        kblk = sb("kblk", [P, 2, 2, 8, SEQ])
        vblk = sb("vblk", [P, 2, 16, 2, 9])
        mS = sb("mS", [P, 4, 8])
        mstack = sb("mstack", [P, 4, 32], BF16)
        mT = sb("mT", [P, P], BF16)
        rden = sb("rden", [P, HEADS])
        o2 = sb("o2", [P, D])
        o2T = sb("o2T", [P, D])
        xn3 = sb("xn3", [P, D])
        xrow = sb("xrow", [P, ROW])
        xn3T = sb("xn3T", [P, D])
        lmx = sb("lmx", [P, 1])
        lsh = sb("lsh", [P, E])
        lex = sb("lex", [P, E])
        lsum = sb("lsum", [P, 1])
        lrs = sb("lrs", [P, 1])
        prb = sb("prb", [P, E])
        gmax = sb("gmax", [P, 8])
        gtop = sb("gtop", [P, 8])
        gidx = sb("gidx", [P, 8], U32)
        gidf = sb("gidf", [P, TOPG])
        ghot = sb("ghot", [P, TOPG, GROUPS])
        gm = sb("gm", [P, GROUPS])
        msc = sb("msc", [P, E])
        etop = sb("etop", [P, 8])
        eidx = sb("eidx", [P, 8], U32)
        eidf = sb("eidf", [P, TOPK])
        ehot = sb("ehot", [P, TOPK, E])
        self32 = sb("self32", [P, E])
        sel = sb("sel", [P, E], BF16)
        msel = sb("msel", [P, E])
        wsum = sb("wsum", [P, 1])
        wsum1 = sb("wsum1", [P, 1])
        wrec = sb("wrec", [P, 1])
        macc = sb("macc", [P, E], BF16)
        slotE = sb("slotE", [P, E])
        slot4 = sb("slot4", [P, TOPK, E])
        slotf = sb("slotf", [P, TOPK])
        sloti = sb("sloti", [P, TOPK], I32)
        cnt = sb("cnt", [P, E])
        tail_f = sb("tail_f", [1, E])
        tail_i = sb("tail_i", [1, E], I32)
        cpad = sb("cpad", [P, E])
        cfl = sb("cfl", [P, E])
        cgt = sb("cgt", [P, E])
        nt = sb("nt", [P, E])
        tend = sb("tend", [P, E])
        past = sb("past", [P, E])
        rowt = sb("rowt", [P, E])
        tcols = sb("tcols", [P, 4])
        tabT = sb("tabT", [1, 2, P], I32)
        sg = prob[:, 0:SIP]
        saT = prob[:, SIP:2 * SIP]
        y = [cosT[:, D * k:D * k + D] for k in range(RING)]
        xg = [(sinT[:], probT[:].rearrange("p c q -> p (c q)"))[k % 2][:, ROW * (k // 2):ROW * (k // 2) + ROW] for k in range(RING)]
        xgT = xn1T
        sil = xn1[:, 0:INTER]
        act_ = xn2[:, 0:INTER]
        aT = xn2T[0:HALF_I, :].rearrange("p (c q) -> p c q", c=2)

        spare = {(eng.engine, k): eng.alloc_register(f"spare{k}") for eng in (nc.vector, nc.gpsimd, nc.tensor) for k in range(3)}

        block = ctx.enter_context(nc.Block())

        S = {name: sem(name) for name in (
            "aT_ev aTp_done a_done abs_done acc_zeroed agg0 agg1 agg2 angle angle_step av_done "
            "bn0 bn1 bn2 c1_in cnt_done cos_done ctxK_in ctxV_in cw_done dn_done eidf_done eidx_done lmx_done wrec_done fin_add fin_in0 fin_in1 "
            "fin_step gate_done ident_in inj_done kT1_ev kT_done kblk_done kp_done kr_done ks_done lex_done "
            "lnv0 lnv1 lnv2 lsh_done mT_ev mTp_done macc_done max_done mhi_done mlo_done mx1_done nmx1_done "
            "nt0 nt1 nt2 o2T_ev o2Tp_done o2_done oT1_done oT1_ev out_done p1T_ev p1Tp_done p1a p1b p1n_done "
            "pad_out pads_done pos_in pr1_done pre_done prob_done qT_done q_done qkv1_done qr_done qs_done "
            "r_step rden_done rs00 rs01 rs02 rstd0 rstd1 rstd2 rsum1_done row_done rw_in s1_done s_done saT_done "
            "scattered sdn_done sel_done selx_done sg_done sil_done sin_done slot4_done slotE_done "
            "slotf_done slots_done supg_done supu_done sw_in t_step tabTp_done tab_done tcols_done tok_done "
            "tpA_ev tpD_ev tp_done up_done v1_ev vT1_ev v_done vblk_ev vblk_set w1_in wo_in wosum_done "
            "wosum_step wout_done ws_step x0_in x1_done x2_done xTp_done x_in xbo_done xbout_done xgT_ev "
            "xn1T_ev xn1Tp_done xn1_done xn2T_ev xn2Tp_done xn2_done xn3T_ev xn3T_kept xn3Tp_done xn3_done "
            "xs_done xw_in y_done zero_set ").split()}
        S.update({f"xg_in{k}": sem(f"xg_in{k}") for k in range(RING)})
        S.update({f"added{k}": sem(f"added{k}") for k in range(2)})

        def tile_of(buf, t):
            return buf[:, bass.ds(t, 1), :].rearrange("p a d -> p (a d)")

        def hold(eng, count, k=0):
            if isinstance(count, int):
                return count
            eng.reg_add(spare[eng.engine, k], count, 0)
            return spare[eng.engine, k]

        def past_wait(eng):
            eng.wait_ge(S["zero_set"], 5)

        def fin_part(h, q):
            return ((cosT[:], sinT[:]), (prob[:], probT[:].rearrange("p c q -> p (c q)")))[h][q] \
                .rearrange("p (t d) -> p t d", d=D)

        def first(t):
            return isinstance(t, int) and t == 0

        def more(n):
            return not isinstance(n, int) or n + 1 < T

        def loop1(eng, body):
            for n in range(AHEAD + 1):
                body(n, lambda k, n=n: k <= n)
            with eng.Fori(AHEAD + 1, T - 1) as n:
                body(n, lambda k: True)
            for n in range(T - 1, T + AHEAD):
                body(n, lambda k, n=n: n - k < T)

        posb = xn3T_all[:, 0:8, :].rearrange("p t d -> p (t d)")
        angle = xn3T_all[:, 8:16, :].rearrange("p t d -> p (t d)")
        LN = [{what: f"{what}{k}" for what in ("bn", "agg", "lnv", "rs0", "nt", "rstd")} for k in range(3)]

        @block.sync
        def _(sp):
            sp.dma_start(ident[:], identity).then_inc(S["ident_in"], 16)
            sp.dma_start(tile_of(xres, 0), x[0:P, :]).then_inc(S["x0_in"], 16)
            sp.dma_start(wk_s[:], wk.rearrange("(c p) n -> p c n", p=P)).then_inc(S["w1_in"], 16)
            sp.dma_start(wv_s[:], wv.rearrange("(c p) n -> p c n", p=P)).then_inc(S["w1_in"], 16)
            sp.dma_start(bk_s[:], bk.rearrange("(p a) -> p a", a=1)).then_inc(S["w1_in"], 16)
            sp.dma_start(bv_s[:], bv.rearrange("(p a) -> p a", a=1)).then_inc(S["w1_in"], 16)
            sp.dma_start(bo_s[:], bo.partition_broadcast(P)).then_inc(S["w1_in"], 16)
            for dst, src in ((hmask, head_mask), (inj, inject_rows), (tri, before), (ones, ones_b), (identb, identity_b), (onesf, ones_f),
                             (base_e, region_base), (iota, iota_e), (tokid, token_ids), (tileid, tile_ids), (pad, pad_rows)):
                sp.dma_start(dst[:], src).then_inc(S["c1_in"], 16)
            sp.dma_start(xres[:, 1:T, :], x[P:TOK, :].rearrange("(t p) d -> p t d", p=P)).then_inc(S["x_in"], 16)
            sp.dma_start(xwq_s[:], xwq).then_inc(S["xw_in"], 16)
            sp.dma_start(xwout_s[:], xwout.rearrange("(c p) n -> p c n", p=P)).then_inc(S["xw_in"], 16)
            sp.dma_start(gate_s[:], gate.rearrange("(c p) n -> p c n", p=P)).then_inc(S["xw_in"], 16)

            def step(n, live):
                if live(0):
                    if not first(n):
                        sp.wait_ge(S["kp_done"], n)
                    sp.dma_start(ctxK[:], ctxT[:, bass.ds(n * P, P)]).then_inc(S["ctxK_in"], 16)
                if live(1):
                    if not first(n - 1):
                        sp.wait_ge(S["v_done"], n - 1)
                    for hp in range(2):
                        sp.dma_start(ctxV[:, :, hp, :], ctxT[:, bass.ds((n - 1) * P, P)].rearrange("c (s k) -> c s k", s=2)) \
                            .then_inc(S["ctxV_in"], 16)

            loop1(sp, step)

            sp.wait_ge(S["tab_done"], 2)
            sp.wait_ge(S["scattered"], 16 * TOPK * T)
            for e in range(E):
                end = sp.value_load(tail_i[0:1, e:e + 1], min_val=e * REGION, max_val=e * REGION + TOK)
                sp.dma_start(routed[bass.ds(end, P), :], pad[:]).then_inc(S["pads_done"], 16)
            sp.wait_ge(S["pads_done"], 16 * E)
            sp.wait_ge(S["pad_out"], 16)

            for k in range(RING):
                row = sp.value_load(tabT[0:1, 0, k:k + 1], min_val=0, max_val=PAD_TILE)
                sp.dma_start(xg[k], routed[bass.ds(row, P), :]).then_inc(S[f"xg_in{k}"], 16)
            with sp.Fori(1, RT // RING) as g:
                for k in range(RING):
                    sp.wait_ge(S[f"added{k % 2}"], g * 16 * (RING // 2) - 16 * (RING // 2 - 1 - k // 2))
                    row = sp.value_load(tabT[0:1, 0, bass.ds(g * RING + k, 1)], min_val=0, max_val=PAD_TILE)
                    sp.dma_start(xg[k], routed[bass.ds(row, P), :]).then_inc(S[f"xg_in{k}"], 16)

            sp.wait_ge(S["added0"], 16 * (RT // 2))
            sp.wait_ge(S["added1"], 16 * (RT // 2))
            for h in range(2):
                for q in range(2):
                    sp.dma_start(fin_part(h, q), acc[q][1024 * h:1024 * h + 1024, :].rearrange("(t p) d -> p t d", p=P)) \
                        .then_inc(S[f"fin_in{h}"], 16)
            for h in range(2):
                sp.wait_ge(S["fin_add"], h + 1)
                sp.dma_start(out[1024 * h:1024 * h + 1024, :].rearrange("(t p) d -> p t d", p=P),
                             xres[:, 8 * h:8 * h + 8, :]).then_inc(S["out_done"], 16)
            sp.wait_ge(S["out_done"], 32)

        @block.gpsimd
        def _(pool):
            pool.memset(zeros[:], 0.0).then_inc(S["zero_set"], 1)
            pool.memset(p1[:], 0.0).then_inc(S["zero_set"], 1)
            pool.memset(mstack[:], 0.0).then_inc(S["zero_set"], 1)
            pool.memset(macc[:], 0.0).then_inc(S["zero_set"], 1)
            pool.memset(gmax[:], -1.0).then_inc(S["zero_set"], 1)
            pool.memset(vblk[:], 0.0).then_inc(S["vblk_set"], 1)
            pool.wait_ge(S["vblk_set"], 1)
            for hp in range(2):
                pool.memset(vblk[64 * hp:64 * hp + 64, :, :, hp, 8:9], 1.0).then_inc(S["vblk_set"], 1)
            pool.wait_ge(S["vblk_set"], 3)
            pool.wait_ge(S["wo_in"], 32)
            wob = prob[:]
            wob2 = probT[:].rearrange("p c q -> p (c q)")
            pool.tensor_tensor(wob, wob, wob2, op=ALU.add).then_inc(S["wosum_step"], 1)
            for k, w in enumerate((1024, 512)):
                pool.wait_ge(S["wosum_step"], k + 1)
                pool.tensor_tensor(wob[:, 0:w], wob[:, 0:w], wob[:, w:2 * w], op=ALU.add).then_inc(S["wosum_step"], 1)
            pool.wait_ge(S["wosum_step"], 3)
            pool.tensor_tensor(wosum[:], wob[:, 0:D], wob[:, D:2 * D], op=ALU.add).then_inc(S["wosum_done"], 1)
            pool.wait_ge(S["w1_in"], 80)
            pool.wait_ge(S["x0_in"], 16)
            pool.wait_ge(S["x_in"], 16)
            pool.wait_ge(S["xw_in"], 16 * 6)

            def next_xbo(t):
                if not first(t):
                    pool.wait_ge(S["x1_done"], t)
                pool.tensor_tensor(xbo[:], tile_of(xres, t), bo_s[:], op=ALU.add).then_inc(S["xbo_done"], 1)

            next_xbo(0)

            def step(n, live):
                a, b, c, d = n, n - 1, n - 2, n - 3
                if live(3):
                    pool.wait_ge(S["xn3T_ev"], d + 1)
                    pool.tensor_copy(tile_of(xn3T_all, d), xn3T[:]).then_inc(S["xn3T_kept"], 1)
                    held, away = hold(pool, d + 1), hold(pool, d * 16 * TOPK, 1)
                    past_wait(pool)
                    pool.wait_ge(S["xn3_done"], held)
                    if not first(d):
                        pool.wait_ge(S["scattered"], away)
                    pool.tensor_copy(xrow[:, 0:D], xn3[:]).then_inc(S["row_done"], 1)
                    pool.tensor_copy(xrow[:, D:D + 1].bitcast(I32), tokid[:, bass.ds(d, 1)]).then_inc(S["tok_done"], 1)
                    past_wait(pool)
                    pool.wait_ge(S["row_done"], held)
                    pool.wait_ge(S["tok_done"], held)
                    pool.wait_ge(S["cw_done"], held)
                    pool.wait_ge(S["slots_done"], held)
                    for k in range(TOPK):
                        pool.indirect_dma_start(routed, bass.IndirectOffsetOnAxis(ap=sloti[:, k:k + 1], axis=0),
                                                xrow[:], None).then_inc(S["scattered"], 16)
                if live(0):
                    pool.wait_ge(S["ks_done"], n + 1)
                    pool.tensor_tensor(kT[:], kr[:], ks[:], op=ALU.add).then_inc(S["kT_done"], 1)
                    pool.wait_ge(S["kT_done"], n + 1)
                    if not first(n):
                        pool.wait_ge(S["s_done"], 2 * n)
                    pool.tensor_tensor(kblk[:].rearrange("p f b h k -> p (f b) h k"),
                                       kT[:].rearrange("p f (b k) -> p (f b) k", k=SEQ)[:, :, None, :].to_broadcast([P, 4, 8, SEQ]),
                                       hmask[:, None, :, None].to_broadcast([P, 4, 8, SEQ]), op=ALU.mult).then_inc(S["kblk_done"], 1)
                if more(n):
                    next_xbo(n + 1)
                if live(1):
                    pool.wait_ge(S["x1_done"], b + 1)
                    if not first(b):
                        pool.wait_ge(S["x2_done"], b)
                    pool.tensor_tensor(xbout1[:], tile_of(xres, b), xbout_s[:], op=ALU.add).then_inc(S["xbout_done"], 1)

            loop1(pool, step)

            pool.wait_ge(S["acc_zeroed"], 32)
            def add(t, k, seen):
                made = hold(pool, t + 1)
                before_it = None if seen is None else hold(pool, seen, 1)
                past_wait(pool)
                pool.wait_ge(S["y_done"], made)
                if before_it is not None:
                    pool.wait_ge(S[f"added{k % 2}"], before_it)
                pool.indirect_dma_start(acc[k % 2], bass.IndirectOffsetOnAxis(ap=xg[k][:, D:D + 1].bitcast(I32), axis=0),
                                        y[k], None, compute_op=ALU.add).then_inc(S[f"added{k % 2}"], 16)

            for k in range(RING):
                add(k, k, None if k < 2 else 16 * (k // 2))
            with pool.Fori(1, RT // RING) as g:
                for k in range(RING):
                    add(g * RING + k, k, g * 16 * (RING // 2) + 16 * (k // 2))

        @block.scalar
        def _(act):
            act.dma_start(freq[:], rope_freq).then_inc(S["pos_in"], 16)
            act.dma_start(posb, pos).then_inc(S["pos_in"], 16)
            act.dma_start(prob[:].rearrange("p (h n) -> p h n", n=D),
                          wo.rearrange("(h d) n -> d h n", d=P)[:, 0:8, :]).then_inc(S["wo_in"], 16)
            act.dma_start(probT[:].rearrange("p c q -> p (c q)").rearrange("p (h n) -> p h n", n=D),
                          wo.rearrange("(h d) n -> d h n", d=P)[:, 8:16, :]).then_inc(S["wo_in"], 16)
            act.dma_start(xwk_s[:], xwk.rearrange("v p n -> p v n")).then_inc(S["xw_in"], 16)
            act.dma_start(xwv_s[:], xwv).then_inc(S["xw_in"], 16)
            act.dma_start(xbout_s[:], xbout.partition_broadcast(P)).then_inc(S["xw_in"], 16)
            act.preload_act_table_set("natural_log_exp_and_others")

            def rsqrt(k, t):
                mv, lnv, rs, _, _ = ln[k]
                act.wait_ge(S[LN[k]["agg"]], t + 1)
                act.activation(lnv[:], mv[:, 1:2], ACT.Ln, bias=EPS).then_inc(S[LN[k]["lnv"]], 1)
                act.wait_ge(S[LN[k]["lnv"]], t + 1)
                act.activation(rs[:], lnv[:], ACT.Exp, scale=-0.5).then_inc(S[LN[k]["rs0"]], 1)

            def next_xn1T(t):
                act.wait_ge(S["xn1Tp_done"], t + 1)
                act.activation(xn1T[:], B4[:, 0:D], ACT.Copy).then_inc(S["xn1T_ev"], 1)

            def next_qkv(t):
                act.wait_ge(S["qkv1_done"], t + 1)
                act.activation(kT1[:], B4[:, 0:P], ACT.Identity, bias=bk_s[:]).then_inc(S["kT1_ev"], 1)
                act.activation(vT1[:], B4[:, P:2 * P], ACT.Identity, bias=bv_s[:]).then_inc(S["vT1_ev"], 1)
                act.activation(v1[:], B4[:, 2 * P:3 * P], ACT.Copy).then_inc(S["v1_ev"], 1)

            rsqrt(0, 0)
            next_xn1T(0)
            next_qkv(0)
            act.wait_ge(S["angle"], 1)
            act.activation(sinT[:], angle, ACT.Sin, scale=freq[:, 1:2]).then_inc(S["sin_done"], 1)
            act.activation(posb, angle, ACT.Abs).then_inc(S["abs_done"], 1)
            act.wait_ge(S["abs_done"], 1)
            act.activation(cosT[:], posb, ACT.Sin, scale=-1.0, bias=1.5707963267948966).then_inc(S["cos_done"], 1)
            act.wait_ge(S["zero_set"], 5)
            for a in acc:
                act.dma_start(a.rearrange("(t p) d -> p t d", p=P),
                              zeros[:, None, :].to_broadcast([P, ACC // P, D])).then_inc(S["acc_zeroed"], 16)
            act.wait_ge(S["c1_in"], 16 * 11)
            act.dma_start(routed[PAD_TILE:PAD_TILE + P, :], pad[:]).then_inc(S["pad_out"], 16)
            act.dma_start(sup_s[:], supw).then_inc(S["sw_in"], 16)
            act.dma_start(sdown_s[:], sdownw.rearrange("(c p) n -> p c n", p=P)).then_inc(S["sw_in"], 16)
            act.dma_start(up_s[:], upw).then_inc(S["rw_in"], 16)
            act.dma_start(down_s[:], downw).then_inc(S["rw_in"], 16)
            act.preload_act_table_set("natural_log_exp_and_others")

            def probabilities(t, h):
                act.wait_ge(S["inj_done"], 2 * t + 1 + h)
                if h == 0 and not first(t):
                    act.wait_ge(S["tp_done"], 4 * t)
                act.activation(prob[:, 1024 * h:1024 * h + 1024], scores[:, 1024 * h:1024 * h + 1024],
                               ACT.Exp, scale=XSCALE).then_inc(S["prob_done"], 1)

            def quarter(t, q, bank):
                act.wait_ge(S["tp_done"], 4 * t + q + 1)
                act.activation(probT[:, 4 * q:4 * q + 4, :].rearrange("p c q -> p (c q)"), bank[:], ACT.Copy) \
                    .then_inc(S["tpA_ev"], 1)

            def step(n, live):
                a, b, c, d = n, n - 1, n - 2, n - 3
                if live(3):
                    act.wait_ge(S["xn3Tp_done"], d + 1)
                    if not first(d):
                        act.wait_ge(S["xn3T_kept"], d)
                    act.activation(xn3T[:], B6[:, 0:D], ACT.Copy).then_inc(S["xn3T_ev"], 1)
                if live(2):
                    probabilities(c, 1)
                    quarter(c, 0, B4)
                if live(0):
                    for h, name in ((0, "p1a"), (1, "p1b")):
                        r = slice(SEQ * h, SEQ * h + SEQ)
                        if h == 0:
                            act.wait_ge(S["nmx1_done"], a + 1)
                            if not first(a):
                                act.wait_ge(S["p1n_done"], a)
                        act.activation(p1[r, r], B5[r, r], ACT.Exp, bias=nmx1[r, :], scale=ASCALE,
                                       accum_out=sum1[r, :]).then_inc(S[name], 1)
                if live(2):
                    quarter(c, 1, B7)
                if live(3):
                    act.wait_ge(S["lsh_done"], d + 1)
                    act.activation(lex[:], lsh[:], ACT.Exp, accum_out=lsum[:]).then_inc(S["lex_done"], 1)
                if live(2):
                    quarter(c, 2, B4)
                if live(1):
                    act.wait_ge(S["xn2Tp_done"], b + 1)
                    act.activation(xn2T[:], B6[:, 0:D], ACT.Copy).then_inc(S["xn2T_ev"], 1)
                if more(n):
                    rsqrt(0, n + 1)
                if live(0):
                    act.wait_ge(S["p1Tp_done"], a + 1)
                    act.activation(p1T[:], B5[:, 0:P], ACT.Copy).then_inc(S["p1T_ev"], 1)
                    act.wait_ge(S["oT1_done"], a + 1)
                    act.activation(oT1[:], B5[:, 0:P], ACT.Identity, bias=bv_s[:]).then_inc(S["oT1_ev"], 1)
                if live(2):
                    act.wait_ge(S["o2Tp_done"], c + 1)
                    act.activation(o2T[:], B5[:, 0:D], ACT.Copy).then_inc(S["o2T_ev"], 1)
                if live(1):
                    act.wait_ge(S["v_done"], b + 1)
                    if first(b):
                        act.wait_ge(S["vblk_set"], 3)
                    for hp in range(2):
                        r = slice(64 * hp, 64 * hp + 64)
                        act.activation(vblk[r, :, :, hp, 0:8],
                                       B7[r, :].rearrange("p (b c h d) -> p b c h d", b=2, h=2, d=HD)[:, :, :, hp, :],
                                       ACT.Copy).then_inc(S["vblk_ev"], 1)
                if live(0):
                    rsqrt(1, a)
                if live(2):
                    rsqrt(2, c)
                if more(n):
                    next_xn1T(n + 1)
                if live(1):
                    act.wait_ge(S["mTp_done"], b + 1)
                    act.activation(mT[:], B6[:, 0:64].bitcast(BF16), ACT.Copy).then_inc(S["mT_ev"], 1)
                if more(n):
                    next_qkv(n + 1)
                if live(1):
                    probabilities(b, 0)

            loop1(act, step)

            act.preload_act_table_set("silu_and_others")

            def shared(t):
                act.wait_ge(S["supg_done"], t + 1)
                if not first(t):
                    act.wait_ge(S["saT_done"], t)
                act.activation(sg, SB[0][:, 0:SIP], ACT.Silu).then_inc(S["sg_done"], 1)

            shared(0)
            with act.Fori(1, T) as t:
                shared(t)

            def transposed(k, n):
                act.wait_ge(S["xTp_done"], n)
                act.activation(xgT[:], B4[:, 0:D], ACT.Copy).then_inc(S["xgT_ev"], 1)

            def routed_tile(t, k, more):
                act.wait_ge(S["up_done"], t + 1)
                act.activation(sil, SB[0][:, 0:INTER], ACT.Silu).then_inc(S["sil_done"], 1)
                if more:
                    transposed(k, t + 2)
                act.wait_ge(S["aTp_done"], t + 1)
                act.activation(aT.rearrange("p c q -> p (c q)"), SB[2][0:HALF_I, 0:2 * P], ACT.Copy).then_inc(S["aT_ev"], 1)

            transposed(0, 1)
            for k in range(RING):
                routed_tile(k, k, True)
            with act.Fori(1, RT // RING - 1) as g:
                for k in range(RING):
                    routed_tile(g * RING + k, k, True)
            for k in range(RING):
                routed_tile(RT - RING + k, k, k < RING - 1)

        @block.vector
        def _(dve):
            def ln_stats(k, t):
                mv = ln[k][0]
                dve.bn_stats(st[:], tile_of(xres, t)).then_inc(S[LN[k]["bn"]], 1)
                held = hold(dve, t + 1)
                past_wait(dve)
                dve.wait_ge(S[LN[k]["bn"]], held)
                dve.bn_aggr(mv[:], st[:]).then_inc(S[LN[k]["agg"]], 1)

            def ln_finish(k, t, dst):
                mv, _, rs, ntm, rstd = ln[k]
                dve.wait_ge(S[LN[k]["rs0"]], t + 1)
                dve.tensor_scalar(ntm[:, 0:1], mv[:, 1:2], EPS, rs[:], ALU.add, ALU.mult).then_inc(S[LN[k]["nt"]], 1)
                dve.wait_ge(S[LN[k]["nt"]], 2 * t + 1)
                dve.tensor_scalar(ntm[:, 1:2], ntm[:, 0:1], rs[:], -0.5, ALU.mult, ALU.mult).then_inc(S[LN[k]["nt"]], 1)
                dve.wait_ge(S[LN[k]["nt"]], 2 * t + 2)
                dve.tensor_scalar(rstd[:], ntm[:, 1:2], 1.5, rs[:], ALU.add, ALU.mult).then_inc(S[LN[k]["rstd"]], 1)
                dve.wait_ge(S[LN[k]["rstd"]], t + 1)
                return dve.tensor_scalar(dst, tile_of(xres, t), mv[:, 0:1], rstd[:], ALU.subtract, ALU.mult)

            dve.wait_ge(S["zero_set"], 5)
            dve.wait_ge(S["x0_in"], 16)
            ln_stats(0, 0)
            ln_finish(0, 0, xn1[:]).then_inc(S["xn1_done"], 1)

            dve.wait_ge(S["pos_in"], 32)
            st_n = [0]

            def turn(ins):
                ins.then_inc(S["angle_step"], 1)
                st_n[0] += 1
                dve.wait_ge(S["angle_step"], st_n[0])

            turn(dve.tensor_scalar(angle, posb, freq[:, 0:1], None, ALU.mult))
            turn(dve.tensor_scalar(cosT[:], angle, 1.0 / 6.283185307179586, ROUND, ALU.mult, ALU.add))
            turn(dve.tensor_scalar(cosT[:], cosT[:], ROUND, None, ALU.subtract))
            turn(dve.scalar_tensor_tensor(sinT[:], cosT[:], -TWO_PI_HI, angle, ALU.mult, ALU.add))
            turn(dve.scalar_tensor_tensor(angle, cosT[:], -TWO_PI_LO, sinT[:], ALU.mult, ALU.add))
            dve.tensor_scalar(angle, angle, PI_IN, -PI_IN, ALU.min, ALU.max).then_inc(S["angle"], 1)
            dve.wait_ge(S["x_in"], 16)
            dve.wait_ge(S["c1_in"], 176)

            def logits(d):
                dve.wait_ge(S["gate_done"], d + 1)
                dve.reduce_max(lmx[:], B6[:, 0:E], AX.X).then_inc(S["lmx_done"], 1)
                dve.wait_ge(S["lmx_done"], d + 1)
                dve.tensor_scalar(lsh[:], B6[:, 0:E], lmx[:], None, ALU.subtract).then_inc(S["lsh_done"], 1)

            R = 14

            def then(d, k, ins, next_is_max=False):
                ins.then_inc(S["r_step"], 1)
                if next_is_max:
                    held = hold(dve, d * R + k)
                    past_wait(dve)
                    dve.wait_ge(S["r_step"], held)
                else:
                    dve.wait_ge(S["r_step"], d * R + k)

            def best_groups(d):
                dve.wait_ge(S["lex_done"], d + 1)
                then(d, 1, dve.reciprocal(lrs[:], lsum[:]))
                then(d, 2, dve.tensor_scalar(prb[:], lex[:], lrs[:], None, ALU.mult))
                then(d, 3, dve.reduce_max(gmax[:, 0:GROUPS], prb[:].rearrange("p (g e) -> p g e", g=GROUPS), AX.X), True)
                then(d, 4, dve.max(gtop[:], gmax[:]), True)
                then(d, 5, dve.max_index(gidx[:], gtop[:], gmax[:]))
                then(d, 6, dve.tensor_copy(gidf[:], gidx[:, 0:TOPG]))
                then(d, 7, dve.tensor_tensor(ghot[:], gidf[:, :, None].to_broadcast([P, TOPG, GROUPS]),
                                             iota[:, None, 0:GROUPS].to_broadcast([P, TOPG, GROUPS]), op=ALU.is_equal))
                then(d, 8, dve.tensor_tensor(gm[:], ghot[:, 0, :], ghot[:, 1, :], op=ALU.add))
                dve.tensor_tensor(msc[:].rearrange("p (g e) -> p g e", g=GROUPS), prb[:].rearrange("p (g e) -> p g e", g=GROUPS),
                                  gm[:, :, None].to_broadcast([P, GROUPS, E // GROUPS]), op=ALU.mult).then_inc(S["r_step"], 1)

            def best_experts(d):
                held = hold(dve, d * R + 9)
                past_wait(dve)
                dve.wait_ge(S["r_step"], held)
                then(d, 10, dve.max(etop[:], msc[:]), True)
                dve.max_index(eidx[:], etop[:], msc[:]).then_inc(S["eidx_done"], 1)
                dve.reduce_sum(wsum[:], etop[:, 0:TOPK], AX.X).then_inc(S["ws_step"], 1)
                dve.wait_ge(S["eidx_done"], d + 1)
                dve.tensor_copy(eidf[:], eidx[:, 0:TOPK]).then_inc(S["eidf_done"], 1)
                dve.wait_ge(S["ws_step"], d + 1)
                then(d, 11, dve.tensor_scalar(wsum1[:], wsum[:], 1e-20, None, ALU.add))
                dve.reciprocal(wrec[:], wsum1[:]).then_inc(S["wrec_done"], 1)
                dve.wait_ge(S["eidf_done"], d + 1)
                then(d, 12, dve.tensor_tensor(ehot[:], eidf[:, :, None].to_broadcast([P, TOPK, E]),
                                              iota[:, None, :].to_broadcast([P, TOPK, E]), op=ALU.is_equal))
                then(d, 13, dve.tensor_reduce(self32[:], ehot[:].rearrange("p k e -> p e k"), AX.X, ALU.add))
                dve.tensor_copy(sel[:], self32[:]).then_inc(S["sel_done"], 1)
                dve.wait_ge(S["wrec_done"], d + 1)
                then(d, 14, dve.tensor_tensor(msel[:], msc[:], self32[:], op=ALU.mult))
                if not first(d):
                    dve.wait_ge(S["scattered"], d * 16 * TOPK)
                dve.tensor_scalar(xrow[:, D + 1:ROW], msel[:], wrec[:], None, ALU.mult).then_inc(S["cw_done"], 1)

            def step(n, live):
                a, b, c, d = n, n - 1, n - 2, n - 3
                if live(0):
                    dve.wait_ge(S["s1_done"], a + 1)
                    for h in range(2):
                        r = slice(SEQ * h, SEQ * h + SEQ)
                        dve.reduce_max(mx1[r, :], B5[r, r], AX.X).then_inc(S["mx1_done"], 1)
                    dve.wait_ge(S["mx1_done"], 2 * a + 2)
                    dve.tensor_scalar(nmx1[:], mx1[:], -ASCALE, None, ALU.mult).then_inc(S["nmx1_done"], 1)
                if live(3):
                    logits(d)
                if more(n):
                    ln_stats(0, n + 1)
                if live(0):
                    dve.wait_ge(S["p1a"], a + 1)
                    dve.wait_ge(S["p1b"], a + 1)
                    dve.reciprocal(rsum1[:], sum1[:]).then_inc(S["rsum1_done"], 1)
                    dve.wait_ge(S["rsum1_done"], a + 1)
                    dve.tensor_scalar(p1n[:], p1[:], rsum1[:], None, ALU.mult).then_inc(S["p1n_done"], 1)
                if live(2):
                    dve.wait_ge(S["tp_done"], 4 * c + 4)
                    dve.tensor_copy(probT[:, 12:16, :].rearrange("p c q -> p (c q)"), B7[:]).then_inc(S["tpD_ev"], 1)
                if live(3):
                    best_groups(d)
                if live(1):
                    dve.wait_ge(S["q_done"], b + 1)
                    rope(B6, qr, qs, b, "qr_done", "qs_done")
                    dve.wait_ge(S["qs_done"], b + 1)
                    dve.tensor_tensor(qT[:], qr[:], qs[:], op=ALU.add).then_inc(S["qT_done"], 1)
                if live(2):
                    dve.wait_ge(S["av_done"], c + 1)
                    av = B4[:, 0:HEADS * 9].rearrange("p (h d) -> p h d", d=9)
                    dve.reciprocal(rden[:, :, None], av[:, :, 8:9]).then_inc(S["rden_done"], 1)
                    dve.wait_ge(S["rden_done"], c + 1)
                    dve.tensor_tensor(o2[:].rearrange("p (h d) -> p h d", d=HD), av[:, :, 0:HD],
                                      rden[:, :, None].to_broadcast([P, HEADS, HD]), op=ALU.mult).then_inc(S["o2_done"], 1)
                if more(n):
                    ln_finish(0, n + 1, xn1[:]).then_inc(S["xn1_done"], 1)
                if live(0):
                    dve.wait_ge(S["pr1_done"], a + 1)
                    dve.wait_ge(S["xbo_done"], a + 1)
                    dve.tensor_tensor(tile_of(xres, a), B4[:, 0:D], xbo[:], op=ALU.add).then_inc(S["x1_done"], 1)
                    held = hold(dve, a + 1)
                    past_wait(dve)
                    dve.wait_ge(S["x1_done"], held)
                    ln_stats(1, a)
                if live(2):
                    dve.wait_ge(S["wout_done"], c + 1)
                    dve.wait_ge(S["xbout_done"], c + 1)
                    dve.tensor_tensor(tile_of(xres, c), B6[:, 0:D], xbout1[:], op=ALU.add).then_inc(S["x2_done"], 1)
                    held = hold(dve, c + 1)
                    past_wait(dve)
                    dve.wait_ge(S["x2_done"], held)
                    ln_stats(2, c)
                if live(3):
                    best_experts(d)
                if live(1):
                    maxima(b, 0)
                    maxima(b, 1)
                    dve.wait_ge(S["max_done"], 2 * b + 2)
                    dve.tensor_scalar(mstack[:, :, 0:8], mS[:], -1.0, None, ALU.mult).then_inc(S["mhi_done"], 1)
                    dve.wait_ge(S["mhi_done"], b + 1)
                    dve.scalar_tensor_tensor(mstack[:, :, 8:16], mS[:], -1.0, mstack[:, :, 0:8], ALU.mult, ALU.subtract) \
                        .then_inc(S["mlo_done"], 1)
                if live(2):
                    if not first(c):
                        dve.wait_ge(S["row_done"], c)
                    ln_finish(2, c, xn3[:]).then_inc(S["xn3_done"], 1)
                if live(3):
                    dve.wait_ge(S["pre_done"], d + 1)
                    dve.tensor_tensor(slotE[:], B5[:, 0:E], base_e[:], op=ALU.add).then_inc(S["slotE_done"], 1)
                    dve.tensor_tensor(macc[:], macc[:], sel[:], op=ALU.add).then_inc(S["macc_done"], 1)
                    dve.wait_ge(S["slotE_done"], d + 1)
                    dve.tensor_tensor(slot4[:], ehot[:], slotE[:, None, :].to_broadcast([P, TOPK, E]), op=ALU.mult) \
                        .then_inc(S["slot4_done"], 1)
                    dve.wait_ge(S["slot4_done"], d + 1)
                    dve.reduce_sum(slotf[:], slot4[:], AX.X).then_inc(S["slotf_done"], 1)
                    dve.wait_ge(S["slotf_done"], d + 1)
                    dve.tensor_copy(sloti[:], slotf[:]).then_inc(S["slots_done"], 1)
                if live(0):
                    dve.wait_ge(S["kp_done"], a + 1)
                    if first(a):
                        dve.wait_ge(S["cos_done"], 1)
                        dve.wait_ge(S["sin_done"], 1)
                    else:
                        dve.wait_ge(S["kT_done"], a)
                    rope(B7, kr, ks, a, "kr_done", "ks_done")
                    ln_finish(1, a, xn2[:]).then_inc(S["xn2_done"], 1)

            def maxima(t, h):
                dve.wait_ge(S["s_done"], 2 * t + 1 + h)
                dve.reduce_max(mS[:, 2 * h:2 * h + 2, :], scores[:, 1024 * h:1024 * h + 1024]
                               .rearrange("p (r h k) -> p r h k", r=2, k=SEQ), AX.X).then_inc(S["max_done"], 1)

            def rope(bank, r, s_, t, r_name, s_name):
                both = bank[:].rearrange("p (f v q) -> p f v q", f=2, v=2)
                tab = lambda x: x[:, None, bass.ds(t * P, P)].to_broadcast([P, 2, P])
                dve.tensor_tensor(r[:], both[:, :, 0, :], tab(cosT), op=ALU.mult).then_inc(S[r_name], 1)
                dve.tensor_tensor(s_[:], both[:, :, 1, :], tab(sinT), op=ALU.mult).then_inc(S[s_name], 1)

            loop1(dve, step)

            dve.wait_ge(S["cnt_done"], 1)
            tn = [0]

            def then(ins):
                ins.then_inc(S["t_step"], 1)
                tn[0] += 1
                dve.wait_ge(S["t_step"], tn[0])

            then(dve.tensor_copy(cnt[:], B5[:, 0:E]))
            then(dve.tensor_tensor(tail_f[:], cnt[0:1, :], base_e[0:1, :], op=ALU.add))
            dve.tensor_copy(tail_i[:], tail_f[:]).then_inc(S["tab_done"], 1)
            then(dve.tensor_scalar(cpad[:], cnt[:], 1.0 / P, (P - 1.0) / (2 * P), ALU.mult, ALU.add))
            then(dve.tensor_scalar(cfl[:], cpad[:], ROUND, None, ALU.add))
            then(dve.tensor_scalar(nt[:], cfl[:], ROUND, None, ALU.subtract))
            then(dve.tensor_tensor_scan(tend[:], onesf[:, 0:E], nt[:], 0.0, ALU.mult, ALU.add))
            then(dve.tensor_scalar(past[:], tend[:], tileid[:], None, ALU.is_le))
            then(dve.reduce_sum(tcols[:, 2:3], past[:], AX.X))
            then(dve.tensor_tensor(rowt[:], past[:], nt[:], op=ALU.mult))
            then(dve.reduce_sum(tcols[:, 3:4], rowt[:], AX.X))
            then(dve.tensor_scalar(tcols[:, 1:2], tcols[:, 2:3], E - 1.0, None, ALU.min))
            then(dve.tensor_scalar(cgt[:, 0:1], tcols[:, 2:3], float(E), float(P), ALU.is_lt, ALU.mult))
            then(dve.tensor_tensor(cgt[:, 1:2], tileid[:], tcols[:, 3:4], op=ALU.subtract))
            then(dve.tensor_tensor(cgt[:, 2:3], cgt[:, 0:1], cgt[:, 1:2], op=ALU.mult))
            dve.scalar_tensor_tensor(tcols[:, 0:1], tcols[:, 2:3], float(REGION), cgt[:, 2:3], ALU.mult, ALU.add) \
                .then_inc(S["tcols_done"], 1)
            dve.wait_ge(S["tabTp_done"], 1)
            dve.tensor_copy(tabT[:].rearrange("a b t -> a (b t)"), B5[0:1, 0:2 * P]).then_inc(S["tab_done"], 1)

            def shared_act(t):
                dve.wait_ge(S["sg_done"], t + 1)
                dve.wait_ge(S["supu_done"], t + 1)
                if not first(t):
                    dve.wait_ge(S["sdn_done"], t)
                dve.tensor_tensor(saT, sg, SB[1][:, 0:SIP], op=ALU.mult).then_inc(S["saT_done"], 1)

            def shared_sum(t):
                dve.wait_ge(S["sdn_done"], t + 1)
                dve.tensor_tensor(tile_of(xres, t), SB[2][:, 0:D], tile_of(xres, t), op=ALU.add).then_inc(S["xs_done"], 1)

            shared_act(0)
            shared_act(1)
            shared_sum(0)
            with dve.Fori(2, T) as t:
                shared_act(t)
                shared_sum(t - 1)
            shared_sum(T - 1)

            dve.wait_ge(S["tab_done"], 2)

            def gated(t):
                dve.wait_ge(S["sil_done"], t + 1)
                dve.tensor_tensor(act_, sil, SB[0][:, INTER:2 * INTER], op=ALU.mult).then_inc(S["a_done"], 1)

            def weighted(t, k):
                dve.wait_ge(S["dn_done"], t + 1)
                e = dve.value_load(tabT[0:1, 1, bass.ds(t, 1)], min_val=0, max_val=E - 1)
                dve.tensor_scalar(y[k], SB[1][:, 0:D], xg[k][:, bass.ds(e + (D + 1), 1)], None, ALU.mult).then_inc(S["y_done"], 1)

            for k in range(RING):
                gated(k)
                if k:
                    weighted(k - 1, k - 1)
            with dve.Fori(1, RT // RING) as g:
                for k in range(RING):
                    gated(g * RING + k)
                    weighted(g * RING + k - 1, (k - 1) % RING)
            weighted(RT - 1, RING - 1)

            for h in range(2):
                dve.wait_ge(S[f"fin_in{h}"], 32)
                part = xres[:, 8 * h:8 * h + 8, :]
                dve.tensor_tensor(part, part, fin_part(h, 0), op=ALU.add).then_inc(S["fin_step"], 1)
                dve.wait_ge(S["fin_step"], h + 1)
                dve.tensor_tensor(part, part, fin_part(h, 1), op=ALU.add).then_inc(S["fin_add"], 1)

        @block.tensor
        def _(pe):
            pe.wait_ge(S["ident_in"], 16)
            pe.wait_ge(S["w1_in"], 80)

            def transpose2(bank, src):
                for h in range(2):
                    last = pe.transpose(bank[:, h * P:h * P + P], src[:, h * P:h * P + P], ident[:])
                return last

            def quarter(bank, q):
                for j in range(4):
                    cc = 4 * q + j
                    last = pe.transpose(bank[:, j * P:j * P + P], prob[:, cc * P:cc * P + P], ident[:])
                return last

            def av_half(h):
                for cc in range(8 * h, 8 * h + 8):
                    for s_ in range(2):
                        r = slice(SEQ * s_, SEQ * s_ + SEQ)
                        last = pe.matmul(B4[r, 18 * cc:18 * cc + 18], probT[:, cc, r],
                                         vblk[:, s_, cc, :, :].rearrange("p h d -> p (h d)"), start=True, stop=True)
                return last

            def next_xn1T(t):
                pe.wait_ge(S["xn1_done"], t + 1)
                if not first(t):
                    pe.wait_ge(S["x1_done"], t)
                transpose2(B4, xn1).then_inc(S["xn1Tp_done"], 1)

            def next_qkv(t):
                pe.wait_ge(S["xn1T_ev"], t + 1)
                for i, w in enumerate((wk_s, wv_s)):
                    for h in range(C2):
                        pe.matmul(B4[:, i * P:i * P + P], w[:, h, :], xn1T[:, h * P:h * P + P], start=h == 0, stop=h == 1)
                for h in range(C2):
                    last = pe.matmul(B4[:, 2 * P:3 * P], xn1T[:, h * P:h * P + P], wv_s[:, h, :], start=h == 0, stop=h == 1)
                last.then_inc(S["qkv1_done"], 1)

            def step(n, live):
                a, b, c, d = n, n - 1, n - 2, n - 3
                if live(3):
                    pe.wait_ge(S["xn3_done"], d + 1)
                    if live(2):
                        pe.wait_ge(S["mT_ev"], c + 1)
                    transpose2(B6, xn3).then_inc(S["xn3Tp_done"], 1)
                if live(0):
                    pe.wait_ge(S["kT1_ev"], a + 1)
                    pe.wait_ge(S["vT1_ev"], a + 1)
                    if live(3) and not first(d):
                        pe.wait_ge(S["slotE_done"], d)
                    elif live(3):
                        pe.wait_ge(S["o2T_ev"], d + 1)
                    elif not first(a):
                        pe.wait_ge(S["oT1_ev"], a)
                    pe.matmul(B5[:, 0:P], vT1[:], kT1[:], start=True, stop=True).then_inc(S["s1_done"], 1)
                if live(3):
                    pe.wait_ge(S["xn3T_ev"], d + 1)
                    for h in range(C2):
                        last = pe.matmul(B6[:, 0:E], xn3T[:, h * P:h * P + P], gate_s[:, h, :], start=h == 0, stop=h == 1)
                    last.then_inc(S["gate_done"], 1)
                if live(2):
                    pe.wait_ge(S["prob_done"], 2 * c + 1)
                    if live(0):
                        pe.wait_ge(S["v1_ev"], a + 1)
                        pe.wait_ge(S["ks_done"], a)
                    else:
                        pe.wait_ge(S["x1_done"], T)
                        pe.wait_ge(S["o2_done"], c)
                        pe.wait_ge(S["ks_done"], T)
                        pe.wait_ge(S["vblk_ev"], 2 * c + 2)
                    quarter(B4, 0).then_inc(S["tp_done"], 1)
                    quarter(B7, 1).then_inc(S["tp_done"], 1)
                    pe.wait_ge(S["prob_done"], 2 * c + 2)
                    pe.wait_ge(S["tpA_ev"], 3 * c + 1)
                    quarter(B4, 2).then_inc(S["tp_done"], 1)
                    pe.wait_ge(S["tpA_ev"], 3 * c + 2)
                    quarter(B7, 3).then_inc(S["tp_done"], 1)
                if live(1):
                    pe.wait_ge(S["xn2_done"], b + 1)
                    if live(3):
                        pe.wait_ge(S["lsh_done"], d + 1)
                    elif not first(b):
                        pe.wait_ge(S["mT_ev"], b)
                    transpose2(B6, xn2).then_inc(S["xn2Tp_done"], 1)
                if live(2):
                    pe.wait_ge(S["tpA_ev"], 3 * c + 3)
                    pe.wait_ge(S["vblk_ev"], 2 * c + 2)
                    av_half(0)
                if live(1):
                    pe.wait_ge(S["xn2T_ev"], b + 1)
                    for f in range(2):
                        for v in range(2):
                            o = (2 * f + v) * P
                            for h in range(C2):
                                last = pe.matmul(B6[:, o:o + P], xwq_s[:, h, v, f * P:f * P + P], xn2T[:, h * P:h * P + P],
                                                 start=h == 0, stop=h == 1)
                    last.then_inc(S["q_done"], 1)
                if live(0):
                    pe.wait_ge(S["p1n_done"], a + 1)
                    pe.transpose(B5[:, 0:P], p1n[:], ident[:]).then_inc(S["p1Tp_done"], 1)
                if live(2):
                    pe.wait_ge(S["tpD_ev"], c + 1)
                    av_half(1).then_inc(S["av_done"], 1)
                if live(0):
                    pe.wait_ge(S["p1T_ev"], a + 1)
                    pe.matmul(B5[:, 0:P], v1[:], p1T[:], start=True, stop=True).then_inc(S["oT1_done"], 1)
                if live(1):
                    pe.wait_ge(S["ctxV_in"], 32 * (b + 1))
                    if not live(2):
                        pe.wait_ge(S["ks_done"], a)
                    for s_ in range(2):
                        last = pe.matmul(B7[:, D * s_:D * s_ + D], ctxV[:, s_, :, :].rearrange("c h k -> c (h k)"),
                                         xwv_s[:], start=True, stop=True)
                    last.then_inc(S["v_done"], 1)
                if live(2):
                    pe.wait_ge(S["o2_done"], c + 1)
                    if live(0):
                        pe.wait_ge(S["oT1_ev"], a + 1)
                    else:
                        pe.wait_ge(S["slotE_done"], d)
                    transpose2(B5, o2).then_inc(S["o2Tp_done"], 1)
                if live(0):
                    pe.wait_ge(S["oT1_ev"], a + 1)
                    pe.matmul(B4[:, 0:D], oT1[:], wosum[:], start=True, stop=True).then_inc(S["pr1_done"], 1)
                if live(2):
                    pe.wait_ge(S["o2T_ev"], c + 1)
                    if live(1):
                        pe.wait_ge(S["qs_done"], b + 1)
                    else:
                        pe.wait_ge(S["lsh_done"], d + 1)
                    for h in range(C2):
                        last = pe.matmul(B6[:, 0:D], o2T[:, h * P:h * P + P], xwout_s[:, h, :], start=h == 0, stop=h == 1)
                    last.then_inc(S["wout_done"], 1)
                if live(1):
                    made, read = hold(pe, b + 1), hold(pe, 2 * b, 1)
                    past_wait(pe)
                    pe.wait_ge(S["qT_done"], made)
                    pe.wait_ge(S["kblk_done"], made)
                    if not first(b):
                        pe.wait_ge(S["prob_done"], read)
                    for f in range(2):
                        for s_ in range(2):
                            for r_ in range(2):
                                g = slice(64 * r_, 64 * r_ + 64)
                                q = slice(SEQ * s_, SEQ * s_ + SEQ)
                                last = pe.matmul(SB[2 * f + r_][q, :], qT[g, f, q],
                                                 kblk[g, f, s_, :, :].rearrange("p h k -> p (h k)"),
                                                 start=True, stop=False, skip_group_check=True)
                        last.then_inc(S["s_done"], 1)
                if more(n):
                    next_xn1T(a + 1)
                if live(0):
                    pe.wait_ge(S["ctxK_in"], 16 * (a + 1))
                    if live(1):
                        pe.wait_ge(S["vblk_ev"], 2 * b + 2)
                    for f in range(2):
                        for v in range(2):
                            o = (2 * f + v) * P
                            last = pe.matmul(B7[:, o:o + P], xwk_s[:, v, f * P:f * P + P], ctxK[:], start=True, stop=True)
                    last.then_inc(S["kp_done"], 1)
                if live(3):
                    pe.wait_ge(S["sel_done"], d + 1)
                    if not first(d):
                        pe.wait_ge(S["macc_done"], d)
                    if live(2):
                        pe.wait_ge(S["o2T_ev"], c + 1)
                    pe.matmul(B5[:, 0:E], tri[:], sel[:], start=True, stop=False)
                    pe.matmul(B5[:, 0:E], ones[:], macc[:], start=False, stop=True).then_inc(S["pre_done"], 1)
                if live(1):
                    pe.wait_ge(S["mlo_done"], b + 1)
                    if live(2):
                        pe.wait_ge(S["x2_done"], c + 1)
                    pe.transpose(B6[:, 0:64].bitcast(BF16), mstack[:].rearrange("p r m -> p (r m)"), identb[:]) \
                        .then_inc(S["mTp_done"], 1)
                if more(n):
                    next_qkv(a + 1)
                if live(1):
                    pe.wait_ge(S["mT_ev"], b + 1)
                    for r_ in range(4):
                        g = slice(32 * r_, 32 * r_ + 32)
                        last = pe.matmul(SB[r_], mT[g, :], inj[g, :], start=False, stop=True, skip_group_check=True)
                        if r_ % 2:
                            last.then_inc(S["inj_done"], 1)

            next_xn1T(0)
            next_qkv(0)
            pe.wait_ge(S["wosum_done"], 1)
            pe.wait_ge(S["xw_in"], 96)
            pe.wait_ge(S["c1_in"], 176)

            loop1(pe, step)

            pe.wait_ge(S["macc_done"], T)
            pe.matmul(B5[:, 0:E], ones[:], macc[:], start=True, stop=True).then_inc(S["cnt_done"], 1)

            pe.wait_ge(S["sw_in"], 32)
            pe.wait_ge(S["xn3T_kept"], T)

            def shared_up(t):
                for v, name in ((0, "supg_done"), (1, "supu_done")):
                    if not first(t):
                        pe.wait_ge(S[("sg_done", "saT_done")[v]], t)
                    for j in range(SC):
                        for h in range(C2):
                            last = pe.matmul(SB[v][:, j * P:j * P + P], sup_s[:, h, v, j * P:j * P + P],
                                             xn3T_all[:, bass.ds(t, 1), h * P:h * P + P].rearrange("p a q -> p (a q)"),
                                             start=h == 0, stop=h == 1)
                    last.then_inc(S[name], 1)

            def shared_down(t):
                pe.wait_ge(S["saT_done"], t + 1)
                if not first(t):
                    pe.wait_ge(S["xs_done"], t)
                for j in range(SC):
                    last = pe.matmul(SB[2][:, 0:D], saT[:, j * P:j * P + P], sdown_s[:, j, :], start=j == 0, stop=j == SC - 1)
                last.then_inc(S["sdn_done"], 1)

            shared_up(0)
            pe.wait_ge(S["tcols_done"], 1)
            pe.matmul(B5[0:1, 0:P], tcols[:, 0:1], ident[:], start=True, stop=True)
            pe.matmul(B5[0:1, P:2 * P], tcols[:, 1:2], ident[:], start=True, stop=True).then_inc(S["tabTp_done"], 1)
            shared_up(1)
            shared_down(0)
            with pe.Fori(2, T) as t:
                shared_up(t)
                shared_down(t - 1)
            shared_down(T - 1)

            pe.wait_ge(S["rw_in"], 32)
            pe.wait_ge(S["tab_done"], 2)
            pe.wait_ge(S["xs_done"], T)

            def expert(t):
                return pe.value_load(tabT[0:1, 1, bass.ds(t, 1)], min_val=0, max_val=E - 1)

            def rows_in(t, k, g):
                pe.wait_ge(S[f"xg_in{k}"], (g + 1) * 16)
                transpose2(B4, xg[k]).then_inc(S["xTp_done"], 1)

            def up(t, e):
                pe.wait_ge(S["xgT_ev"], t + 1)
                for h in range(C2):
                    last = pe.matmul(SB[0][:, 0:2 * INTER], xgT[:, h * P:h * P + P],
                                     up_s[:, bass.ds(e, 1), h, :].rearrange("p a n -> p (a n)"), start=h == 0, stop=h == 1)
                last.then_inc(S["up_done"], 1)

            def down(t, e):
                pe.wait_ge(S["aT_ev"], t + 1)
                if not first(t):
                    pe.wait_ge(S["y_done"], t)
                for h in range(2):
                    last = pe.matmul(SB[1][:, 0:D], aT[:, h, :], down_s[:, bass.ds(e, 1), h, :].rearrange("p a n -> p (a n)"),
                                     start=h == 0, stop=h == 1)
                last.then_inc(S["dn_done"], 1)

            def gated_T(t):
                pe.wait_ge(S["a_done"], t + 1)
                for h in range(2):
                    last = pe.transpose(SB[2][0:HALF_I, h * P:h * P + P], act_[:, h * HALF_I:h * HALF_I + HALF_I], ident[:])
                last.then_inc(S["aTp_done"], 1)

            def four(g, is_first, is_last):
                t0 = g * RING
                e_before = None if is_first else expert(t0 - 1)
                for k in range(RING):
                    t = t0 + k
                    e = expert(t)
                    up(t, e)
                    if not (is_last and k == RING - 1):
                        rows_in(t + 1, (k + 1) % RING, g + (1 if k == RING - 1 else 0))
                    if e_before is not None:
                        down(t - 1, e_before)
                    gated_T(t)
                    e_before = e
                if is_last:
                    down(t0 + RING - 1, e_before)

            rows_in(0, 0, 0)
            four(0, True, False)
            with pe.Fori(1, RT // RING - 1) as g:
                four(g, False, False)
            four(RT // RING - 1, False, True)


def kernel(**inputs):
    import numpy as np
    import ml_dtypes
    import concourse.bacc as bacc
    from concourse import mybir as mb
    from concourse.bass_utils import run_bass_kernel_spmd

    f = np.float32
    a = {k: np.asarray(v) for k, v in inputs.items()}

    def swapped(w):
        return np.stack([w, w.reshape(w.shape[0], -1, 2)[:, :, ::-1].reshape(w.shape)])

    wkv = a["L0_xattn_Wkv"]
    sup = np.zeros((D, 2, SIP), f)
    sup[:, :, :SI] = a["L0_ffn_shared_up_w"].T.reshape(D, 2, SI)
    sdown = np.zeros((SIP, D), f)
    sdown[:SI] = a["L0_ffn_shared_down_w"].T
    part = np.arange(P)
    inject = np.zeros((P, 512), f)
    for r in range(P):
        if r % 32 < 16:
            inject[r] = np.arange(512) // SEQ == r % 8
    arrays = {
        "x": a["x"].reshape(TOK, D),
        "ctxT": a["ctx_1024"].reshape(TOK, CTX).T,
        "pos": a["fside_BxSx2_0"].reshape(TOK, 2).T[(part % HD) // 4],
        "wk": a["L0_attn_Wk"], "wv": a["L0_attn_Wv"], "bk": a["L0_attn_bk"], "bv": a["L0_attn_bv"],
        "wo": a["L0_attn_Wo"], "bo": a["L0_attn_bo"],
        "xwq": swapped(a["L0_xattn_Wq"]).reshape(2, C2, P, D).transpose(2, 1, 0, 3), "xwk": swapped(wkv[:, :D]), "xwv": wkv[:, D:], "xwout": a["L0_xattn_Wout"],
        "xbout": a["L0_xattn_bout"], "gate": a["L0_ffn_gate_w"].T,
        "upw": a["L0_ffn_expert_up_w"].reshape(E, 2 * INTER, C2, P).transpose(3, 0, 2, 1),
        "downw": a["L0_ffn_expert_down_w"].reshape(E, D, 2, HALF_I).transpose(3, 0, 2, 1),
        "supw": sup.reshape(C2, P, 2, SIP).transpose(1, 0, 2, 3),
        "sdownw": sdown,
        "identity": np.eye(P, dtype=f),
        "identity_b": np.eye(P, dtype=ml_dtypes.bfloat16),
        "head_mask": ((part // HD % 8)[:, None] == np.arange(8)[None]).astype(f),
        "inject_rows": inject.astype(ml_dtypes.bfloat16),
        "before": (part[:, None] < part[None]).astype(ml_dtypes.bfloat16),
        "rope_freq": np.stack([np.where(part % 4 // 2 == 0, 1.0, 0.01), np.where(part % 2 == 0, -1.0, 1.0)], 1).astype(f),
        "region_base": np.broadcast_to(np.arange(E) * REGION, (P, E)).astype(f),
        "iota_e": np.broadcast_to(np.arange(E), (P, E)).astype(f),
        "token_ids": (part[:, None] + P * np.arange(T)[None]).astype(np.int32),
        "pad_rows": np.zeros((P, ROW), f),
        "tile_ids": part[:, None].astype(f),
        "ones_f": np.ones((P, P), f),
        "ones_b": np.ones((P, P), ml_dtypes.bfloat16),
    }
    arrays["pad_rows"].view(np.int32)[:, D] = TOK + part
    nc = bacc.Bacc("TRN2", target_bir_lowering=False, num_devices=1)
    sent, args = {}, {}
    for name, value in arrays.items():
        value = np.ascontiguousarray(value)
        sent[f"in_{name}"] = value
        args[name] = nc.dram_tensor(f"in_{name}", value.shape, mb.dt.from_np(value.dtype), kind="ExternalInput").ap()
    args["out"] = nc.dram_tensor("out_0", (TOK, D), mb.dt.float32, kind="ExternalOutput").ap()
    decoder_kernel(nc, **args)
    got = run_bass_kernel_spmd(nc, [sent], core_ids=[0])
    return got.results[0]["out_0"].reshape(inputs["x"].shape)
```

```python
from contextlib import ExitStack

import concourse.bass as bass
from concourse import mybir

ALU = mybir.AluOpType
ACT = mybir.ActivationFunctionType
AX = mybir.AxisListType
F32 = mybir.dt.float32
BF16 = mybir.dt.bfloat16
I32 = mybir.dt.int32
U32 = mybir.dt.uint32

P = 128
D = 256
C2 = D // P
SEQ = 64
TOK = 2048
T = TOK // P
HEADS, HD = 32, 8
CTX = 128
E, TOPK, GROUPS, TOPG = 16, 4, 4, 2
INTER = 176
HALF_I = INTER // 2
SI = 352
SC = (SI + P - 1) // P
SIP = SC * P
REGION = TOK + P
ROW = D + 1 + E
PAD_TILE = E * REGION
FILL = 5
FT = T // 4
RING = 8
RT = -(-((TOK * TOPK + E * (P - 1)) // P) // RING) * RING
ACC = TOK + P
EPS = 1e-5
XSCALE = float(HD) ** -0.5
ASCALE = 1.0 / 128.0
TWO_PI_HI = 6.28125
TWO_PI_LO = 6.283185307179586 - 6.28125
ROUND = 1.5 * 2.0 ** 23
PI_IN = 3.1415925
AHEAD = 3


def decoder_kernel(nc, x, ctxT, pos, wk, wv, bk, bv, wo, bo, xwq, xwk, xwv, xwout, xbout, gate, upw, downw,
                   supw, sdownw, identity, identity_b, head_mask, inject_rows, before, rope_freq, region_base, iota_e,
                   token_ids, pad_rows, tile_ids, ones_f, ones_b, out):
    with ExitStack() as ctx:
        def sb(name, shape, dt=F32):
            return ctx.enter_context(nc.sbuf_tensor(name, shape, dt))

        def sem(name):
            return ctx.enter_context(nc.semaphore(name))

        routed = nc.dram_tensor("routed", [PAD_TILE + P, ROW], F32).ap()
        acc = [nc.dram_tensor(f"acc{k}", [ACC, D], F32).ap() for k in range(2)]

        scores = ctx.enter_context(nc.psum_tensor("scores", [P, 2048], F32))
        B4, B5, B6, B7 = (ctx.enter_context(nc.psum_tensor(f"bank{k}", [P, 512], F32)) for k in range(4, 8))
        SB = [scores[:, 512 * k:512 * k + 512] for k in range(4)]

        ident = sb("ident", [P, P])
        hmask = sb("hmask", [P, 8])
        inj = sb("inj", [P, 512], BF16)
        tri = sb("tri", [P, P], BF16)
        ones = sb("ones", [P, P], BF16)
        identb = sb("identb", [P, P], BF16)
        onesf = sb("onesf", [P, P])
        freq = sb("freq", [P, 2])
        base_e = sb("base_e", [P, E])
        iota = sb("iota", [P, E])
        tokid = sb("tokid", [P, T], I32)
        tileid = sb("tileid", [P, 1])
        pad = sb("pad", [P, ROW])
        zeros = sb("zeros", [P, D])
        wk_s = sb("wk_s", [P, C2, P])
        wv_s = sb("wv_s", [P, C2, P])
        bk_s = sb("bk_s", [P, 1])
        bv_s = sb("bv_s", [P, 1])
        wosum = sb("wosum", [P, D])
        bo_s = sb("bo_s", [P, D])
        xwq_s = sb("xwq_s", [P, C2, 2, D])
        xwk_s = sb("xwk_s", [P, 2, D])
        xwv_s = sb("xwv_s", [P, D])
        xwout_s = sb("xwout_s", [P, C2, D])
        xbout_s = sb("xbout_s", [P, D])
        gate_s = sb("gate_s", [P, C2, E])
        up_s = sb("up_s", [P, E, C2, 2 * INTER])
        down_s = sb("down_s", [HALF_I, E, 2, D])
        sup_s = sb("sup_s", [P, C2, 2, SIP])
        sdown_s = sb("sdown_s", [P, SC, D])
        xres = sb("xres", [P, T, D])
        xn3T_all = sb("xn3T_all", [P, T, D])
        cosT = sb("cosT", [P, TOK])
        sinT = sb("sinT", [P, TOK])
        prob = sb("prob", [P, 2048])
        probT = sb("probT", [P, 16, P])
        ctxK = sb("ctxK", [P, P])
        ctxV = sb("ctxV", [P, 2, 2, SEQ])
        st = sb("st", [P, 6])
        ln = [(sb(f"mv{k}", [P, 2]), sb(f"lnv{k}", [P, 1]), sb(f"rs{k}", [P, 1]), sb(f"nt{k}", [P, 2]),
               sb(f"rstd{k}", [P, 1])) for k in range(3)]
        xn1 = sb("xn1", [P, D])
        xn1T = sb("xn1T", [P, D])
        xbo = sb("xbo", [P, D])
        kT1 = sb("kT1", [P, P])
        vT1 = sb("vT1", [P, P])
        v1 = sb("v1", [P, P])
        mx1 = sb("mx1", [P, 1])
        nmx1 = sb("nmx1", [P, 1])
        p1 = sb("p1", [P, P])
        p1n = sb("p1n", [P, P])
        sum1 = sb("sum1", [P, 1])
        rsum1 = sb("rsum1", [P, 1])
        p1T = sb("p1T", [P, P])
        oT1 = sb("oT1", [P, P])
        xn2 = sb("xn2", [P, D])
        xn2T = sb("xn2T", [P, D])
        xbout1 = sb("xbout1", [P, D])
        qr = sb("qr", [P, 2, P])
        qs = sb("qs", [P, 2, P])
        qT = sb("qT", [P, 2, P])
        kr = sb("kr", [P, 2, P])
        ks = sb("ks", [P, 2, P])
        kT = sb("kT", [P, 2, P])
        kblk = sb("kblk", [P, 2, 2, 8, SEQ])
        vblk = sb("vblk", [P, 2, 16, 2, 9])
        mS = sb("mS", [P, 4, 8])
        mstack = sb("mstack", [P, 4, 32], BF16)
        mT = sb("mT", [P, P], BF16)
        rden = sb("rden", [P, HEADS])
        o2 = sb("o2", [P, D])
        o2T = sb("o2T", [P, D])
        xn3 = sb("xn3", [P, D])
        xrow = sb("xrow", [P, ROW])
        xn3T = sb("xn3T", [P, D])
        lmx = sb("lmx", [P, 1])
        lsh = sb("lsh", [P, E])
        lex = sb("lex", [P, E])
        lsum = sb("lsum", [P, 1])
        lrs = sb("lrs", [P, 1])
        prb = sb("prb", [P, E])
        gmax = sb("gmax", [P, 8])
        gtop = sb("gtop", [P, 8])
        gidx = sb("gidx", [P, 8], U32)
        gidf = sb("gidf", [P, TOPG])
        ghot = sb("ghot", [P, TOPG, GROUPS])
        gm = sb("gm", [P, GROUPS])
        msc = sb("msc", [P, E])
        etop = sb("etop", [P, 8])
        eidx = sb("eidx", [P, 8], U32)
        eidf = sb("eidf", [P, TOPK])
        ehot = sb("ehot", [P, TOPK, E])
        self32 = sb("self32", [P, E])
        sel = sb("sel", [P, E], BF16)
        msel = sb("msel", [P, E])
        wsum = sb("wsum", [P, 1])
        wsum1 = sb("wsum1", [P, 1])
        wrec = sb("wrec", [P, 1])
        macc = sb("macc", [P, E], BF16)
        slotE = sb("slotE", [P, E])
        slot4 = sb("slot4", [P, TOPK, E])
        slotf = sb("slotf", [P, TOPK])
        sloti = sb("sloti", [P, TOPK], I32)
        cnt = sb("cnt", [P, E])
        tail_f = sb("tail_f", [1, E])
        tail_i = sb("tail_i", [1, E], I32)
        cpad = sb("cpad", [P, E])
        cfl = sb("cfl", [P, E])
        cgt = sb("cgt", [P, E])
        nt = sb("nt", [P, E])
        tend = sb("tend", [P, E])
        past = sb("past", [P, E])
        rowt = sb("rowt", [P, E])
        tcols = sb("tcols", [P, 4])
        tabT = sb("tabT", [1, 2, P], I32)
        kblk_flat = kblk[:].rearrange("p f b h k -> p (f b h k)")
        sg, saT = kblk_flat[:, 0:SIP], kblk_flat[:, SIP:2 * SIP]
        y = [cosT[:, D * k:D * k + D] for k in range(RING)]
        xg = [(sinT[:], probT[:].rearrange("p c q -> p (c q)"))[k % 2][:, ROW * (k // 2):ROW * (k // 2) + ROW] for k in range(RING)]
        xgT = xn1T
        sil = xn1[:, 0:INTER]
        act_ = xn2[:, 0:INTER]
        aT = xn2T[0:HALF_I, :].rearrange("p (c q) -> p c q", c=2)

        spare = {(eng.engine, k): eng.alloc_register(f"spare{k}") for eng in (nc.vector, nc.gpsimd, nc.tensor) for k in range(3)}

        e_of = [nc.tensor.alloc_register(f"expert{k}") for k in range(4)]

        block = ctx.enter_context(nc.Block())

        S = {name: sem(name) for name in (
            "aT_ev aTp_done a_done abs_done acc_zeroed agg0 agg1 agg2 angle_step av_done bn0 bn1 bn2 c1_in "
            "cnt_done cos_done ctxK_in ctxV_in cw_done dn_done eidf_done eidx_done fin_add fin_in0 fin_in1 "
            "fin_in2 fin_in3 fin_step gate_done ident_in inj_done kT1_ev kT_done kblk_done kp_done ks_done "
            "lex_done lmx_done lnv0 lnv1 lnv2 lsh_done mT_ev mTp_done macc_done max_done mhi_done mlo_done "
            "msel_done mx1_done nmx1_done nt0 nt1 nt2 o2T_ev o2Tp_done o2_done oT1_done oT1_ev out_done "
            "p1T_ev p1Tp_done p1a p1b p1n_done pad_out pads_done pos_in pr1_done pre_done prob_done qT_done "
            "q_done qkv1_done qs_done r_step rden_done row_done rs00 rs01 rs02 rstd0 rstd1 rstd2 rsum1_done "
            "rw_in s1_done s_done saT_done scattered sdn_done sel_done sg_done sil_done sin_done slot4_done "
            "slotE_done slotf_done slots_done supg_done supu_done sw_in t_step tabTp_done tab_done "
            "tcols_done tok_done tpA_ev tpD_ev tp_done up_done v1_ev vT1_ev v_done vblk_ev vblk_set w1_in "
            "wo_in wosum_done wosum_step wout_done wrec_done ws_step x0_in x1_done x2_done xTp_done x_in "
            "xbo_done xbout_done xgT_ev xn1T_ev xn1Tp_done xn1_done xn2T_ev xn2Tp_done xn2_done xn3T_ev "
            "xn3T_kept xn3Tp_done xn3_done xs_done xw_in y_done zero_set ").split()}
        S.update({f"xg_in{k}": sem(f"xg_in{k}") for k in range(RING)})
        S.update({f"added{k}": sem(f"added{k}") for k in range(2)})

        def tile_of(buf, t):
            return buf[:, bass.ds(t, 1), :].rearrange("p a d -> p (a d)")

        def hold(eng, count, k=0):
            if isinstance(count, int):
                return count
            eng.reg_add(spare[eng.engine, k], count, 0)
            return spare[eng.engine, k]

        def past_wait(eng):
            eng.wait_ge(S["zero_set"], 5)

        def fin_part(k, q):
            place = ((cosT[:], sinT[:]), (prob[:], probT[:].rearrange("p c q -> p (c q)")))[k // 2][q]
            return place.rearrange("p (t d) -> p t d", d=D)[:, FT * (k % 2):FT * (k % 2) + FT, :]

        def first(t):
            return isinstance(t, int) and t == 0

        def drain(n, k):
            return isinstance(n, int) and n == T - 1 + k

        def more(n):
            return not isinstance(n, int) or n + 1 < T

        def loop1(eng, body):
            for n in range(AHEAD + 1):
                body(n, lambda k, n=n: k <= n)
            with eng.Fori(AHEAD + 1, T - 1) as n:
                body(n, lambda k: True)
            for n in range(T - 1, T + AHEAD):
                body(n, lambda k, n=n: n - k < T)

        posb = xn3T_all[:, 0:8, :].rearrange("p t d -> p (t d)")
        angle = xn3T_all[:, 8:16, :].rearrange("p t d -> p (t d)")
        LN = [{what: f"{what}{k}" for what in ("bn", "agg", "lnv", "rs0", "nt", "rstd")} for k in range(3)]

        @block.sync
        def _(sp):
            sp.dma_start(ident[:], identity).then_inc(S["ident_in"], 16)
            sp.dma_start(xres[:, 0:2, :], x[0:2 * P, :].rearrange("(t p) d -> p t d", p=P)).then_inc(S["x0_in"], 16)
            sp.dma_start(wk_s[:], wk.rearrange("(c p) n -> p c n", p=P)).then_inc(S["w1_in"], 16)
            sp.dma_start(wv_s[:], wv.rearrange("(c p) n -> p c n", p=P)).then_inc(S["w1_in"], 16)
            sp.dma_start(bk_s[:], bk.rearrange("(p a) -> p a", a=1)).then_inc(S["w1_in"], 16)
            sp.dma_start(bv_s[:], bv.rearrange("(p a) -> p a", a=1)).then_inc(S["w1_in"], 16)
            sp.dma_start(bo_s[:], bo.partition_broadcast(P)).then_inc(S["w1_in"], 16)
            sp.dma_start(hmask[:], head_mask).then_inc(S["w1_in"], 16)
            sp.dma_start(xwk_s[:], xwk.rearrange("v p n -> p v n")).then_inc(S["w1_in"], 16)
            sp.dma_start(prob[:].rearrange("p (h n) -> p h n", n=D),
                          wo.rearrange("(h d) n -> d h n", d=P)[:, 0:8, :]).then_inc(S["wo_in"], 16)
            sp.dma_start(probT[:].rearrange("p c q -> p (c q)").rearrange("p (h n) -> p h n", n=D),
                          wo.rearrange("(h d) n -> d h n", d=P)[:, 8:16, :]).then_inc(S["wo_in"], 16)
            for dst, src in ((inj, inject_rows), (tri, before), (ones, ones_b), (identb, identity_b), (onesf, ones_f),
                             (base_e, region_base), (iota, iota_e), (tokid, token_ids), (tileid, tile_ids), (pad, pad_rows)):
                sp.dma_start(dst[:], src).then_inc(S["c1_in"], 16)
            sp.dma_start(xres[:, 2:T, :], x[2 * P:TOK, :].rearrange("(t p) d -> p t d", p=P)).then_inc(S["x_in"], 16)
            sp.dma_start(xwv_s[:], xwv).then_inc(S["xw_in"], 16)
            sp.dma_start(xbout_s[:], xbout.partition_broadcast(P)).then_inc(S["xw_in"], 16)
            sp.dma_start(xwq_s[:], xwq).then_inc(S["xw_in"], 16)
            sp.dma_start(xwout_s[:], xwout.rearrange("(c p) n -> p c n", p=P)).then_inc(S["xw_in"], 16)
            sp.dma_start(gate_s[:], gate.rearrange("(c p) n -> p c n", p=P)).then_inc(S["xw_in"], 16)
            sp.dma_start(sup_s[:], supw).then_inc(S["sw_in"], 16)
            sp.dma_start(sdown_s[:], sdownw.rearrange("(c p) n -> p c n", p=P)).then_inc(S["sw_in"], 16)

            def step(n, live):
                if live(0):
                    if not first(n):
                        sp.wait_ge(S["kp_done"], n)
                    sp.dma_start(ctxK[:], ctxT[:, bass.ds(n * P, P)]).then_inc(S["ctxK_in"], 16)
                if live(1):
                    if not first(n - 1):
                        sp.wait_ge(S["v_done"], n - 1)
                    for hp in range(2):
                        sp.dma_start(ctxV[:, :, hp, :], ctxT[:, bass.ds((n - 1) * P, P)].rearrange("c (s k) -> c s k", s=2)) \
                            .then_inc(S["ctxV_in"], 16)
                if live(3):
                    d = n - 3
                    if first(d):
                        sp.wait_ge(S["zero_set"], 5)
                    for a in acc:
                        sp.dma_start(a[bass.ds(d * P, P), :], zeros[:]).then_inc(S["acc_zeroed"], 16)
                    sp.dma_start(up_s[:, bass.ds(d, 1), :, :].rearrange("p a c n -> p (a c n)"),
                                 upw[:, bass.ds(d, 1), :, :].rearrange("p a c n -> p (a c n)")).then_inc(S["rw_in"], 16)
                    sp.dma_start(down_s[:, bass.ds(d, 1), :, :].rearrange("p a c n -> p (a c n)"),
                                 downw[:, bass.ds(d, 1), :, :].rearrange("p a c n -> p (a c n)")).then_inc(S["rw_in"], 16)

            loop1(sp, step)
            for a in acc:
                sp.dma_start(a[TOK:ACC, :], zeros[:]).then_inc(S["acc_zeroed"], 16)
            sp.dma_start(routed[PAD_TILE:PAD_TILE + P, :], pad[:]).then_inc(S["pad_out"], 16)

            sp.wait_ge(S["tab_done"], 2)
            sp.wait_ge(S["scattered"], 16 * TOPK * T)
            for e in range(E):
                end = sp.value_load(tail_i[0:1, e:e + 1], min_val=e * REGION, max_val=e * REGION + TOK)
                sp.dma_start(routed[bass.ds(end, P), :], pad[:]).then_inc(S["pads_done"], 16)
            sp.wait_ge(S["pads_done"], 16 * E)
            sp.wait_ge(S["pad_out"], 16)

            for k in range(RING):
                row = sp.value_load(tabT[0:1, 0, k:k + 1], min_val=0, max_val=PAD_TILE)
                sp.dma_start(xg[k], routed[bass.ds(row, P), :]).then_inc(S[f"xg_in{k}"], 16)
            with sp.Fori(1, RT // RING) as g:
                for k in range(RING):
                    sp.wait_ge(S[f"added{k % 2}"], g * 16 * (RING // 2) - 16 * (RING // 2 - 1 - k // 2))
                    row = sp.value_load(tabT[0:1, 0, bass.ds(g * RING + k, 1)], min_val=0, max_val=PAD_TILE)
                    sp.dma_start(xg[k], routed[bass.ds(row, P), :]).then_inc(S[f"xg_in{k}"], 16)

            sp.wait_ge(S["added0"], 16 * (RT // 2))
            sp.wait_ge(S["added1"], 16 * (RT // 2))
            for k in range(4):
                for q in range(2):
                    sp.dma_start(fin_part(k, q), acc[q][FT * P * k:FT * P * (k + 1), :].rearrange("(t p) d -> p t d", p=P)) \
                        .then_inc(S[f"fin_in{k}"], 16)
            for k in range(4):
                sp.wait_ge(S["fin_add"], k + 1)
                sp.dma_start(out[FT * P * k:FT * P * (k + 1), :].rearrange("(t p) d -> p t d", p=P),
                             xres[:, FT * k:FT * (k + 1), :]).then_inc(S["out_done"], 16)
            sp.wait_ge(S["out_done"], 64)

        @block.gpsimd
        def _(pool):
            pool.memset(zeros[:], 0.0).then_inc(S["zero_set"], 1)
            pool.memset(p1[:], 0.0).then_inc(S["zero_set"], 1)
            pool.memset(mstack[:], 0.0).then_inc(S["zero_set"], 1)
            pool.memset(macc[:], 0.0).then_inc(S["zero_set"], 1)
            pool.memset(gmax[:], -1.0).then_inc(S["zero_set"], 1)
            pool.memset(vblk[:], 0.0).then_inc(S["vblk_set"], 1)
            pool.wait_ge(S["vblk_set"], 1)
            for hp in range(2):
                pool.memset(vblk[64 * hp:64 * hp + 64, :, :, hp, 8:9], 1.0).then_inc(S["vblk_set"], 1)
            pool.wait_ge(S["vblk_set"], 3)
            pool.wait_ge(S["wo_in"], 32)
            wob = prob[:]
            wob2 = probT[:].rearrange("p c q -> p (c q)")
            pool.tensor_tensor(wob, wob, wob2, op=ALU.add).then_inc(S["wosum_step"], 1)
            for k, w in enumerate((1024, 512)):
                pool.wait_ge(S["wosum_step"], k + 1)
                pool.tensor_tensor(wob[:, 0:w], wob[:, 0:w], wob[:, w:2 * w], op=ALU.add).then_inc(S["wosum_step"], 1)
            pool.wait_ge(S["wosum_step"], 3)
            pool.tensor_tensor(wosum[:], wob[:, 0:D], wob[:, D:2 * D], op=ALU.add).then_inc(S["wosum_done"], 1)
            pool.wait_ge(S["w1_in"], 112)
            pool.wait_ge(S["x0_in"], 16)

            def next_xbo(t):
                if not first(t):
                    pool.wait_ge(S["x1_done"], t)
                pool.tensor_tensor(xbo[:], tile_of(xres, t), bo_s[:], op=ALU.add).then_inc(S["xbo_done"], 1)

            next_xbo(0)

            def step(n, live):
                a, b, c, d = n, n - 1, n - 2, n - 3
                if live(3):
                    pool.wait_ge(S["xn3T_ev"], d + 1)
                    pool.tensor_copy(tile_of(xn3T_all, d), xn3T[:]).then_inc(S["xn3T_kept"], 1)
                    held, away = hold(pool, d + 1), hold(pool, d * 16 * TOPK, 1)
                    past_wait(pool)
                    pool.wait_ge(S["xn3_done"], held)
                    if not first(d):
                        pool.wait_ge(S["scattered"], away)
                    pool.tensor_copy(xrow[:, 0:D], xn3[:]).then_inc(S["row_done"], 1)
                    pool.tensor_copy(xrow[:, D:D + 1].bitcast(I32), tokid[:, bass.ds(d, 1)]).then_inc(S["tok_done"], 1)
                if live(0):
                    pool.wait_ge(S["ks_done"], n + 1)
                    pool.tensor_tensor(kT[:], kr[:], ks[:], op=ALU.add).then_inc(S["kT_done"], 1)
                    pool.wait_ge(S["kT_done"], n + 1)
                    if not first(n):
                        pool.wait_ge(S["s_done"], 2 * n)
                    pool.tensor_tensor(kblk[:].rearrange("p f b h k -> p (f b) h k"),
                                       kT[:].rearrange("p f (b k) -> p (f b) k", k=SEQ)[:, :, None, :].to_broadcast([P, 4, 8, SEQ]),
                                       hmask[:, None, :, None].to_broadcast([P, 4, 8, SEQ]), op=ALU.mult).then_inc(S["kblk_done"], 1)
                if live(3):
                    held = hold(pool, d + 1)
                    past_wait(pool)
                    pool.wait_ge(S["row_done"], held)
                    pool.wait_ge(S["tok_done"], held)
                    pool.wait_ge(S["cw_done"], held)
                    pool.wait_ge(S["slots_done"], held)
                    for k in range(TOPK):
                        pool.indirect_dma_start(routed, bass.IndirectOffsetOnAxis(ap=sloti[:, k:k + 1], axis=0),
                                                xrow[:], None).then_inc(S["scattered"], 16)
                if more(n):
                    if first(n - 1):
                        pool.wait_ge(S["x_in"], 16)
                    next_xbo(n + 1)
                if live(1):
                    pool.wait_ge(S["x1_done"], b + 1)
                    if not first(b):
                        pool.wait_ge(S["x2_done"], b)
                    if first(b):
                        pool.wait_ge(S["xw_in"], 80)
                    pool.tensor_tensor(xbout1[:], tile_of(xres, b), xbout_s[:], op=ALU.add).then_inc(S["xbout_done"], 1)

            loop1(pool, step)

            pool.wait_ge(S["acc_zeroed"], 32 * (ACC // P))
            def add(t, k, seen):
                made = hold(pool, t + 1)
                before_it = None if seen is None else hold(pool, seen, 1)
                past_wait(pool)
                pool.wait_ge(S["y_done"], made)
                if before_it is not None:
                    pool.wait_ge(S[f"added{k % 2}"], before_it)
                pool.indirect_dma_start(acc[k % 2], bass.IndirectOffsetOnAxis(ap=xg[k][:, D:D + 1].bitcast(I32), axis=0),
                                        y[k], None, compute_op=ALU.add).then_inc(S[f"added{k % 2}"], 16)

            for k in range(RING):
                add(k, k, None if k < 2 else 16 * (k // 2))
            with pool.Fori(1, RT // RING) as g:
                for k in range(RING):
                    add(g * RING + k, k, g * 16 * (RING // 2) + 16 * (k // 2))

        @block.scalar
        def _(act):
            act.dma_start(freq[:], rope_freq).then_inc(S["pos_in"], 16)
            act.dma_start(posb, pos).then_inc(S["pos_in"], 16)
            act.preload_act_table_set("natural_log_exp_and_others")

            def rsqrt(k, t):
                mv, lnv, rs, _, _ = ln[k]
                act.wait_ge(S[LN[k]["agg"]], t + 1)
                act.activation(lnv[:], mv[:, 1:2], ACT.Ln, bias=EPS).then_inc(S[LN[k]["lnv"]], 1)
                act.wait_ge(S[LN[k]["lnv"]], t + 1)
                act.activation(rs[:], lnv[:], ACT.Exp, scale=-0.5).then_inc(S[LN[k]["rs0"]], 1)

            def next_xn1T(t):
                act.wait_ge(S["xn1Tp_done"], t + 1)
                act.activation(xn1T[:], B4[:, 0:D], ACT.Copy).then_inc(S["xn1T_ev"], 1)

            def next_qkv(t):
                act.wait_ge(S["qkv1_done"], t + 1)
                act.activation(kT1[:], B4[:, 0:P], ACT.Identity, bias=bk_s[:]).then_inc(S["kT1_ev"], 1)
                act.activation(vT1[:], B4[:, P:2 * P], ACT.Identity, bias=bv_s[:]).then_inc(S["vT1_ev"], 1)
                act.activation(v1[:], B4[:, 2 * P:3 * P], ACT.Copy).then_inc(S["v1_ev"], 1)

            rsqrt(0, 0)
            next_xn1T(0)
            next_qkv(0)
            act.wait_ge(S["angle_step"], 6)
            act.activation(sinT[:], angle, ACT.Sin, scale=freq[:, 1:2]).then_inc(S["sin_done"], 1)
            act.activation(posb, angle, ACT.Abs).then_inc(S["abs_done"], 1)
            act.wait_ge(S["abs_done"], 1)
            act.activation(cosT[:], posb, ACT.Sin, scale=-1.0, bias=1.5707963267948966).then_inc(S["cos_done"], 1)
            act.preload_act_table_set("natural_log_exp_and_others")

            def probabilities(t, h):
                act.wait_ge(S["inj_done"], 2 * t + 1 + h)
                if h == 0 and not first(t):
                    act.wait_ge(S["tp_done"], 4 * t)
                act.activation(prob[:, 1024 * h:1024 * h + 1024], scores[:, 1024 * h:1024 * h + 1024],
                               ACT.Exp, scale=XSCALE).then_inc(S["prob_done"], 1)

            def quarter(t, q, bank):
                act.wait_ge(S["tp_done"], 4 * t + q + 1)
                act.activation(probT[:, 4 * q:4 * q + 4, :].rearrange("p c q -> p (c q)"), bank[:], ACT.Copy) \
                    .then_inc(S["tpA_ev"], 1)

            def shared_silu(t):
                act.wait_ge(S["supg_done"], t + 1)
                if not first(t):
                    act.wait_ge(S["saT_done"], t)
                act.activation(sg, SB[0][:, 0:SIP], ACT.Silu).then_inc(S["sg_done"], 1)

            def step(n, live):
                a, b, c, d = n, n - 1, n - 2, n - 3
                if live(2):
                    probabilities(c, 1)
                    quarter(c, 1, B7)
                if live(0):
                    for h, name in ((0, "p1a"), (1, "p1b")):
                        r = slice(SEQ * h, SEQ * h + SEQ)
                        if h == 0:
                            act.wait_ge(S["nmx1_done"], a + 1)
                            if not first(a):
                                act.wait_ge(S["p1n_done"], a)
                        act.activation(p1[r, r], B5[r, r], ACT.Exp, bias=nmx1[r, :], scale=ASCALE,
                                       accum_out=sum1[r, :]).then_inc(S[name], 1)
                if live(3):
                    act.wait_ge(S["lsh_done"], d + 1)
                    act.activation(lex[:], lsh[:], ACT.Exp, accum_out=lsum[:]).then_inc(S["lex_done"], 1)
                if more(n):
                    rsqrt(0, n + 1)
                if live(2):
                    quarter(c, 3, B7)
                if live(1):
                    act.wait_ge(S["xn2Tp_done"], b + 1)
                    act.activation(xn2T[:], B6[:, 0:D], ACT.Copy).then_inc(S["xn2T_ev"], 1)
                if live(0):
                    act.wait_ge(S["p1Tp_done"], a + 1)
                    act.activation(p1T[:], B5[:, 0:P], ACT.Copy).then_inc(S["p1T_ev"], 1)
                    act.wait_ge(S["oT1_done"], a + 1)
                    act.activation(oT1[:], B5[:, 0:P], ACT.Identity, bias=bv_s[:]).then_inc(S["oT1_ev"], 1)
                if drain(n, 2):
                    act.preload_act_table_set("silu_and_others")
                    shared_silu(0)
                if live(2):
                    act.wait_ge(S["o2Tp_done"], c + 1)
                    act.activation(o2T[:], B5[:, 0:D], ACT.Copy).then_inc(S["o2T_ev"], 1)
                if drain(n, 2):
                    shared_silu(1)
                    act.preload_act_table_set("natural_log_exp_and_others")
                if live(0):
                    rsqrt(1, a)
                if live(2):
                    rsqrt(2, c)
                if more(n):
                    next_xn1T(n + 1)
                if live(1):
                    act.wait_ge(S["v_done"], b + 1)
                    if first(b):
                        act.wait_ge(S["vblk_set"], 3)
                    for hp in range(2):
                        r = slice(64 * hp, 64 * hp + 64)
                        act.activation(vblk[r, :, :, hp, 0:8],
                                       B5[r, :].rearrange("p (b c h d) -> p b c h d", b=2, h=2, d=HD)[:, :, :, hp, :],
                                       ACT.Copy).then_inc(S["vblk_ev"], 1)
                if live(1):
                    act.wait_ge(S["mTp_done"], b + 1)
                    act.activation(mT[:], B6[:, 0:64].bitcast(BF16), ACT.Copy).then_inc(S["mT_ev"], 1)
                if more(n):
                    next_qkv(n + 1)
                if live(1):
                    probabilities(b, 0)
                if drain(n, 2):
                    act.preload_act_table_set("silu_and_others")
                    shared_silu(2)
                    act.preload_act_table_set("natural_log_exp_and_others")
                if drain(n, 3):
                    act.preload_act_table_set("silu_and_others")
                    shared_silu(3)

            loop1(act, step)

            shared_silu(FILL - 1)
            with act.Fori(FILL, T) as t:
                shared_silu(t)

            def transposed(k, n):
                act.wait_ge(S["xTp_done"], n)
                act.activation(xgT[:], B4[:, 0:D], ACT.Copy).then_inc(S["xgT_ev"], 1)

            def routed_tile(t, k, more):
                act.wait_ge(S["up_done"], t + 1)
                act.activation(sil, SB[0][:, 0:INTER], ACT.Silu).then_inc(S["sil_done"], 1)
                if more:
                    transposed(k, t + 2)
                act.wait_ge(S["aTp_done"], t + 1)
                act.activation(aT.rearrange("p c q -> p (c q)"), SB[2][0:HALF_I, 0:2 * P], ACT.Copy).then_inc(S["aT_ev"], 1)

            transposed(0, 1)
            for k in range(RING):
                routed_tile(k, k, True)
            with act.Fori(1, RT // RING - 1) as g:
                for k in range(RING):
                    routed_tile(g * RING + k, k, True)
            for k in range(RING):
                routed_tile(RT - RING + k, k, k < RING - 1)

        @block.vector
        def _(dve):
            def ln_aggregate(k, t):
                held = hold(dve, t + 1)
                past_wait(dve)
                dve.wait_ge(S[LN[k]["bn"]], held)
                dve.bn_aggr(ln[k][0][:], st[:]).then_inc(S[LN[k]["agg"]], 1)

            def ln_stats(k, t):
                dve.bn_stats(st[:], tile_of(xres, t)).then_inc(S[LN[k]["bn"]], 1)
                ln_aggregate(k, t)

            def ln_step1(k, t):
                mv, _, rs, ntm, _ = ln[k]
                dve.wait_ge(S[LN[k]["rs0"]], t + 1)
                dve.tensor_scalar(ntm[:, 0:1], mv[:, 1:2], EPS, rs[:], ALU.add, ALU.mult).then_inc(S[LN[k]["nt"]], 1)

            def ln_step2(k, t):
                _, _, rs, ntm, _ = ln[k]
                dve.wait_ge(S[LN[k]["nt"]], 2 * t + 1)
                dve.tensor_scalar(ntm[:, 1:2], ntm[:, 0:1], rs[:], -0.5, ALU.mult, ALU.mult).then_inc(S[LN[k]["nt"]], 1)

            def ln_step3(k, t):
                _, _, rs, ntm, rstd = ln[k]
                dve.wait_ge(S[LN[k]["nt"]], 2 * t + 2)
                dve.tensor_scalar(rstd[:], ntm[:, 1:2], 1.5, rs[:], ALU.add, ALU.mult).then_inc(S[LN[k]["rstd"]], 1)

            def ln_step4(k, t, dst, name):
                mv, _, _, _, rstd = ln[k]
                dve.wait_ge(S[LN[k]["rstd"]], t + 1)
                dve.tensor_scalar(dst[:], tile_of(xres, t), mv[:, 0:1], rstd[:], ALU.subtract, ALU.mult).then_inc(S[name], 1)

            dve.wait_ge(S["zero_set"], 5)
            dve.wait_ge(S["x0_in"], 16)
            ln_stats(0, 0)
            ln_step1(0, 0)
            ln_step2(0, 0)
            ln_step3(0, 0)
            ln_step4(0, 0, xn1, "xn1_done")

            dve.wait_ge(S["pos_in"], 32)
            st_n = [0]

            def turn(ins):
                ins.then_inc(S["angle_step"], 1)
                st_n[0] += 1
                dve.wait_ge(S["angle_step"], st_n[0])

            turn(dve.tensor_scalar(angle, posb, freq[:, 0:1], None, ALU.mult))
            turn(dve.tensor_scalar(cosT[:], angle, 1.0 / 6.283185307179586, ROUND, ALU.mult, ALU.add))
            turn(dve.tensor_scalar(cosT[:], cosT[:], ROUND, None, ALU.subtract))
            turn(dve.scalar_tensor_tensor(sinT[:], cosT[:], -TWO_PI_HI, angle, ALU.mult, ALU.add))
            turn(dve.scalar_tensor_tensor(angle, cosT[:], -TWO_PI_LO, sinT[:], ALU.mult, ALU.add))
            dve.tensor_scalar(angle, angle, PI_IN, -PI_IN, ALU.min, ALU.max).then_inc(S["angle_step"], 1)

            def quarter(t, q):
                dve.wait_ge(S["tp_done"], 4 * t + q + 1)
                dve.tensor_copy(probT[:, 4 * q:4 * q + 4, :].rearrange("p c q -> p (c q)"), B4[:]).then_inc(S["tpD_ev"], 1)

            R = 13

            def after(d, k):
                dve.wait_ge(S["r_step"], d * R + k)

            def after_for_max(d, k):
                held = hold(dve, d * R + k)
                past_wait(dve)
                dve.wait_ge(S["r_step"], held)

            def best_groups(d, t, with_ln):
                dve.wait_ge(S["lex_done"], d + 1)
                dve.reciprocal(lrs[:], lsum[:]).then_inc(S["r_step"], 1)
                if with_ln:
                    ln_step1(0, t)
                after(d, 1)
                dve.tensor_scalar(prb[:], lex[:], lrs[:], None, ALU.mult).then_inc(S["r_step"], 1)
                if with_ln:
                    ln_step2(0, t)
                after(d, 2)
                dve.reduce_max(gmax[:, 0:GROUPS], prb[:].rearrange("p (g e) -> p g e", g=GROUPS), AX.X).then_inc(S["r_step"], 1)
                if with_ln:
                    ln_step3(0, t)
                after_for_max(d, 3)
                dve.max(gtop[:], gmax[:]).then_inc(S["r_step"], 1)
                if with_ln:
                    ln_step4(0, t, xn1, "xn1_done")
                after_for_max(d, 4)
                dve.max_index(gidx[:], gtop[:], gmax[:]).then_inc(S["r_step"], 1)
                after(d, 5)
                dve.tensor_copy(gidf[:], gidx[:, 0:TOPG]).then_inc(S["r_step"], 1)
                after(d, 6)
                dve.tensor_tensor(ghot[:], gidf[:, :, None].to_broadcast([P, TOPG, GROUPS]),
                                  iota[:, None, 0:GROUPS].to_broadcast([P, TOPG, GROUPS]), op=ALU.is_equal).then_inc(S["r_step"], 1)
                after(d, 7)
                dve.tensor_tensor(gm[:], ghot[:, 0, :], ghot[:, 1, :], op=ALU.add).then_inc(S["r_step"], 1)
                after(d, 8)
                dve.tensor_tensor(msc[:].rearrange("p (g e) -> p g e", g=GROUPS), prb[:].rearrange("p (g e) -> p g e", g=GROUPS),
                                  gm[:, :, None].to_broadcast([P, GROUPS, E // GROUPS]), op=ALU.mult).then_inc(S["r_step"], 1)

            def weigh_experts(d, c, with_ln):
                dve.wait_ge(S["eidx_done"], d + 1)
                dve.tensor_copy(eidf[:], eidx[:, 0:TOPK]).then_inc(S["eidf_done"], 1)
                if with_ln:
                    ln_step1(2, c)
                dve.wait_ge(S["ws_step"], d + 1)
                dve.tensor_scalar(wsum1[:], wsum[:], 1e-20, None, ALU.add).then_inc(S["r_step"], 1)
                dve.wait_ge(S["eidf_done"], d + 1)
                dve.tensor_tensor(ehot[:], eidf[:, :, None].to_broadcast([P, TOPK, E]),
                                  iota[:, None, :].to_broadcast([P, TOPK, E]), op=ALU.is_equal).then_inc(S["r_step"], 1)
                if with_ln:
                    ln_step2(2, c)
                after(d, 12)
                dve.tensor_reduce(self32[:], ehot[:].rearrange("p k e -> p e k"), AX.X, ALU.add).then_inc(S["r_step"], 1)
                dve.reciprocal(wrec[:], wsum1[:]).then_inc(S["wrec_done"], 1)
                if with_ln:
                    ln_step3(2, c)
                after(d, 13)
                dve.tensor_copy(sel[:], self32[:]).then_inc(S["sel_done"], 1)
                dve.tensor_tensor(msel[:], msc[:], self32[:], op=ALU.mult).then_inc(S["msel_done"], 1)
                if with_ln:
                    if not first(c):
                        dve.wait_ge(S["row_done"], c)
                    ln_step4(2, c, xn3, "xn3_done")
                dve.wait_ge(S["wrec_done"], d + 1)
                dve.wait_ge(S["msel_done"], d + 1)
                if not first(d):
                    dve.wait_ge(S["scattered"], d * 16 * TOPK)
                dve.tensor_scalar(xrow[:, D + 1:ROW], msel[:], wrec[:], None, ALU.mult).then_inc(S["cw_done"], 1)

            def slots_products(d):
                dve.wait_ge(S["slotE_done"], d + 1)
                dve.tensor_tensor(slot4[:], ehot[:], slotE[:, None, :].to_broadcast([P, TOPK, E]), op=ALU.mult) \
                    .then_inc(S["slot4_done"], 1)

            def slots_sums(d):
                dve.wait_ge(S["slot4_done"], d + 1)
                dve.reduce_sum(slotf[:], slot4[:], AX.X).then_inc(S["slotf_done"], 1)

            def slots_whole(d):
                dve.wait_ge(S["slotf_done"], d + 1)
                dve.tensor_copy(sloti[:], slotf[:]).then_inc(S["slots_done"], 1)

            def shared_product(t):
                dve.wait_ge(S["sg_done"], t + 1)
                dve.wait_ge(S["supu_done"], t + 1)
                if not first(t):
                    dve.wait_ge(S["sdn_done"], t)
                dve.tensor_tensor(saT, sg, SB[1][:, 0:SIP], op=ALU.mult).then_inc(S["saT_done"], 1)

            def shared_sum(t):
                dve.wait_ge(S["sdn_done"], t + 1)
                dve.tensor_tensor(tile_of(xres, t), SB[2][:, 0:D], tile_of(xres, t), op=ALU.add).then_inc(S["xs_done"], 1)

            def step(n, live):
                a, b, c, d = n, n - 1, n - 2, n - 3
                if live(2):
                    quarter(c, 0)
                if live(0):
                    dve.wait_ge(S["s1_done"], a + 1)
                    for h in range(2):
                        r = slice(SEQ * h, SEQ * h + SEQ)
                        dve.reduce_max(mx1[r, :], B5[r, r], AX.X).then_inc(S["mx1_done"], 1)
                if live(4):
                    slots_products(n - 4)
                if live(0):
                    dve.wait_ge(S["mx1_done"], 2 * a + 2)
                    dve.tensor_scalar(nmx1[:], mx1[:], -ASCALE, None, ALU.mult).then_inc(S["nmx1_done"], 1)
                if live(3):
                    dve.wait_ge(S["gate_done"], d + 1)
                    dve.reduce_max(lmx[:], B6[:, 0:E], AX.X).then_inc(S["lmx_done"], 1)
                if live(4):
                    slots_sums(n - 4)
                if live(3):
                    dve.wait_ge(S["lmx_done"], d + 1)
                    dve.tensor_scalar(lsh[:], B6[:, 0:E], lmx[:], None, ALU.subtract).then_inc(S["lsh_done"], 1)
                if live(4):
                    slots_whole(n - 4)
                if live(2):
                    quarter(c, 2)
                if more(n):
                    if first(n - 1):
                        dve.wait_ge(S["x_in"], 16)
                        dve.wait_ge(S["c1_in"], 160)
                    dve.bn_stats(st[:], tile_of(xres, n + 1)).then_inc(S["bn0"], 1)
                if more(n):
                    ln_aggregate(0, n + 1)
                if live(0):
                    dve.wait_ge(S["p1a"], a + 1)
                    dve.wait_ge(S["p1b"], a + 1)
                    dve.reciprocal(rsum1[:], sum1[:]).then_inc(S["rsum1_done"], 1)
                    dve.wait_ge(S["rsum1_done"], a + 1)
                    dve.tensor_scalar(p1n[:], p1[:], rsum1[:], None, ALU.mult).then_inc(S["p1n_done"], 1)
                if live(3):
                    best_groups(d, n + 1, more(n))
                elif more(n):
                    ln_step1(0, n + 1)
                    ln_step2(0, n + 1)
                    ln_step3(0, n + 1)
                    ln_step4(0, n + 1, xn1, "xn1_done")
                if live(1):
                    dve.wait_ge(S["q_done"], b + 1)
                    rope(B6, qr, qs, b, "qs_done")
                    dve.wait_ge(S["qs_done"], b + 1)
                    dve.tensor_tensor(qT[:], qr[:], qs[:], op=ALU.add).then_inc(S["qT_done"], 1)
                if live(2):
                    dve.wait_ge(S["av_done"], c + 1)
                    av = B4[:, 0:HEADS * 9].rearrange("p (h d) -> p h d", d=9)
                    dve.reciprocal(rden[:, :, None], av[:, :, 8:9]).then_inc(S["rden_done"], 1)
                    dve.wait_ge(S["rden_done"], c + 1)
                    dve.tensor_tensor(o2[:].rearrange("p (h d) -> p h d", d=HD), av[:, :, 0:HD],
                                      rden[:, :, None].to_broadcast([P, HEADS, HD]), op=ALU.mult).then_inc(S["o2_done"], 1)
                if drain(n, 2):
                    shared_product(0)
                if live(0):
                    dve.wait_ge(S["pr1_done"], a + 1)
                    dve.wait_ge(S["xbo_done"], a + 1)
                    dve.tensor_tensor(tile_of(xres, a), B7[:, 0:D], xbo[:], op=ALU.add).then_inc(S["x1_done"], 1)
                    held = hold(dve, a + 1)
                    past_wait(dve)
                    dve.wait_ge(S["x1_done"], held)
                    ln_stats(1, a)
                if live(1):
                    maxima(b, 0)
                if live(2):
                    dve.wait_ge(S["wout_done"], c + 1)
                    dve.wait_ge(S["xbout_done"], c + 1)
                    dve.tensor_tensor(tile_of(xres, c), B6[:, 0:D], xbout1[:], op=ALU.add).then_inc(S["x2_done"], 1)
                if live(3):
                    after_for_max(d, 9)
                    dve.max(etop[:], msc[:]).then_inc(S["r_step"], 1)
                if live(2):
                    held = hold(dve, c + 1)
                    past_wait(dve)
                    dve.wait_ge(S["x2_done"], held)
                    dve.bn_stats(st[:], tile_of(xres, c)).then_inc(S["bn2"], 1)
                if live(3):
                    after_for_max(d, 10)
                    dve.max_index(eidx[:], etop[:], msc[:]).then_inc(S["eidx_done"], 1)
                    dve.reduce_sum(wsum[:], etop[:, 0:TOPK], AX.X).then_inc(S["ws_step"], 1)
                if live(2):
                    ln_aggregate(2, c)
                if live(1):
                    maxima(b, 1)
                    dve.wait_ge(S["max_done"], 2 * b + 2)
                    dve.tensor_scalar(mstack[:, :, 0:8], mS[:], -1.0, None, ALU.mult).then_inc(S["mhi_done"], 1)
                if live(0):
                    ln_step1(1, a)
                if live(1):
                    dve.wait_ge(S["mhi_done"], b + 1)
                    dve.scalar_tensor_tensor(mstack[:, :, 8:16], mS[:], -1.0, mstack[:, :, 0:8], ALU.mult, ALU.subtract) \
                        .then_inc(S["mlo_done"], 1)
                if live(0):
                    ln_step2(1, a)
                if drain(n, 2):
                    shared_product(1)
                    shared_sum(0)
                if live(3):
                    weigh_experts(d, c, live(2))
                elif live(2):
                    if not first(c):
                        dve.wait_ge(S["row_done"], c)
                    ln_step1(2, c)
                    ln_step2(2, c)
                    ln_step3(2, c)
                    ln_step4(2, c, xn3, "xn3_done")
                if live(0):
                    dve.wait_ge(S["kp_done"], a + 1)
                    if first(a):
                        dve.wait_ge(S["cos_done"], 1)
                        dve.wait_ge(S["sin_done"], 1)
                    else:
                        dve.wait_ge(S["kT_done"], a)
                    rope(B7, kr, ks, a, "ks_done")
                    ln_step3(1, a)
                if live(2):
                    dve.wait_ge(S["xn3Tp_done"], c + 1)
                    if not first(c):
                        dve.wait_ge(S["xn3T_kept"], c)
                    dve.tensor_copy(xn3T[:], B6[:, 0:D]).then_inc(S["xn3T_ev"], 1)
                if live(3):
                    dve.wait_ge(S["pre_done"], d + 1)
                    dve.tensor_tensor(slotE[:], B5[:, 0:E], base_e[:], op=ALU.add).then_inc(S["slotE_done"], 1)
                    dve.tensor_tensor(macc[:], macc[:], sel[:], op=ALU.add).then_inc(S["macc_done"], 1)
                if live(0):
                    ln_step4(1, a, xn2, "xn2_done")
                if drain(n, 2):
                    shared_product(2)
                    shared_sum(1)
                if drain(n, 3):
                    shared_product(3)
                    shared_sum(2)

            def maxima(t, h):
                dve.wait_ge(S["s_done"], 2 * t + 1 + h)
                dve.reduce_max(mS[:, 2 * h:2 * h + 2, :], scores[:, 1024 * h:1024 * h + 1024]
                               .rearrange("p (r h k) -> p r h k", r=2, k=SEQ), AX.X).then_inc(S["max_done"], 1)

            def rope(bank, r, s_, t, s_name):
                both = bank[:].rearrange("p (f v q) -> p f v q", f=2, v=2)
                tab = lambda x: x[:, None, bass.ds(t * P, P)].to_broadcast([P, 2, P])
                dve.tensor_tensor(r[:], both[:, :, 0, :], tab(cosT), op=ALU.mult)
                dve.tensor_tensor(s_[:], both[:, :, 1, :], tab(sinT), op=ALU.mult).then_inc(S[s_name], 1)

            loop1(dve, step)
            slots_products(T - 1)
            slots_sums(T - 1)
            slots_whole(T - 1)

            dve.wait_ge(S["cnt_done"], 1)
            tn = [0]

            def then(ins):
                ins.then_inc(S["t_step"], 1)
                tn[0] += 1
                dve.wait_ge(S["t_step"], tn[0])

            then(dve.tensor_copy(cnt[:], B5[:, 0:E]))
            then(dve.tensor_tensor(tail_f[:], cnt[0:1, :], base_e[0:1, :], op=ALU.add))
            dve.tensor_copy(tail_i[:], tail_f[:]).then_inc(S["tab_done"], 1)
            then(dve.tensor_scalar(cpad[:], cnt[:], 1.0 / P, (P - 1.0) / (2 * P), ALU.mult, ALU.add))
            then(dve.tensor_scalar(cfl[:], cpad[:], ROUND, None, ALU.add))
            then(dve.tensor_scalar(nt[:], cfl[:], ROUND, None, ALU.subtract))
            then(dve.tensor_tensor_scan(tend[:], onesf[:, 0:E], nt[:], 0.0, ALU.mult, ALU.add))
            then(dve.tensor_scalar(past[:], tend[:], tileid[:], None, ALU.is_le))
            then(dve.reduce_sum(tcols[:, 2:3], past[:], AX.X))
            then(dve.tensor_tensor(rowt[:], past[:], nt[:], op=ALU.mult))
            then(dve.reduce_sum(tcols[:, 3:4], rowt[:], AX.X))
            then(dve.tensor_scalar(tcols[:, 1:2], tcols[:, 2:3], E - 1.0, None, ALU.min))
            then(dve.tensor_scalar(cgt[:, 0:1], tcols[:, 2:3], float(E), float(P), ALU.is_lt, ALU.mult))
            then(dve.tensor_tensor(cgt[:, 1:2], tileid[:], tcols[:, 3:4], op=ALU.subtract))
            then(dve.tensor_tensor(cgt[:, 2:3], cgt[:, 0:1], cgt[:, 1:2], op=ALU.mult))
            dve.scalar_tensor_tensor(tcols[:, 0:1], tcols[:, 2:3], float(REGION), cgt[:, 2:3], ALU.mult, ALU.add) \
                .then_inc(S["tcols_done"], 1)
            dve.wait_ge(S["tabTp_done"], 1)
            dve.tensor_copy(tabT[:].rearrange("a b t -> a (b t)"), B5[0:1, 0:2 * P]).then_inc(S["tab_done"], 1)

            shared_product(FILL - 1)
            shared_sum(FILL - 2)
            with dve.Fori(FILL, T) as t:
                shared_product(t)
                shared_sum(t - 1)
            shared_sum(T - 1)

            dve.wait_ge(S["tab_done"], 2)

            def gated(t):
                dve.wait_ge(S["sil_done"], t + 1)
                dve.tensor_tensor(act_, sil, SB[0][:, INTER:2 * INTER], op=ALU.mult).then_inc(S["a_done"], 1)

            def weighted(t, k):
                dve.wait_ge(S["dn_done"], t + 1)
                e = dve.value_load(tabT[0:1, 1, bass.ds(t, 1)], min_val=0, max_val=E - 1)
                dve.tensor_scalar(y[k], SB[1][:, 0:D], xg[k][:, bass.ds(e + (D + 1), 1)], None, ALU.mult).then_inc(S["y_done"], 1)

            for k in range(RING):
                gated(k)
                if k:
                    weighted(k - 1, k - 1)
            with dve.Fori(1, RT // RING) as g:
                for k in range(RING):
                    gated(g * RING + k)
                    weighted(g * RING + k - 1, (k - 1) % RING)
            weighted(RT - 1, RING - 1)

            for k in range(4):
                dve.wait_ge(S[f"fin_in{k}"], 32)
                part = xres[:, FT * k:FT * (k + 1), :]
                dve.tensor_tensor(part, part, fin_part(k, 0), op=ALU.add).then_inc(S["fin_step"], 1)
                dve.wait_ge(S["fin_step"], k + 1)
                dve.tensor_tensor(part, part, fin_part(k, 1), op=ALU.add).then_inc(S["fin_add"], 1)

        @block.tensor
        def _(pe):
            pe.wait_ge(S["ident_in"], 16)
            pe.wait_ge(S["w1_in"], 112)

            def transpose2(bank, src):
                for h in range(2):
                    last = pe.transpose(bank[:, h * P:h * P + P], src[:, h * P:h * P + P], ident[:])
                return last

            def quarter(bank, q):
                for j in range(4):
                    cc = 4 * q + j
                    last = pe.transpose(bank[:, j * P:j * P + P], prob[:, cc * P:cc * P + P], ident[:])
                return last

            def av(c0, c1):
                for cc in range(c0, c1):
                    for s_ in range(2):
                        r = slice(SEQ * s_, SEQ * s_ + SEQ)
                        last = pe.matmul(B4[r, 18 * cc:18 * cc + 18], probT[:, cc, r],
                                         vblk[:, s_, cc, :, :].rearrange("p h d -> p (h d)"), start=True, stop=True)
                return last

            def next_xn1T(t):
                pe.wait_ge(S["xn1_done"], t + 1)
                transpose2(B4, xn1).then_inc(S["xn1Tp_done"], 1)

            def scores_of(f, r_):
                g = slice(64 * r_, 64 * r_ + 64)
                for s_ in range(2):
                    q = slice(SEQ * s_, SEQ * s_ + SEQ)
                    last = pe.matmul(SB[2 * f + r_][q, :], qT[g, f, q], kblk[g, f, s_, :, :].rearrange("p h k -> p (h k)"),
                                     start=True, stop=False, skip_group_check=True)
                return last

            def next_qkv(t):
                pe.wait_ge(S["xn1T_ev"], t + 1)
                for i, w in enumerate((wk_s, wv_s)):
                    for h in range(C2):
                        pe.matmul(B4[:, i * P:i * P + P], w[:, h, :], xn1T[:, h * P:h * P + P], start=h == 0, stop=h == 1)
                for h in range(C2):
                    last = pe.matmul(B4[:, 2 * P:3 * P], xn1T[:, h * P:h * P + P], wv_s[:, h, :], start=h == 0, stop=h == 1)
                last.then_inc(S["qkv1_done"], 1)

            def shared_up(t):
                for v, name in ((0, "supg_done"), (1, "supu_done")):
                    if not first(t):
                        pe.wait_ge(S[("sg_done", "saT_done")[v]], t)
                    for j in range(SC):
                        for h in range(C2):
                            last = pe.matmul(SB[v][:, j * P:j * P + P], sup_s[:, h, v, j * P:j * P + P],
                                             xn3T_all[:, bass.ds(t, 1), h * P:h * P + P].rearrange("p a q -> p (a q)"),
                                             start=h == 0, stop=h == 1)
                    last.then_inc(S[name], 1)

            def shared_down(t):
                pe.wait_ge(S["saT_done"], t + 1)
                if not first(t):
                    pe.wait_ge(S["xs_done"], t)
                for j in range(SC):
                    last = pe.matmul(SB[2][:, 0:D], saT[:, j * P:j * P + P], sdown_s[:, j, :], start=j == 0, stop=j == SC - 1)
                last.then_inc(S["sdn_done"], 1)

            def step(n, live):
                a, b, c, d = n, n - 1, n - 2, n - 3
                if live(2):
                    pe.wait_ge(S["prob_done"], 2 * c + 1)
                    if live(0):
                        pe.wait_ge(S["v1_ev"], a + 1)
                    else:
                        pe.wait_ge(S["o2_done"], c)
                    quarter(B4, 0).then_inc(S["tp_done"], 1)
                if live(0):
                    pe.wait_ge(S["kT1_ev"], a + 1)
                    pe.wait_ge(S["vT1_ev"], a + 1)
                    if live(3) and not first(d):
                        pe.wait_ge(S["slotE_done"], d)
                    elif live(2):
                        pe.wait_ge(S["vblk_ev"], 2 * b)
                    elif not first(a):
                        pe.wait_ge(S["oT1_ev"], a)
                    pe.matmul(B5[:, 0:P], vT1[:], kT1[:], start=True, stop=True).then_inc(S["s1_done"], 1)
                if live(2):
                    if live(0):
                        pe.wait_ge(S["ks_done"], a)
                    else:
                        pe.wait_ge(S["ks_done"], T)
                    quarter(B7, 1).then_inc(S["tp_done"], 1)
                if live(3):
                    pe.wait_ge(S["xn3T_ev"], d + 1)
                    for h in range(C2):
                        last = pe.matmul(B6[:, 0:E], xn3T[:, h * P:h * P + P], gate_s[:, h, :], start=h == 0, stop=h == 1)
                    last.then_inc(S["gate_done"], 1)
                if live(2):
                    pe.wait_ge(S["prob_done"], 2 * c + 2)
                    pe.wait_ge(S["tpD_ev"], 2 * c + 1)
                    quarter(B4, 2).then_inc(S["tp_done"], 1)
                    pe.wait_ge(S["tpA_ev"], 2 * c + 1)
                    quarter(B7, 3).then_inc(S["tp_done"], 1)
                if drain(n, 2):
                    pe.wait_ge(S["sw_in"], 32)
                    pe.wait_ge(S["xn3T_kept"], FILL)
                    shared_up(0)
                if live(1):
                    if first(b):
                        pe.wait_ge(S["xw_in"], 80)
                        pe.wait_ge(S["c1_in"], 160)
                    pe.wait_ge(S["xn2_done"], b + 1)
                    if live(3):
                        pe.wait_ge(S["lsh_done"], d + 1)
                    elif not first(b):
                        pe.wait_ge(S["mT_ev"], b)
                    transpose2(B6, xn2).then_inc(S["xn2Tp_done"], 1)
                if live(2):
                    pe.wait_ge(S["tpD_ev"], 2 * c + 2)
                    pe.wait_ge(S["vblk_ev"], 2 * c + 2)
                    av(0, 8)
                if live(1):
                    pe.wait_ge(S["xn2T_ev"], b + 1)
                    for f in range(2):
                        for v in range(2):
                            o = (2 * f + v) * P
                            for h in range(C2):
                                last = pe.matmul(B6[:, o:o + P], xwq_s[:, h, v, f * P:f * P + P], xn2T[:, h * P:h * P + P],
                                                 start=h == 0, stop=h == 1)
                    last.then_inc(S["q_done"], 1)
                if live(0):
                    pe.wait_ge(S["p1n_done"], a + 1)
                    pe.transpose(B5[:, 0:P], p1n[:], ident[:]).then_inc(S["p1Tp_done"], 1)
                if live(2):
                    pe.wait_ge(S["tpA_ev"], 2 * c + 2)
                    av(8, 12)
                if live(0):
                    pe.wait_ge(S["p1T_ev"], a + 1)
                    pe.matmul(B5[:, 0:P], v1[:], p1T[:], start=True, stop=True).then_inc(S["oT1_done"], 1)
                if live(2):
                    av(12, 16).then_inc(S["av_done"], 1)
                if live(0):
                    pe.wait_ge(S["oT1_ev"], a + 1)
                    if live(2):
                        pe.wait_ge(S["tpA_ev"], 2 * c + 2)
                    elif live(1):
                        pe.wait_ge(S["ks_done"], a)
                    if first(a):
                        pe.wait_ge(S["wosum_done"], 1)
                    pe.matmul(B7[:, 0:D], oT1[:], wosum[:], start=True, stop=True).then_inc(S["pr1_done"], 1)
                if live(1):
                    made, read = hold(pe, b + 1), hold(pe, 2 * b, 1)
                    past_wait(pe)
                    pe.wait_ge(S["qT_done"], made)
                    pe.wait_ge(S["kblk_done"], made)
                    if not first(b):
                        pe.wait_ge(S["prob_done"], read)
                    scores_of(0, 0)
                if live(2):
                    pe.wait_ge(S["o2_done"], c + 1)
                    if live(0):
                        pe.wait_ge(S["oT1_ev"], a + 1)
                    else:
                        pe.wait_ge(S["slotE_done"], d)
                    transpose2(B5, o2).then_inc(S["o2Tp_done"], 1)
                if live(1):
                    scores_of(0, 1).then_inc(S["s_done"], 1)
                if drain(n, 2):
                    shared_up(1)
                    shared_down(0)
                if live(2):
                    pe.wait_ge(S["o2T_ev"], c + 1)
                    if live(1):
                        pe.wait_ge(S["qs_done"], b + 1)
                    else:
                        pe.wait_ge(S["lsh_done"], d + 1)
                    for h in range(C2):
                        last = pe.matmul(B6[:, 0:D], o2T[:, h * P:h * P + P], xwout_s[:, h, :], start=h == 0, stop=h == 1)
                    last.then_inc(S["wout_done"], 1)
                if live(1):
                    scores_of(1, 0)
                    scores_of(1, 1).then_inc(S["s_done"], 1)
                if more(n):
                    if live(2):
                        pe.wait_ge(S["o2_done"], c + 1)
                    else:
                        pe.wait_ge(S["v1_ev"], a + 1)
                    next_xn1T(a + 1)
                if live(1):
                    pe.wait_ge(S["ctxV_in"], 32 * (b + 1))
                    if live(2):
                        pe.wait_ge(S["o2T_ev"], c + 1)
                    for s_ in range(2):
                        last = pe.matmul(B5[:, D * s_:D * s_ + D], ctxV[:, s_, :, :].rearrange("c h k -> c (h k)"),
                                         xwv_s[:], start=True, stop=True)
                    last.then_inc(S["v_done"], 1)
                if live(0):
                    pe.wait_ge(S["ctxK_in"], 16 * (a + 1))
                    pe.wait_ge(S["x1_done"], a + 1)
                    for f in range(2):
                        for v in range(2):
                            o = (2 * f + v) * P
                            last = pe.matmul(B7[:, o:o + P], xwk_s[:, v, f * P:f * P + P], ctxK[:], start=True, stop=True)
                    last.then_inc(S["kp_done"], 1)
                if live(1):
                    pe.wait_ge(S["mlo_done"], b + 1)
                    if live(2):
                        pe.wait_ge(S["x2_done"], c + 1)
                    pe.transpose(B6[:, 0:64].bitcast(BF16), mstack[:].rearrange("p r m -> p (r m)"), identb[:]) \
                        .then_inc(S["mTp_done"], 1)
                if more(n):
                    next_qkv(a + 1)
                if live(1):
                    pe.wait_ge(S["mT_ev"], b + 1)
                    for r_ in range(4):
                        g = slice(32 * r_, 32 * r_ + 32)
                        last = pe.matmul(SB[r_], mT[g, :], inj[g, :], start=False, stop=True, skip_group_check=True)
                        if r_ % 2:
                            last.then_inc(S["inj_done"], 1)
                if drain(n, 2):
                    shared_up(2)
                    shared_down(1)
                if drain(n, 3):
                    shared_up(3)
                    shared_down(2)
                if live(2):
                    pe.wait_ge(S["xn3_done"], c + 1)
                    if live(1):
                        pe.wait_ge(S["mT_ev"], b + 1)
                    transpose2(B6, xn3).then_inc(S["xn3Tp_done"], 1)
                if live(3):
                    pe.wait_ge(S["sel_done"], d + 1)
                    if not first(d):
                        pe.wait_ge(S["macc_done"], d)
                    if live(1):
                        pe.wait_ge(S["vblk_ev"], 2 * b + 2)
                    elif live(2):
                        pe.wait_ge(S["o2T_ev"], c + 1)
                    pe.matmul(B5[:, 0:E], tri[:], sel[:], start=True, stop=False)
                    pe.matmul(B5[:, 0:E], ones[:], macc[:], start=False, stop=True).then_inc(S["pre_done"], 1)

            next_xn1T(0)
            next_qkv(0)

            loop1(pe, step)

            pe.wait_ge(S["macc_done"], T)
            pe.matmul(B5[:, 0:E], ones[:], macc[:], start=True, stop=True).then_inc(S["cnt_done"], 1)

            pe.wait_ge(S["xn3T_kept"], T)
            shared_up(FILL - 1)
            shared_down(FILL - 2)
            pe.wait_ge(S["tcols_done"], 1)
            pe.matmul(B5[0:1, 0:P], tcols[:, 0:1], ident[:], start=True, stop=True)
            pe.matmul(B5[0:1, P:2 * P], tcols[:, 1:2], ident[:], start=True, stop=True).then_inc(S["tabTp_done"], 1)
            with pe.Fori(FILL, T) as t:
                shared_up(t)
                shared_down(t - 1)
            shared_down(T - 1)

            pe.wait_ge(S["rw_in"], 32 * E)
            pe.wait_ge(S["tab_done"], 2)
            pe.wait_ge(S["xs_done"], T)

            def expert(t):
                return pe.value_load(tabT[0:1, 1, bass.ds(t, 1)], min_val=0, max_val=E - 1)

            def rows_in(t, k, g):
                pe.wait_ge(S[f"xg_in{k}"], (g + 1) * 16)
                transpose2(B4, xg[k]).then_inc(S["xTp_done"], 1)

            def up(t, e):
                pe.wait_ge(S["xgT_ev"], t + 1)
                for h in range(C2):
                    last = pe.matmul(SB[0][:, 0:2 * INTER], xgT[:, h * P:h * P + P],
                                     up_s[:, bass.ds(e, 1), h, :].rearrange("p a n -> p (a n)"), start=h == 0, stop=h == 1)
                last.then_inc(S["up_done"], 1)

            def down(t, e):
                pe.wait_ge(S["aT_ev"], t + 1)
                if not first(t):
                    pe.wait_ge(S["y_done"], t)
                for h in range(2):
                    last = pe.matmul(SB[1][:, 0:D], aT[:, h, :], down_s[:, bass.ds(e, 1), h, :].rearrange("p a n -> p (a n)"),
                                     start=h == 0, stop=h == 1)
                last.then_inc(S["dn_done"], 1)

            def gated_T(t):
                pe.wait_ge(S["a_done"], t + 1)
                for h in range(2):
                    last = pe.transpose(SB[2][0:HALF_I, h * P:h * P + P], act_[:, h * HALF_I:h * HALF_I + HALF_I], ident[:])
                last.then_inc(S["aTp_done"], 1)

            def held_expert(k):
                return pe.snap(e_of[k], min_val=0, max_val=E - 1)

            def ring(g, is_first, is_last):
                for k in range(RING):
                    t = g * RING + k
                    more_tiles = not (is_last and k == RING - 1)
                    if more_tiles:
                        pe.reg_add(e_of[(k + 1) % 4], expert(t + 1), 0)
                        rows_in(t + 1, (k + 1) % RING, g + (1 if k == RING - 1 else 0))
                    if not (is_first and k == 0):
                        down(t - 1, held_expert((k - 1) % 4))
                    gated_T(t)
                    if more_tiles:
                        up(t + 1, held_expert((k + 1) % 4))
                if is_last:
                    down(RT - 1, held_expert((RING - 1) % 4))

            rows_in(0, 0, 0)
            pe.reg_add(e_of[0], expert(0), 0)
            up(0, held_expert(0))
            ring(0, True, False)
            with pe.Fori(1, RT // RING - 1) as g:
                ring(g, False, False)
            ring(RT // RING - 1, False, True)


def kernel(**inputs):
    import numpy as np
    import ml_dtypes
    import concourse.bacc as bacc
    from concourse import mybir as mb
    from concourse.bass_utils import run_bass_kernel_spmd

    f = np.float32
    a = {k: np.asarray(v) for k, v in inputs.items()}

    def swapped(w):
        return np.stack([w, w.reshape(w.shape[0], -1, 2)[:, :, ::-1].reshape(w.shape)])

    wkv = a["L0_xattn_Wkv"]
    sup = np.zeros((D, 2, SIP), f)
    sup[:, :, :SI] = a["L0_ffn_shared_up_w"].T.reshape(D, 2, SI)
    sdown = np.zeros((SIP, D), f)
    sdown[:SI] = a["L0_ffn_shared_down_w"].T
    part = np.arange(P)
    inject = np.zeros((P, 512), f)
    for r in range(P):
        if r % 32 < 16:
            inject[r] = np.arange(512) // SEQ == r % 8
    arrays = {
        "x": a["x"].reshape(TOK, D),
        "ctxT": a["ctx_1024"].reshape(TOK, CTX).T,
        "pos": a["fside_BxSx2_0"].reshape(TOK, 2).T[(part % HD) // 4],
        "wk": a["L0_attn_Wk"], "wv": a["L0_attn_Wv"], "bk": a["L0_attn_bk"], "bv": a["L0_attn_bv"],
        "wo": a["L0_attn_Wo"], "bo": a["L0_attn_bo"],
        "xwq": swapped(a["L0_xattn_Wq"]).reshape(2, C2, P, D).transpose(2, 1, 0, 3), "xwk": swapped(wkv[:, :D]), "xwv": wkv[:, D:], "xwout": a["L0_xattn_Wout"],
        "xbout": a["L0_xattn_bout"], "gate": a["L0_ffn_gate_w"].T,
        "upw": a["L0_ffn_expert_up_w"].reshape(E, 2 * INTER, C2, P).transpose(3, 0, 2, 1),
        "downw": a["L0_ffn_expert_down_w"].reshape(E, D, 2, HALF_I).transpose(3, 0, 2, 1),
        "supw": sup.reshape(C2, P, 2, SIP).transpose(1, 0, 2, 3),
        "sdownw": sdown,
        "identity": np.eye(P, dtype=f),
        "identity_b": np.eye(P, dtype=ml_dtypes.bfloat16),
        "head_mask": ((part // HD % 8)[:, None] == np.arange(8)[None]).astype(f),
        "inject_rows": inject.astype(ml_dtypes.bfloat16),
        "before": (part[:, None] < part[None]).astype(ml_dtypes.bfloat16),
        "rope_freq": np.stack([np.where(part % 4 // 2 == 0, 1.0, 0.01), np.where(part % 2 == 0, -1.0, 1.0)], 1).astype(f),
        "region_base": np.broadcast_to(np.arange(E) * REGION, (P, E)).astype(f),
        "iota_e": np.broadcast_to(np.arange(E), (P, E)).astype(f),
        "token_ids": (part[:, None] + P * np.arange(T)[None]).astype(np.int32),
        "pad_rows": np.zeros((P, ROW), f),
        "tile_ids": part[:, None].astype(f),
        "ones_f": np.ones((P, P), f),
        "ones_b": np.ones((P, P), ml_dtypes.bfloat16),
    }
    arrays["pad_rows"].view(np.int32)[:, D] = TOK + part
    nc = bacc.Bacc("TRN2", target_bir_lowering=False, num_devices=1)
    sent, args = {}, {}
    for name, value in arrays.items():
        value = np.ascontiguousarray(value)
        sent[f"in_{name}"] = value
        args[name] = nc.dram_tensor(f"in_{name}", value.shape, mb.dt.from_np(value.dtype), kind="ExternalInput").ap()
    args["out"] = nc.dram_tensor("out_0", (TOK, D), mb.dt.float32, kind="ExternalOutput").ap()
    decoder_kernel(nc, **args)
    got = run_bass_kernel_spmd(nc, [sent], core_ids=[0])
    return got.results[0]["out_0"].reshape(inputs["x"].shape)
```
